# Optimizing a Trainium2 kernel written in Bass

```python
import numpy as np
import jax
import jax.numpy as jnp

def _softmax(x, axis=-1):
    return jax.nn.softmax(x, axis=axis)

def _gelu(x):
    return jax.nn.gelu(x, approximate=True)

def _silu(x):
    return jax.nn.silu(x)

def _sigmoid(x):
    return jax.nn.sigmoid(x)

def _layernorm(x, axis=-1, eps=1e-05):
    m = jnp.mean(x, axis=axis, keepdims=True)
    v = jnp.var(x, axis=axis, keepdims=True)
    return (x - m) / jnp.sqrt(v + eps)

def _scatter_add(tgt, idx, src, axis=0):
    return tgt.at[idx].add(src)

def _segment_sum(src, seg, n):
    return jax.ops.segment_sum(src, seg, n)
kernel_name = 'mk_flamingo_gated_d2_seqx_r4_2f3b0f'

def setup_inputs(seed: int=0):
    np.random.seed(seed)
    _w = jnp.asarray

    def _rec_inputs():
        import jax
        import jax.numpy as jnp
        _rk = jax.random.key(seed)
        x = 7.22e-05 + 1 * jax.random.normal(jax.random.fold_in(_rk, 1), (4, 512, 256), jnp.float32)
        _lenS = 512 - jax.random.randint(jax.random.fold_in(_rk, 7), (4,), 0, max(1, 512 // 4) + 1, jnp.int32)
        _lenS2 = 64 - jax.random.randint(jax.random.fold_in(_rk, 8), (4,), 0, max(1, 64 // 4) + 1, jnp.int32)
        _ctx_768P = jax.random.normal(jax.random.fold_in(_rk, 11), (4, 16, 192), jnp.float32)
        _ctx_768c = jax.random.dirichlet(jax.random.fold_in(_rk, 511), 0.3 * jnp.ones((16,), jnp.float32), (4, 64))
        _ctx_768t = jnp.einsum('bsk,bkd->bsd', _ctx_768c, _ctx_768P)
        _ctx_768t = _ctx_768t * jax.lax.rsqrt(jnp.mean(jnp.square(_ctx_768t)) + 1e-12) * 0.953939
        ctx_768 = -0.000191848 + 0.999787 * (_ctx_768t + 0.3 * jax.random.normal(jax.random.fold_in(_rk, 611), (4, 64, 192), jnp.float32))
        _validS = jnp.arange(512)[None, :] < _lenS[:, None]
        _validS2 = jnp.arange(64)[None, :] < _lenS2[:, None]
        _causal = jnp.tril(jnp.ones((512, 512), dtype=bool))
        mask_BxS_bf1 = jnp.ones((4, 512), dtype=bool)
        mask_BxS2_bf1 = jnp.ones((4, 64), dtype=bool)
        _g = jax.random.normal(jax.random.fold_in(_rk, 9001), (2, 2), jnp.float32)
        _g = jnp.sign(_g) * jnp.maximum(jnp.abs(_g), 1.0) + (_g == 0) * 1.0
        g_xattn = _g[0]
        g_ffn = _g[1]
        return (x, ctx_768, mask_BxS_bf1, mask_BxS2_bf1, g_xattn, g_ffn)
    x, ctx_768, mask_BxS_bf1, mask_BxS2_bf1, g_xattn, g_ffn = _rec_inputs()

    def _L0_xattn_setup():
        import jax, jax.numpy as jnp
        import numpy as np
        NUM_HEADS = 16
        CLAMP = 10000.0
        key = jax.random.key(seed)
        ks = jax.random.split(key, 8)
        B, Nq, Nkv, Cq, Ckv = (4, 512, 512, 256, 192)
        s_q = 1.0 / np.sqrt(Cq)
        s_kv = 1.0 / np.sqrt(Ckv)
        return {'query': jax.random.normal(ks[0], (B, Nq, Cq), jnp.float32), 'key_value': jax.random.normal(ks[1], (B, Nkv, Ckv), jnp.float32), 'Wq': jax.random.normal(ks[2], (Cq, Cq), jnp.float32) * s_q, 'bq': jnp.zeros((Cq,), jnp.float32), 'Wk': jax.random.normal(ks[3], (Ckv, Cq), jnp.float32) * s_kv, 'bk': jnp.zeros((Cq,), jnp.float32), 'Wv': jax.random.normal(ks[4], (Ckv, Cq), jnp.float32) * s_kv, 'bv': jnp.zeros((Cq,), jnp.float32), 'Wo': jax.random.normal(ks[5], (Cq, Cq), jnp.float32) * s_q, 'bo': jnp.zeros((Cq,), jnp.float32)}
    _L0_xattn_all = _L0_xattn_setup()
    _L0_xattn_in = {k: v for k, v in _L0_xattn_all.items() if k in ('Wq', 'bq', 'Wk', 'bk', 'Wv', 'bv', 'Wo', 'bo')}
    del _L0_xattn_all

    def _L0_ffn_setup():
        import jax, jax.numpy as jnp
        import numpy as np
        D_MODEL = 256
        D_HIDDEN = 1024
        NUM_EXPERTS = 8
        B, T = (2, 512)
        key = jax.random.key(seed)
        ks = jax.random.split(key, 8)
        s = 0.02
        x = jax.random.normal(ks[0], (B, T, D_MODEL), dtype=jnp.float32)
        Wg = jax.random.normal(ks[1], (D_MODEL, NUM_EXPERTS), dtype=jnp.float32) * s
        bg = jnp.zeros((NUM_EXPERTS,), dtype=jnp.float32)
        W1 = jax.random.normal(ks[2], (NUM_EXPERTS, D_MODEL, D_HIDDEN), dtype=jnp.float32) * s
        b1 = jnp.zeros((NUM_EXPERTS, D_HIDDEN), dtype=jnp.float32)
        W2 = jax.random.normal(ks[3], (NUM_EXPERTS, D_HIDDEN, D_MODEL), dtype=jnp.float32) * s
        b2 = jnp.zeros((NUM_EXPERTS, D_MODEL), dtype=jnp.float32)
        return {'x': x, 'Wg': Wg, 'bg': bg, 'W1': W1, 'b1': b1, 'W2': W2, 'b2': b2}
    _L0_ffn_all = _L0_ffn_setup()
    _L0_ffn_in = {k: v for k, v in _L0_ffn_all.items() if k in ('Wg', 'bg', 'W1', 'b1', 'W2', 'b2')}
    del _L0_ffn_all

    def _L1_xattn_setup():
        import jax, jax.numpy as jnp
        import numpy as np
        B, T, DT, G, DV = (16, 128, 256, 144, 192)
        H, DH = (4, 32)
        INNER = H * DH
        HID = 4 * DT
        N_STATE = 64
        K_TOP = 32

        def layernorm(x, g, b, eps=1e-05):
            m = x.mean(-1, keepdims=True)
            v = x.var(-1, keepdims=True)
            return (x - m) * jax.lax.rsqrt(v + eps) * g + b

        def s4d(x, log_dt, A_re, A_im, C_re, C_im, D_skip):
            Bb, L, D = x.shape
            dt = jnp.exp(log_dt)
            A = A_re + 1j * A_im
            C = C_re + 1j * C_im
            dtA = dt[:, None] * A
            dC = C * (jnp.exp(dtA) - 1.0) / A
            powers = jnp.exp(dtA[:, :, None] * jnp.arange(L))
            K = 2.0 * jnp.einsum('dn,dnl->dl', dC, powers).real
            n = 2 * L
            Kf = jnp.fft.rfft(K, n=n, axis=-1)
            xf = jnp.fft.rfft(x, n=n, axis=1)
            y = jnp.fft.irfft(xf * Kf.T[None], n=n, axis=1)[:, :L]
            return y + x * D_skip
        key = jax.random.key(seed)
        ks = jax.random.split(key, 16)
        s = 0.02
        inp = {'x_text': jax.random.normal(ks[0], (B, T, DT), jnp.float32), 'x_vision': jax.random.normal(ks[1], (B, G, DV), jnp.float32), 'text_mask': jnp.ones((B, T), bool), 'vision_mask': jnp.ones((B, G), bool), 'Wq': jax.random.normal(ks[2], (DT, INNER), jnp.float32) * s, 'Wk': jax.random.normal(ks[3], (DV, INNER), jnp.float32) * s, 'Wv': jax.random.normal(ks[4], (DV, DT), jnp.float32) * s, 'W_film_in': jax.random.normal(ks[5], (DT, 2 * DT), jnp.float32) * s, 'b_film_in': jnp.zeros((2 * DT,), jnp.float32), 'W_film_out': jax.random.normal(ks[6], (DT, 2 * DT), jnp.float32) * s, 'b_film_out': jnp.zeros((2 * DT,), jnp.float32), 'g_norm_in': jnp.ones((DT,), jnp.float32), 'b_norm_in': jnp.zeros((DT,), jnp.float32), 'g_norm_out': jnp.ones((DT,), jnp.float32), 'b_norm_out': jnp.zeros((DT,), jnp.float32), 'g_ffn': jnp.ones((DT,), jnp.float32), 'b_ffn': jnp.zeros((DT,), jnp.float32), 'W1': jax.random.normal(ks[7], (DT, HID), jnp.float32) * s, 'b1': jnp.zeros((HID,), jnp.float32), 'W2': jax.random.normal(ks[8], (HID, DT), jnp.float32) * s, 'b2': jnp.zeros((DT,), jnp.float32), 'log_dt': jnp.log(0.001) + jax.random.uniform(ks[9], (DT,), jnp.float32) * (jnp.log(0.1) - jnp.log(0.001)), 'A_re': -0.5 * jnp.ones((DT, N_STATE), jnp.float32), 'A_im': jnp.tile(jnp.pi * jnp.arange(N_STATE, dtype=jnp.float32), (DT, 1)), 'C_re': jax.random.normal(ks[10], (DT, N_STATE), jnp.float32) * 0.5 ** 0.5, 'C_im': jax.random.normal(ks[11], (DT, N_STATE), jnp.float32) * 0.5 ** 0.5, 'D_skip': jax.random.normal(ks[12], (DT,), jnp.float32), 'mod_gate': jnp.array(0.5, jnp.float32)}
        return inp
    _L1_xattn_all = _L1_xattn_setup()
    _L1_xattn_in = {k: v for k, v in _L1_xattn_all.items() if k in ('Wq', 'Wk', 'Wv', 'W_film_in', 'b_film_in', 'W_film_out', 'b_film_out', 'g_norm_in', 'b_norm_in', 'g_norm_out', 'b_norm_out', 'g_ffn', 'b_ffn', 'W1', 'b1', 'W2', 'b2', 'log_dt', 'A_re', 'A_im', 'C_re', 'C_im', 'D_skip', 'mod_gate')}
    del _L1_xattn_all

    def _L1_ffn_setup():
        import jax, jax.numpy as jnp
        import numpy as np
        S, B, H, F, E, K = (512, 2, 256, 512, 8, 2)

        def _moe_forward(hidden_states, router_w, w1, b1, w2, b2):
            s, b, h = hidden_states.shape
            T = s * b
            x = hidden_states.reshape(T, h)
            logits = jnp.einsum('th,eh->te', x, router_w)
            topk_logits, topk_idx = jax.lax.top_k(logits, K)
            probs = jax.nn.softmax(topk_logits, axis=-1)
            combine = jnp.zeros((T, E), dtype=x.dtype)
            combine = combine.at[jnp.arange(T)[:, None], topk_idx].add(probs.astype(x.dtype))
            hmid = jnp.einsum('th,efh->etf', x, w1) + b1[:, None, :]
            hmid = jax.nn.gelu(hmid, approximate=False)
            y = jnp.einsum('etf,ehf->eth', hmid, w2) + b2[:, None, :]
            out = jnp.einsum('eth,te->th', y, combine)
            return out.reshape(s, b, h)
        key = jax.random.key(seed)
        ks = jax.random.split(key, 6)
        std = 0.02
        return {'hidden_states': jax.random.normal(ks[0], (S, B, H), dtype=jnp.float32), 'router_w': jax.random.normal(ks[1], (E, H), dtype=jnp.float32) * std, 'w1': jax.random.normal(ks[2], (E, F, H), dtype=jnp.float32) * (1.0 / np.sqrt(H)), 'b1': jnp.zeros((E, F), dtype=jnp.float32), 'w2': jax.random.normal(ks[3], (E, H, F), dtype=jnp.float32) * (1.0 / np.sqrt(F)), 'b2': jnp.zeros((E, H), dtype=jnp.float32)}
    _L1_ffn_all = _L1_ffn_setup()
    _L1_ffn_in = {k: v for k, v in _L1_ffn_all.items() if k in ('router_w', 'w1', 'b1', 'w2', 'b2')}
    del _L1_ffn_all
    return {'x': x, 'ctx_768': ctx_768, 'mask_BxS_bf1': mask_BxS_bf1, 'mask_BxS2_bf1': mask_BxS2_bf1, 'g_xattn': g_xattn, 'g_ffn': g_ffn, 'L0_xattn_Wq': _L0_xattn_in['Wq'], 'L0_xattn_bq': _L0_xattn_in['bq'], 'L0_xattn_Wk': _L0_xattn_in['Wk'], 'L0_xattn_bk': _L0_xattn_in['bk'], 'L0_xattn_Wv': _L0_xattn_in['Wv'], 'L0_xattn_bv': _L0_xattn_in['bv'], 'L0_xattn_Wo': _L0_xattn_in['Wo'], 'L0_xattn_bo': _L0_xattn_in['bo'], 'L0_ffn_Wg': _L0_ffn_in['Wg'], 'L0_ffn_bg': _L0_ffn_in['bg'], 'L0_ffn_W1': _L0_ffn_in['W1'], 'L0_ffn_b1': _L0_ffn_in['b1'], 'L0_ffn_W2': _L0_ffn_in['W2'], 'L0_ffn_b2': _L0_ffn_in['b2'], 'L1_xattn_Wq': _L1_xattn_in['Wq'], 'L1_xattn_Wk': _L1_xattn_in['Wk'], 'L1_xattn_Wv': _L1_xattn_in['Wv'], 'L1_xattn_W_film_in': _L1_xattn_in['W_film_in'], 'L1_xattn_b_film_in': _L1_xattn_in['b_film_in'], 'L1_xattn_W_film_out': _L1_xattn_in['W_film_out'], 'L1_xattn_b_film_out': _L1_xattn_in['b_film_out'], 'L1_xattn_g_norm_in': _L1_xattn_in['g_norm_in'], 'L1_xattn_b_norm_in': _L1_xattn_in['b_norm_in'], 'L1_xattn_g_norm_out': _L1_xattn_in['g_norm_out'], 'L1_xattn_b_norm_out': _L1_xattn_in['b_norm_out'], 'L1_xattn_g_ffn': _L1_xattn_in['g_ffn'], 'L1_xattn_b_ffn': _L1_xattn_in['b_ffn'], 'L1_xattn_W1': _L1_xattn_in['W1'], 'L1_xattn_b1': _L1_xattn_in['b1'], 'L1_xattn_W2': _L1_xattn_in['W2'], 'L1_xattn_b2': _L1_xattn_in['b2'], 'L1_xattn_log_dt': _L1_xattn_in['log_dt'], 'L1_xattn_A_re': _L1_xattn_in['A_re'], 'L1_xattn_A_im': _L1_xattn_in['A_im'], 'L1_xattn_C_re': _L1_xattn_in['C_re'], 'L1_xattn_C_im': _L1_xattn_in['C_im'], 'L1_xattn_D_skip': _L1_xattn_in['D_skip'], 'L1_xattn_mod_gate': _L1_xattn_in['mod_gate'], 'L1_ffn_router_w': _L1_ffn_in['router_w'], 'L1_ffn_w1': _L1_ffn_in['w1'], 'L1_ffn_b1': _L1_ffn_in['b1'], 'L1_ffn_w2': _L1_ffn_in['w2'], 'L1_ffn_b2': _L1_ffn_in['b2']}

def reference(x, ctx_768, mask_BxS_bf1, mask_BxS2_bf1, g_xattn, g_ffn, L0_xattn_Wq, L0_xattn_bq, L0_xattn_Wk, L0_xattn_bk, L0_xattn_Wv, L0_xattn_bv, L0_xattn_Wo, L0_xattn_bo, L0_ffn_Wg, L0_ffn_bg, L0_ffn_W1, L0_ffn_b1, L0_ffn_W2, L0_ffn_b2, L1_xattn_Wq, L1_xattn_Wk, L1_xattn_Wv, L1_xattn_W_film_in, L1_xattn_b_film_in, L1_xattn_W_film_out, L1_xattn_b_film_out, L1_xattn_g_norm_in, L1_xattn_b_norm_in, L1_xattn_g_norm_out, L1_xattn_b_norm_out, L1_xattn_g_ffn, L1_xattn_b_ffn, L1_xattn_W1, L1_xattn_b1, L1_xattn_W2, L1_xattn_b2, L1_xattn_log_dt, L1_xattn_A_re, L1_xattn_A_im, L1_xattn_C_re, L1_xattn_C_im, L1_xattn_D_skip, L1_xattn_mod_gate, L1_ffn_router_w, L1_ffn_w1, L1_ffn_b1, L1_ffn_w2, L1_ffn_b2):
    import jax
    import jax.numpy as jnp

    def _L0_xattn_ref(query, key_value, Wq, bq, Wk, bk, Wv, bv, Wo, bo):
        import jax, jax.numpy as jnp
        import numpy as np
        NUM_HEADS = 16
        CLAMP = 10000.0
        B, Nq, Cq = query.shape
        Nkv = key_value.shape[1]
        H = NUM_HEADS
        D = Cq // H
        scale = D ** (-0.5)
        q = (query @ Wq + bq).reshape(B, Nq, H, D).transpose(0, 2, 1, 3)
        k = (key_value @ Wk + bk).reshape(B, Nkv, H, D).transpose(0, 2, 1, 3)
        v = (key_value @ Wv + bv).reshape(B, Nkv, H, D).transpose(0, 2, 1, 3)
        attn = jnp.einsum('bhqd,bhkd->bhqk', q, k) * scale
        attn = jnp.clip(attn, -CLAMP, CLAMP)
        attn = jax.nn.softmax(attn, axis=-1)
        attn = jnp.where(jnp.any(jnp.isnan(attn)), jnp.asarray(1.0 / Nkv, attn.dtype), attn)
        x = jnp.einsum('bhqk,bhkd->bqhd', attn, v).reshape(B, Nq, Cq)
        return x @ Wo + bo

    def _L0_ffn_ref(x, Wg, bg, W1, b1, W2, b2):
        import jax, jax.numpy as jnp
        import numpy as np
        D_MODEL = 256
        D_HIDDEN = 1024
        NUM_EXPERTS = 8
        B, T = (2, 512)
        gate_logits = jnp.einsum('btd,de->bte', x, Wg) + bg
        gate_scores = jax.nn.softmax(gate_logits, axis=-1)
        top1_idx = jnp.argmax(gate_scores, axis=-1)
        top1_mask = jax.nn.one_hot(top1_idx, NUM_EXPERTS, dtype=x.dtype)
        top1_weight = jnp.sum(gate_scores * top1_mask, axis=-1, keepdims=True)
        h = jax.nn.silu(jnp.einsum('btd,edh->bteh', x, W1) + b1)
        o = jnp.einsum('bteh,ehd->bted', h, W2) + b2
        y = jnp.sum(o * top1_mask[..., None], axis=2) * top1_weight
        return y

    def _L1_xattn_ref(x_text, x_vision, text_mask, vision_mask, Wq, Wk, Wv, W_film_in, b_film_in, W_film_out, b_film_out, g_norm_in, b_norm_in, g_norm_out, b_norm_out, g_ffn, b_ffn, W1, b1, W2, b2, log_dt, A_re, A_im, C_re, C_im, D_skip, mod_gate):
        import jax, jax.numpy as jnp
        import numpy as np
        B, T, DT, G, DV = (16, 128, 256, 144, 192)
        H, DH = (4, 32)
        INNER = H * DH
        HID = 4 * DT
        N_STATE = 64
        K_TOP = 32

        def layernorm(x, g, b, eps=1e-05):
            m = x.mean(-1, keepdims=True)
            v = x.var(-1, keepdims=True)
            return (x - m) * jax.lax.rsqrt(v + eps) * g + b

        def s4d(x, log_dt, A_re, A_im, C_re, C_im, D_skip):
            Bb, L, D = x.shape
            dt = jnp.exp(log_dt)
            A = A_re + 1j * A_im
            C = C_re + 1j * C_im
            dtA = dt[:, None] * A
            dC = C * (jnp.exp(dtA) - 1.0) / A
            powers = jnp.exp(dtA[:, :, None] * jnp.arange(L))
            K = 2.0 * jnp.einsum('dn,dnl->dl', dC, powers).real
            n = 2 * L
            Kf = jnp.fft.rfft(K, n=n, axis=-1)
            xf = jnp.fft.rfft(x, n=n, axis=1)
            y = jnp.fft.irfft(xf * Kf.T[None], n=n, axis=1)[:, :L]
            return y + x * D_skip
        Bb, Tt, D = x_text.shape
        Gg = x_vision.shape[1]
        Q = (x_text @ Wq).reshape(Bb, Tt, H, DH)
        K = (x_vision @ Wk).reshape(Bb, Gg, H, DH)
        scores = jnp.einsum('bthd,bghd->bhtg', Q, K) / np.sqrt(DH).astype(np.float32)
        scores = jnp.where(vision_mask[:, None, None, :], scores, -jnp.inf)
        topv, topi = jax.lax.top_k(scores, K_TOP)
        probs = jax.nn.softmax(topv, axis=-1)
        bi = jnp.arange(Bb)[:, None, None, None]
        hi = jnp.arange(H)[None, :, None, None]
        ti = jnp.arange(Tt)[None, None, :, None]
        attn = jnp.zeros_like(scores).at[bi, hi, ti, topi].set(probs)
        attn_mean = attn.mean(axis=1)
        V = x_vision @ Wv
        c_t = jnp.einsum('btg,bgd->btd', attn_mean, V)
        c_t = c_t * text_mask[..., None]
        x = layernorm(x_text, g_norm_in, b_norm_in)
        scale_in, shift_in = jnp.split(c_t @ W_film_in + b_film_in, 2, axis=-1)
        x = x * (1.0 + mod_gate * scale_in) + mod_gate * shift_in
        y = s4d(x, log_dt, A_re, A_im, C_re, C_im, D_skip)
        scale_out, shift_out = jnp.split(c_t @ W_film_out + b_film_out, 2, axis=-1)
        y = y * (1.0 + mod_gate * scale_out) + mod_gate * shift_out
        xt = x_text + y
        h = layernorm(xt, g_ffn, b_ffn)
        h = jax.nn.gelu(h @ W1 + b1, approximate=False) @ W2 + b2
        xt = xt + h
        return layernorm(xt, g_norm_out, b_norm_out)

    def _L1_ffn_ref(hidden_states, router_w, w1, b1, w2, b2):
        import jax, jax.numpy as jnp
        import numpy as np
        S, B, H, F, E, K = (512, 2, 256, 512, 8, 2)

        def _moe_forward(hidden_states, router_w, w1, b1, w2, b2):
            s, b, h = hidden_states.shape
            T = s * b
            x = hidden_states.reshape(T, h)
            logits = jnp.einsum('th,eh->te', x, router_w)
            topk_logits, topk_idx = jax.lax.top_k(logits, K)
            probs = jax.nn.softmax(topk_logits, axis=-1)
            combine = jnp.zeros((T, E), dtype=x.dtype)
            combine = combine.at[jnp.arange(T)[:, None], topk_idx].add(probs.astype(x.dtype))
            hmid = jnp.einsum('th,efh->etf', x, w1) + b1[:, None, :]
            hmid = jax.nn.gelu(hmid, approximate=False)
            y = jnp.einsum('etf,ehf->eth', hmid, w2) + b2[:, None, :]
            out = jnp.einsum('eth,te->th', y, combine)
            return out.reshape(s, b, h)
        return _moe_forward(hidden_states, router_w, w1, b1, w2, b2)
    x = x + jnp.tanh(g_xattn[0]) * _L0_xattn_ref(_layernorm(x, axis=-1), ctx_768, L0_xattn_Wq, L0_xattn_bq, L0_xattn_Wk, L0_xattn_bk, L0_xattn_Wv, L0_xattn_bv, L0_xattn_Wo, L0_xattn_bo)
    x = x + jnp.tanh(g_ffn[0]) * _L0_ffn_ref(_layernorm(x, axis=-1), L0_ffn_Wg, L0_ffn_bg, L0_ffn_W1, L0_ffn_b1, L0_ffn_W2, L0_ffn_b2)
    x = x + jnp.tanh(g_xattn[1]) * _L1_xattn_ref(_layernorm(x, axis=-1), ctx_768, mask_BxS_bf1, mask_BxS2_bf1, L1_xattn_Wq, L1_xattn_Wk, L1_xattn_Wv, L1_xattn_W_film_in, L1_xattn_b_film_in, L1_xattn_W_film_out, L1_xattn_b_film_out, L1_xattn_g_norm_in, L1_xattn_b_norm_in, L1_xattn_g_norm_out, L1_xattn_b_norm_out, L1_xattn_g_ffn, L1_xattn_b_ffn, L1_xattn_W1, L1_xattn_b1, L1_xattn_W2, L1_xattn_b2, L1_xattn_log_dt, L1_xattn_A_re, L1_xattn_A_im, L1_xattn_C_re, L1_xattn_C_im, L1_xattn_D_skip, L1_xattn_mod_gate)
    x = x + jnp.tanh(g_ffn[1]) * _L1_ffn_ref(_layernorm(x, axis=-1), L1_ffn_router_w, L1_ffn_w1, L1_ffn_b1, L1_ffn_w2, L1_ffn_b2)
    return x

_drawn_inputs = setup_inputs


def setup_inputs(seed=0):
    import zlib

    import numpy as np

    out = dict(_drawn_inputs(seed))
    spreads = {'g_ffn': (-1.0, 0.551),
     'L0_xattn_bq': (0.0, 0.1),
     'L0_xattn_bk': (0.0, 0.8),
     'L0_xattn_bv': (0.0, 0.1),
     'L0_xattn_bo': (0.0, 0.1),
     'L0_ffn_bg': (0.0, 0.1),
     'L0_ffn_b1': (0.0, 0.342),
     'L0_ffn_b2': (0.0, 0.1),
     'L1_xattn_b_film_in': (0.0, 0.1),
     'L1_xattn_b_film_out': (0.0, 0.1),
     'L1_xattn_g_norm_in': (1.0, 0.2),
     'L1_xattn_b_norm_in': (0.0, 0.1),
     'L1_xattn_g_norm_out': (1.0, 0.2),
     'L1_xattn_b_norm_out': (0.0, 0.1),
     'L1_xattn_g_ffn': (1.0, 0.2),
     'L1_xattn_b_ffn': (0.0, 0.1),
     'L1_xattn_b1': (0.0, 0.1),
     'L1_xattn_b2': (0.0, 0.1),
     'L1_xattn_A_re': (-0.5, 0.2),
     'L1_ffn_b1': (0.0, 0.1),
     'L1_ffn_b2': (0.0, 0.1)}
    factors = {}
    for name, (base, spread) in spreads.items():
        noise = np.random.default_rng([zlib.crc32(name.encode()), seed]).standard_normal(out[name].shape)
        drawn = base * np.exp(spread * noise) if base else spread * noise
        out[name] = jnp.asarray(drawn.astype(out[name].dtype))
    for name, factor in factors.items():
        out[name] = (out[name] * factor).astype(out[name].dtype)
    return out
```

```python
from contextlib import ExitStack

import concourse.bass as bass
from concourse import mybir

ALU = mybir.AluOpType
ACT = mybir.ActivationFunctionType
F32 = mybir.dt.float32
BF16 = mybir.dt.bfloat16
I32 = mybir.dt.int32
U32 = mybir.dt.uint32
U8 = mybir.dt.uint8
AX = mybir.AxisListType.X

P = 128
B, S, D = 4, 512, 256
SK, DC = 64, 192
T = B * S // P
TB = S // P
KD = D // P
KC = 96
H0 = 16
DH0 = D // H0
HP0 = H0 // 2
CLAMP = 10000.0
EPS = 1e-5
E = 8
F0, F1 = 1024, 512
LOWEST = -3.0e38


def static(v):
    return isinstance(v, int)


def wait(eng, sem, value, at):
    if at >= 1:
        eng.wait_ge(sem, value)


def pipeline(eng, slot, first, steady, stop, last):
    for t in range(first, steady):
        slot(t, t)
    with eng.Fori(0, (stop - steady) // 2) as i:
        for u in range(2):
            slot(i * 2 + (steady + u), steady + u)
    for t in range(stop, last + 1):
        slot(t, t)


def row(buf, t):
    return buf[:, bass.ds(t, 1), :].rearrange("p a n -> p (a n)")


def halves(stats):
    return stats[:, :, 1], stats[:, :, 2], stats[:, :, 4], stats[:, :, 5]


def norm_from_stats(v, act_done, sem, stats, tmp, mean, rstd, var_only=None):
    m0, q0, m1, q1 = halves(stats)
    v.tensor_tensor(tmp[:, 1, :], m0, m1, ALU.subtract).then_inc(sem, 1)
    v.tensor_tensor(tmp[:, 2, :], q0, q1, ALU.add).then_inc(sem, 1)
    v.tensor_tensor(mean[:, :], m0, m1, ALU.add).then_inc(sem, 1)
    v.wait_ge(sem, act_done + 3)
    v.tensor_tensor(tmp[:, 3, :], tmp[:, 1, :], tmp[:, 1, :], ALU.mult).then_inc(sem, 1)
    v.tensor_scalar(tmp[:, 2, :], tmp[:, 2, :], 1.0 / D, EPS, ALU.mult, ALU.add).then_inc(sem, 1)
    v.tensor_scalar(mean[:, :], mean[:, :], 0.5, None, ALU.mult).then_inc(sem, 1)
    v.wait_ge(sem, act_done + 6)
    v.scalar_tensor_tensor(tmp[:, 0, :], tmp[:, 3, :], 0.25, tmp[:, 2, :], ALU.mult, ALU.add).then_inc(sem, 1)
    return act_done + 7


class LayerSemaphores:

    def __init__(self, nc):
        self.nc, self.held = nc, []

    def __enter__(self):
        return self

    def new(self, name):
        self.held.append(self.nc.alloc_semaphore(name))
        return self.held[-1]

    def __exit__(self, *failed):
        if failed[0] is None:
            self.nc.clear_and_free_semaphores(self.held)
            self.nc.all_engine_barrier()


def layer0_attention(nc, io, keep):
    with ExitStack() as ctx:
        def sb(name, shape, dt=F32):
            return ctx.enter_context(nc.sbuf_tensor(name, shape, dt))

        def bank(name):
            return ctx.enter_context(nc.psum_tensor(name, [P, 512], F32))

        sem = keep.sems.new

        x = sb("x_in", [P, T, D])
        ctxT = sb("ctxT", [KC, 2, B, 2, SK])
        wq, wo = sb("wq0", [P, KD, D]), sb("wo0", [P, KD, D])
        wk, wv = sb("wk0", [KC, 2, D]), sb("wv0", [KC, 2, D])
        bqT, bkT, bvT = sb("bqT", [P, KD]), sb("bkT", [P, KD]), sb("bvT", [P, KD])
        bv, bo = sb("bv_rows", [P, D]), sb("bo_rows", [P, D])
        headmask = sb("headmask", [P, 8])
        kT = sb("kT", [P, KD, B, SK])
        kbd = sb("k_blockdiag", [P, B, KD, 8, SK])
        vbd = sb("v_blockdiag", [P, B, HP0, 2 * (DH0 + 1)])
        csum = sb("ctx_sum", [KC, 2, B])
        vmT = sb("vmeanT", [P, KD, B])
        vmTw = sb("vmeanT_wide", [P, KD, B, P])
        gv = sb("guard_rows", [P, B, D])
        stats = sb("stats_x", [P, T, 6])
        tmp, mean, rstd = sb("tmp_x", [P, 4, T]), sb("mean_x", [P, T]), sb("rstd_x", [P, T])
        xn = sb("xn", [P, 2, D])
        xnT, qT = sb("xnT", [P, 2, KD, P]), sb("qT", [P, 2, KD, P])
        sc = sb("scores", [P, 2, H0, SK])
        top = sb("rowmax", [P, 2, H0])
        pT = sb("probsT", [P, 2, HP0, P])
        junk = sb("junk", [P, 2, 512], BF16)
        nanp, nans, nanm = sb("nan_part", [P, 4]), sb("nan_sum", [P, 1]), sb("nan_mask", [P, 1])
        ones = sb("ones", [P, P])
        nanw = sb("nan_wide", [P, D], I32)
        zeros = sb("zeros", [P, 2 * D])
        rden, oN, oT = sb("rden", [P, H0]), sb("oN", [P, D]), sb("oT", [P, KD, P])

        s0 = [ctx.enter_context(nc.psum_tensor(f"S{i}", [P, 2, 512], F32)) for i in range(2)]
        pt0 = ctx.enter_context(nc.psum_tensor("PT", [P, 2, 512], F32))
        m0, m1 = bank("M0"), bank("M1")

        ld_x = [sem(f"ld_x{b}") for b in range(B)]
        ld_w = sem("ld_w")
        ld_ctx = sem("ld_ctx")
        gates = sem("gates_done")
        dve = sem("dve_chain")
        pool = sem("pool_chain")
        setup_mm = sem("setup_matmuls")
        kbd_ok, vbd_ok = sem("kbd_ready"), sem("vbd_ready")
        std_ok, rstd_ok = sem("std_ready"), sem("rstd_ready")
        xn_ok, xT_ok, xnT_ok, q_ok, qT_ok = (sem(n) for n in ("xn_ready", "xT_in_psum", "xnT_ready", "q_in_psum", "qT_ready"))
        s_ok, max_ok, cmax_ok, clip_ok, abs_ok = (sem(n) for n in ("scores_ready", "max_ready", "cmax_ready", "clip_ready", "abs_done"))
        sub_ok, exp_ok = sem("shifted_ready"), sem("probs_ready")
        pT_ok, pTa_ok, pTd_ok = sem("probsT_in_psum"), sem("probsT_act_half"), sem("probsT_dve_half")
        o_ok, rden_ok, oN_ok, oT_ok, oTs_ok, wo_ok = (sem(n) for n in ("o_in_psum", "rden_ready", "oN_ready", "oT_in_psum", "oT_ready", "proj_ready"))
        res_ok, xb_ok, xg_ok = sem("x1_ready"), sem("xb_ready"), sem("xg_ready")
        st_ok, nan_ok, flag_ok = sem("stats_done"), sem("nan_added"), sem("flag_ready")
        zero_ok = sem("zeros_ready")
        gv_ok, vm_ok = sem("gv_ready"), sem("vm_ready")

        xv = io["x"].rearrange("(n p) d -> p n d", p=P)
        cv = io["ctxT"].rearrange("(k c) (b s) -> c k b s", k=2, b=B)

        N_SMALL = 10
        blk = ctx.enter_context(nc.Block())

        @blk.sync
        def _(sp):
            for b in range(B):
                sp.dma_start(x[:, TB * b:TB * b + TB, :], xv[:, TB * b:TB * b + TB, :]).then_inc(ld_x[b], 16)
            for k in range(2):
                for dup in range(2):
                    sp.dma_start(ctxT[:, k, :, dup, :], cv[:, k]).then_inc(ld_ctx, 16)
            sp.dma_start(wk[:, :, :], io["wk0"].rearrange("(k c) n -> c k n", k=2)).then_inc(ld_ctx, 16)
            sp.dma_start(wv[:, :, :], io["wv0"].rearrange("(k c) n -> c k n", k=2)).then_inc(ld_ctx, 16)
            sp.dma_start(wq[:, :, :], io["wq0"].rearrange("(k c) n -> c k n", k=KD)).then_inc(ld_w, 16)
            sp.dma_start(wo[:, :, :], io["wo0"].rearrange("(k c) n -> c k n", k=KD)).then_inc(ld_w, 16)
            sp.dma_start(keep.gate[:, 0:2], io["g_xattn"].partition_broadcast(P)).then_inc(ld_w, 16)
            sp.dma_start(keep.gate[:, 2:4], io["g_ffn"].partition_broadcast(P)).then_inc(ld_w, 16)
            sp.dma_start(bqT[:, :], io["bq0T"]).then_inc(ld_w, 16)
            sp.dma_start(bkT[:, :], io["bk0T"]).then_inc(ld_w, 16)
            sp.dma_start(bvT[:, :], io["bv0T"]).then_inc(ld_w, 16)
            sp.dma_start(bv[:, :], io["bv0"].partition_broadcast(P)).then_inc(ld_w, 16)
            sp.dma_start(bo[:, :], io["bo0"].partition_broadcast(P)).then_inc(ld_w, 16)
            sp.dma_start(headmask[:, :], io["headmask16"]).then_inc(ld_w, 16)
            sp.dma_start(keep.ident[:, :], io["ident"]).then_inc(ld_w, 16)
            sp.dma_start(keep.ustrict[:, :], io["ustrict"]).then_inc(ld_w, 16)
            sp.wait_ge(zero_ok, 1)
            for tag, slots in keep.xslots.items():
                sp.dma_start(slots.rearrange("(n p) d -> p n d", p=P),
                             zeros[:, 0:D].unsqueeze(1).to_broadcast([P, slots.shape[0] // P, D])).then_inc(keep.zeroed[tag], 16)
            for e in range(E):
                sp.dma_start(keep.w1[:, e, :, :], io["w1_0"][e].rearrange("(k c) n -> c k n", k=KD)).then_inc(keep.ld_w1, 16)


        @blk.gpsimd
        def _(gp):
            gp.memset(zeros[:, :], 0.0).then_inc(zero_ok, 1)
            gp.memset(ones[:, :], 1.0).then_inc(pool, 1)
            gp.memset(vbd[:, :, :, :], 0.0).then_inc(pool, 1)
            gp.wait_ge(gates, 1)
            gp.tensor_scalar(bo[:, :], bo[:, :], keep.gate[:, 0:1], None, ALU.mult).then_inc(pool, 1)
            gp.wait_ge(pool, 3)
            def slot(t, at):
                if 0 <= at < T:
                    gp.wait_ge(clip_ok, t + 1)
                    gp.wait_ge(cmax_ok, t + 1)
                    b = sc[:, at % 2, :, :]
                    gp.tensor_tensor(b, b, top[:, at % 2, :].unsqueeze(2).to_broadcast([P, H0, SK]), ALU.subtract).then_inc(sub_ok, 1)
                    gp.tensor_tensor(row(x, t), row(x, t), bo[:, :], ALU.add).then_inc(xb_ok, 1)
            for b in range(B):
                gp.wait_ge(ld_x[b], 16)
            gp.wait_ge(rstd_ok, 1)
            gp.wait_ge(xn_ok, 1)
            pipeline(gp, slot, 0, 2, T, T - 1)
            gp.wait_ge(res_ok, T)
            gp.wait_ge(gv_ok, B)
            for b in range(B):
                xr = x[:, TB * b:TB * b + TB, :]
                gp.tensor_tensor(xr, xr, gv[:, b, :].unsqueeze(1).to_broadcast([P, TB, D]), ALU.add).then_inc(xg_ok, 1)

        @blk.scalar
        def _(act):
            act.wait_ge(ld_w, 16 * (N_SMALL + 2))
            nc.scalar.activation(keep.gate[:, :], keep.gate[:, :], ACT.Tanh).then_inc(gates, 1)
            act.wait_ge(rstd_ok, 1)
            nc.scalar.activation(rstd[:, :], tmp[:, 0, :], ACT.Sqrt).then_inc(std_ok, 1)

            def slot(t, at):
                if 0 <= at + 1 < T:
                    u = (at + 1) % 2
                    act.wait_ge(xT_ok, t + 2)
                    wait(act, q_ok, t, at)
                    nc.scalar.activation(xnT[:, u, :, :], m0[:, 0:KD * P].rearrange("p (k n) -> p k n", k=KD), ACT.Copy).then_inc(xnT_ok, 1)
                if 0 <= at - 2 < T:
                    act.wait_ge(oT_ok, t - 1)
                    wait(act, wo_ok, t - 2, at - 2)
                    nc.scalar.activation(oT[:, :, :], m1[:, 0:KD * P].rearrange("p (k n) -> p k n", k=KD), ACT.Copy).then_inc(oTs_ok, 1)
                if 0 <= at < T:
                    act.wait_ge(clip_ok, t + 1)
                    for h in range(2):
                        if h == 0:
                            wait(act, nan_ok, t - 1, at - 1)
                        nc.scalar.activation(junk[:, h, :], s0[at % 2][:, h, :], ACT.Abs,
                                             accum_out=nanp[:, 2 * (at % 2) + h:2 * (at % 2) + h + 1]).then_inc(abs_ok, 1)
                if 0 <= at - 1 < T:
                    act.wait_ge(pT_ok, t)
                    nc.scalar.activation(pT[:, (at - 1) % 2, 0:4, :], pt0[:, 0, :].rearrange("p (a n) -> p a n", n=P), ACT.Copy).then_inc(pTa_ok, 1)
                if 0 <= at < T:
                    act.wait_ge(sub_ok, t + 1)
                    nc.scalar.activation(sc[:, at % 2, :, :], sc[:, at % 2, :, :], ACT.Exp).then_inc(exp_ok, 1)
            pipeline(act, slot, -1, 3, T - 1, T + 1)

        @blk.tensor
        def _(pe):
            pe.wait_ge(ld_ctx, 16 * 6)
            for m in range(KD):
                for k in range(2):
                    mm = nc.tensor.matmul(s0[0][:, m, 0:B * SK], wk[:, k, m * P:(m + 1) * P], ctxT[:, k, :, 0, :],
                                          start=(k == 0), stop=(k == 1))
                mm.then_inc(setup_mm, 1)
            for b in range(B):
                for k in range(2):
                    mm = nc.tensor.matmul((s0[1], pt0)[b // 2][:, b % 2, 0:D], ctxT[:, k, b, :, :].rearrange("c u s -> c (u s)"), wv[:, k, :],
                                          start=(k == 0), stop=(k == 1))
                mm.then_inc(setup_mm, 1)
            pe.wait_ge(vm_ok, 1)
            for m in range(KD):
                for k in range(2):
                    mm = nc.tensor.matmul(m1[:, m * B:(m + 1) * B], wv[:, k, m * P:(m + 1) * P], csum[:, k, :],
                                          start=(k == 0), stop=(k == 1))
            mm.then_inc(setup_mm, 1)
            pe.wait_ge(vm_ok, 3)
            pe.wait_ge(ld_w, 16 * (N_SMALL + 2))
            for b in range(B):
                pe.wait_ge(vbd_ok, 2 * B + 2)
                for k in range(KD):
                    mm = nc.tensor.matmul((s0[1], pt0)[b // 2][:, b % 2, 0:D], vmTw[:, k, b, :], wo[:, k, :],
                                          start=(k == 0), stop=(k == KD - 1))
                mm.then_inc(setup_mm, 1)
            pe.wait_ge(gv_ok, B)
            pe.wait_ge(kbd_ok, B * KD)

            def slot(t, at):
                if 0 <= at + 1 < T:
                    u = (at + 1) % 2
                    pe.wait_ge(xn_ok, t + 2)
                    wait(pe, qT_ok, t + 1, at + 1)
                    for k in range(KD):
                        mm = nc.tensor.transpose(m0[:, k * P:(k + 1) * P], xn[:, u, k * P:(k + 1) * P], keep.ident[:, :])
                    mm.then_inc(xT_ok, 1)
                if 0 <= at - 2 < T:
                    pe.wait_ge(oN_ok, t - 1)
                    for k in range(KD):
                        mm = nc.tensor.transpose(m1[:, k * P:(k + 1) * P], oN[:, k * P:(k + 1) * P], keep.ident[:, :])
                    mm.then_inc(oT_ok, 1)
                if 0 <= at < T:
                    pe.wait_ge(qT_ok, t + 1)
                    wait(pe, clip_ok, t - 1, at - 1)
                    wait(pe, abs_ok, 2 * t - 2, 2 * at - 2)
                    for m in range(KD):
                        mm = nc.tensor.matmul(s0[at % 2][:, m, :], qT[:, at % 2, m, :],
                                              kbd[:, bass.ds(t // TB, 1), m, :, :].rearrange("p a h s -> p (a h s)"),
                                              start=True, stop=True)
                    mm.then_inc(s_ok, 1)
                if 0 <= at + 1 < T:
                    u = (at + 1) % 2
                    pe.wait_ge(xnT_ok, t + 2)
                    for m in range(KD):
                        for k in range(KD):
                            mm = nc.tensor.matmul(m0[:, m * P:(m + 1) * P], wq[:, k, m * P:(m + 1) * P], xnT[:, u, k, :],
                                                  start=(k == 0), stop=(k == KD - 1))
                    mm.then_inc(q_ok, 1)
                if 0 <= at - 2 < T:
                    pe.wait_ge(oTs_ok, t - 1)
                    for k in range(KD):
                        mm = nc.tensor.matmul(m1[:, 0:D], oT[:, k, :], wo[:, k, :], start=(k == 0), stop=(k == KD - 1))
                    mm.then_inc(wo_ok, 1)
                if 0 <= at - 1 < T:
                    u = (at - 1) % 2
                    pe.wait_ge(exp_ok, t)
                    wait(pe, pTa_ok, t - 1, at - 1)
                    wait(pe, pTd_ok, t - 1, at - 1)
                    for a in range(HP0):
                        mm = nc.tensor.transpose(pt0[:, a // 4, (a % 4) * P:(a % 4 + 1) * P],
                                                 sc[:, u, 2 * a:2 * a + 2, :].rearrange("p h s -> p (h s)"), keep.ident[:, :])
                    mm.then_inc(pT_ok, 1)
                    pe.wait_ge(pTa_ok, t)
                    pe.wait_ge(pTd_ok, t)
                    wait(pe, res_ok, t - 1, at - 1)
                    for a in range(HP0):
                        mm = nc.tensor.matmul(m1[:, 34 * a:34 * a + 34], pT[:, u, a, :],
                                              vbd[:, bass.ds((t - 1) // TB, 1), a, :].rearrange("p a n -> p (a n)"), start=True, stop=True)
                    mm.then_inc(o_ok, 1)
            pipeline(pe, slot, -1, 3, T - 1, T + 1)
            pe.wait_ge(flag_ok, 1)
            nc.tensor.matmul(m0[:, 0:1], ones[:, :], nans[:, :], start=True, stop=True).then_inc(setup_mm, 1)

        @blk.vector
        def _(v):
            v.memset(nans[:, :], 0.0).then_inc(dve, 1)
            for b in range(B):
                v.wait_ge(ld_x[b], 16)
                for t in range(TB * b, TB * b + TB):
                    v.bn_stats(stats[:, t, :], x[:, t, :]).then_inc(dve, 1)
            v.wait_ge(dve, 1 + T)
            n = norm_from_stats(v, 1 + T, dve, stats, tmp, mean, rstd)
            v.wait_ge(dve, n)
            v.sem_inc(rstd_ok, 1)
            v.wait_ge(ld_ctx, 16 * 6)
            v.reduce_sum(csum[:, :, :], ctxT[:, :, :, 0, :], AX).then_inc(vm_ok, 1)
            v.wait_ge(ld_w, 16 * (N_SMALL + 2))
            for m in range(KD):
                v.wait_ge(setup_mm, m + 1)
                v.tensor_scalar(kT[:, m, :, :], s0[0][:, m, 0:B * SK].rearrange("p (b s) -> p b s", b=B), bkT[:, m:m + 1], None, ALU.add).then_inc(dve, 1)
            v.wait_ge(dve, n + 2)
            for m in range(KD):
                for b in range(B):
                    v.tensor_tensor(kbd[:, b, m, :, :], kT[:, m, b, :].unsqueeze(1).to_broadcast([P, 8, SK]),
                                    headmask[:, :].unsqueeze(2).to_broadcast([P, 8, SK]), ALU.mult).then_inc(kbd_ok, 1)
            v.wait_ge(pool, 2)
            for u in range(2):
                v.memset(vbd[64 * u:64 * u + 64, :, :, 17 * u + DH0:17 * u + DH0 + 1], 1.0).then_inc(vbd_ok, 1)
            bvv = bv[:, :].rearrange("p (a u j) -> p a u j", u=2, j=DH0)
            for b in range(B):
                v.wait_ge(setup_mm, KD + b + 1)
                vp = (s0[1], pt0)[b // 2][:, b % 2, 0:D].rearrange("p (a u j) -> p a u j", u=2, j=DH0)
                for u in range(2):
                    q = slice(64 * u, 64 * u + 64)
                    v.tensor_tensor(vbd[q, b, :, 17 * u:17 * u + DH0], vp[q, :, u, :], bvv[q, :, u, :], ALU.add).then_inc(vbd_ok, 1)
            v.wait_ge(setup_mm, KD + B + 1)
            for m in range(KD):
                v.tensor_scalar(vmT[:, m, :], m1[:, m * B:(m + 1) * B], 1.0 / SK, bvT[:, m:m + 1], ALU.mult, ALU.add).then_inc(dve, 1)
            v.wait_ge(dve, n + 4)
            for m in range(KD):
                v.tensor_copy(vmTw[:, m, :, :], vmT[:, m, :].unsqueeze(2).to_broadcast([P, B, P])).then_inc(vm_ok, 1)
            v.wait_ge(gates, 1)
            for b in range(B):
                v.wait_ge(setup_mm, KD + B + 2 + b)
                v.tensor_scalar(gv[:, b, :], (s0[1], pt0)[b // 2][:, b % 2, 0:D], keep.gate[:, 0:1], None, ALU.mult).then_inc(gv_ok, 1)
            v.wait_ge(std_ok, 1)
            v.reciprocal(rstd[:, :], rstd[:, :]).then_inc(dve, 1)
            v.wait_ge(dve, n + 5)

            def slot(t, at):
                if 0 <= at + 2 < T:
                    wait(v, xT_ok, t + 1, at + 1)
                    v.tensor_scalar(xn[:, at % 2, :], row(x, t + 2), mean[:, bass.ds(t + 2, 1)], rstd[:, bass.ds(t + 2, 1)],
                                    ALU.subtract, ALU.mult).then_inc(xn_ok, 1)
                if 0 <= at + 1 < T:
                    u = (at + 1) % 2
                    v.wait_ge(q_ok, t + 2)
                    wait(v, s_ok, t, at)
                    v.tensor_tensor(qT[:, u, :, :], m0[:, 0:KD * P].rearrange("p (k n) -> p k n", k=KD),
                                    bqT[:, :].unsqueeze(2).to_broadcast([P, KD, P]), ALU.add).then_inc(qT_ok, 1)
                if 0 <= at < T:
                    u = at % 2
                    sv = s0[u][:, :, :].rearrange("p m (h s) -> p (m h) s", s=SK)
                    v.wait_ge(s_ok, t + 1)
                    wait(v, sub_ok, t - 1, at - 1)
                    v.reduce_max(top[:, u, :], sv, AX).then_inc(max_ok, 1)
                    wait(v, pT_ok, t - 1, at - 1)
                    v.tensor_scalar(sc[:, u, :, :], sv, CLAMP, -CLAMP, ALU.min, ALU.max).then_inc(clip_ok, 1)
                    v.wait_ge(max_ok, t + 1)
                    v.tensor_scalar(top[:, u, :], top[:, u, :], CLAMP, -CLAMP, ALU.min, ALU.max).then_inc(cmax_ok, 1)
                if 0 <= at - 2 < T:
                    v.wait_ge(wo_ok, t - 1)
                    v.wait_ge(xb_ok, t - 1)
                    v.scalar_tensor_tensor(row(keep.x1, t - 2), m1[:, 0:D], keep.gate[:, 0:1], row(x, t - 2), ALU.mult, ALU.add).then_inc(res_ok, 1)
                if 0 <= at - 1 < T:
                    v.wait_ge(pT_ok, t)
                    v.tensor_copy(pT[:, (at - 1) % 2, 4:8, :], pt0[:, 1, :].rearrange("p (a n) -> p a n", n=P)).then_inc(pTd_ok, 1)
                    ov = m1[:, 0:34 * HP0].rearrange("p (h j) -> p h j", j=DH0 + 1)
                    v.wait_ge(o_ok, t)
                    v.reciprocal(rden[:, :], ov[:, :, DH0]).then_inc(rden_ok, 1)
                    v.wait_ge(rden_ok, t)
                    wait(v, oT_ok, t - 1, at - 1)
                    v.tensor_tensor(oN[:, :].rearrange("p (h j) -> p h j", j=DH0), ov[:, :, 0:DH0],
                                    rden[:, :].unsqueeze(2).to_broadcast([P, H0, DH0]), ALU.mult).then_inc(oN_ok, 1)
                if 0 <= at < T:
                    v.wait_ge(abs_ok, 2 * t + 2)
                    wait(v, nan_ok, t, at)
                    v.scalar_tensor_tensor(nans[:, :], nanp[:, 2 * (at % 2):2 * (at % 2) + 1], nanp[:, 2 * (at % 2) + 1:2 * (at % 2) + 2],
                                           nans[:, :], ALU.add, ALU.add).then_inc(nan_ok, 1)
            pipeline(v, slot, -2, 4, T - 2, T + 1)
            v.wait_ge(nan_ok, T)
            v.tensor_tensor(nans[:, :], nans[:, :], nans[:, :], ALU.not_equal).then_inc(flag_ok, 1)
            v.wait_ge(setup_mm, KD + B + 1 + B + 1)
            v.tensor_scalar(nanm[:, :], m0[:, 0:1], 0.0, None, ALU.is_gt).then_inc(flag_ok, 1)
            v.wait_ge(flag_ok, 2)
            v.tensor_copy(nanw[:, :], nanm[:, :].to_broadcast([P, D])).then_inc(flag_ok, 1)
            v.wait_ge(flag_ok, 3)
            v.wait_ge(xg_ok, B)
            v.wait_ge(res_ok, T)
            v.copy_predicated(keep.x1[:, :, :], nanw[:, :].unsqueeze(1).to_broadcast([P, T, D]), x[:, :, :]).then_inc(st_ok, 1)
            v.wait_ge(st_ok, 1)
            with v.Fori(0, T) as t:
                v.bn_stats(row(keep.stats, t), row(keep.x1, t)).then_inc(st_ok, 1)



def routed_experts(nc, io, keep, K, F, act_fn, gate_col, tag):
    V = K * T
    NT = V + E - 1
    KF = F // P
    HB = F // 512
    xslots, yslots = keep.xslots[tag], keep.yslots[tag]

    with ExitStack() as ctx:
        def sb(name, shape, dt=F32):
            return ctx.enter_context(nc.sbuf_tensor(f"{name}{tag}", shape, dt))

        rows = sb("ln_rows", [P, T, D])
        picks = sb("picks", [P, V], U32)
        prob = sb("prob", [P, V])
        tile_expert = sb("tile_expert", [P, NT], I32)
        hot = sb("tile_hot", [3 * E, NT, P], BF16)
        b1x, b2x = sb("b1_parts", [3 * E, F], BF16), sb("b2_parts", [3 * E, D], BF16)

        with ExitStack() as rctx:
            def rb(name, shape, dt=F32):
                return rctx.enter_context(nc.sbuf_tensor(f"{name}{tag}", shape, dt))

            def rsem(name):
                return keep.sems.new(f"{name}{tag}")

            xs, xsT = rb("xs", [P, 2, D]), rb("xsT", [P, 2, KD, P])
            tmp, mean, rstd = rb("tmp", [P, 4, T]), rb("mean", [P, T]), rb("rstd", [P, T])
            wg = rb("wg", [P, KD, E])
            bg = rb("bg", [P, E])
            lg, ex = rb("logits", [P, T, E]), rb("ex", [P, T, E])
            oh = rb("onehot", [P, V, E])
            pre = [rb(f"prefix{i}", [P, V, E]) for i in range(2)]
            lmax = rb("lmax", [P, 2, T])
            first = rb("first", [P, T])
            iota = rb("iota", [P, 2, E])
            iota_t = rb("iota_t", [P, NT])
            cnt, cnti = rb("cnt", [P, E]), rb("cnti", [P, E], I32)
            ends = [rb(f"ends{i}", [P, E]) for i in range(2)]
            base = rb("base", [P, E])
            slotf = rb("slot_f", [P, V])
            past = rb("past", [P, NT, E])
            tef = rb("tile_expert_f", [P, NT])
            part = rb("part", [3 * E, 4])
            bf = rb("b_split", [3 * E, 2, F])
            bh = rb("b_high", [3 * E, 2, F], BF16)
            xT_bank = [rctx.enter_context(nc.psum_tensor(f"xT_ps{tag}{i}", [P, 512], F32)) for i in range(2)]
            lg_bank = rctx.enter_context(nc.psum_tensor(f"lg{tag}", [P, 512], F32))
            rank_bank = rctx.enter_context(nc.psum_tensor(f"rank{tag}", [P, 512], F32))
            cnt_bank = rctx.enter_context(nc.psum_tensor(f"count_ps{tag}", [P, 512], F32))

            ld, dve, pool = rsem("ld_route"), rsem("dve_chain"), rsem("pool_chain")
            var_ok, std_ok, ones_ok = rsem("var_ready"), rsem("std_ready"), rsem("ones_ready")
            xs_ok, xT_ok, xsT_ok, lg_ok = rsem("xs_ready"), rsem("xT_in_psum"), rsem("xsT_ready"), rsem("logits_ready")
            rows_ok, shift_ok, ex_ok = rsem("rows_ready"), rsem("shifted_ready"), rsem("exp_ready")
            oh_ok, pre_ok, rank_ok = rsem("onehot_ready"), rsem("prefix_ready"), rsem("rank_ready")
            pick_ok, scattered = rsem("picks_ready"), rsem("scattered")

            blk = rctx.enter_context(nc.Block())

            @blk.sync
            def _(sp):
                sp.dma_start(wg[:, :, :], io["wg" + tag].rearrange("(k c) e -> c k e", k=KD)).then_inc(ld, 16)
                if K == 1:
                    sp.dma_start(bg[:, :], io["bg" + tag].partition_broadcast(P)).then_inc(ld, 16)
                sp.dma_start(iota[:, :, :], io["iota_e"].partition_broadcast(P)).then_inc(ld, 16)
                sp.dma_start(iota_t[:, :], io["iota_t"][0:NT].partition_broadcast(P)).then_inc(ld, 16)
                sp.dma_start(part[:, :], io["part"]).then_inc(ld, 16)
                for q in range(3):
                    sp.dma_start(bf[E * q:E * q + E, 0, :], io["b1_" + tag]).then_inc(ld, 16)
                    sp.dma_start(bf[E * q:E * q + E, 1, 0:D], io["b2_" + tag]).then_inc(ld, 16)
                if K == 1:
                    for e in range(E):
                        sp.dma_start(keep.w2[:, e, :, :], io["w2_" + tag][e].rearrange("(k c) n -> c k n", k=KF)).then_inc(keep.ld_w2, 16)

            LOADS = 16 * (11 if K == 1 else 10)

            @blk.gpsimd
            def _(gp):
                gp.wait_ge(ld, LOADS)
                n = 0
                def link(ins):
                    nonlocal n
                    n += 1
                    ins.then_inc(pool, 1)
                    gp.wait_ge(pool, n)
                for j, w, dst in ((0, F, b1x), (1, D, b2x)):
                    r = bf[:, j, 0:w]
                    hi = bh[:, 0, 0:w]
                    acc = bh[:, 1, 0:w]
                    for q in range(3):
                        link(gp.tensor_copy(hi, r))
                        if q == 0:
                            link(gp.tensor_scalar(dst[:, :], hi, part[:, 0:1], None, ALU.mult))
                        else:
                            link(gp.tensor_scalar(acc, hi, part[:, q:q + 1], None, ALU.mult))
                            link(gp.tensor_tensor(dst[:, :], dst[:, :], acc, ALU.add))
                        if q < 2:
                            link(gp.tensor_tensor(r, r, hi, ALU.subtract))
                gp.wait_ge(pick_ok, 1)
                gp.wait_ge(rows_ok, T)
                gp.wait_ge(keep.zeroed[tag], 16 * keep.zero_loads[tag])
                for c in range(V):
                    gp.indirect_dma_start(xslots, bass.IndirectOffsetOnAxis(ap=picks[:, c:c + 1], axis=0), rows[:, c % T, :], None,
                                          bounds_check=NT * P - 1, oob_is_err=False).then_inc(scattered, 16)
                gp.wait_ge(scattered, 16 * V)

            @blk.scalar
            def _(act):
                act.wait_ge(var_ok, 1)
                nc.scalar.activation(rstd[:, :], tmp[:, 0, :], ACT.Sqrt).then_inc(std_ok, 1)
                with act.Fori(0, T // 2) as i:
                    for u in range(2):
                        act.wait_ge(xT_ok, i * 2 + (u + 1))
                        nc.scalar.activation(xsT[:, u, :, :], xT_bank[u][:, 0:D].rearrange("p (k n) -> p k n", k=KD), ACT.Copy).then_inc(xsT_ok, 1)
                act.wait_ge(shift_ok, 1)
                shifted = ex[:, :, :] if K == 1 else ex[:, :, 0]
                nc.scalar.activation(shifted, shifted, ACT.Exp).then_inc(ex_ok, 1)

            @blk.tensor
            def _(pe):
                pe.wait_ge(ld, LOADS)

                def slot(t, at):
                    u = at % 2
                    if at < T:
                        pe.wait_ge(xs_ok, t + 1)
                        wait(pe, xsT_ok, t - 1, at - 1)
                        for k in range(KD):
                            mm = nc.tensor.transpose(xT_bank[u][:, k * P:(k + 1) * P], xs[:, u, k * P:(k + 1) * P], keep.ident[:, :])
                        mm.then_inc(xT_ok, 1)
                    if at >= 1:
                        pe.wait_ge(xsT_ok, t)
                        for k in range(KD):
                            mm = nc.tensor.matmul(lg_bank[:, bass.ds((t - 1) * E, E)], xsT[:, 1 - u, k, :], wg[:, k, :],
                                                  start=(k == 0), stop=(k == KD - 1))
                        mm.then_inc(lg_ok, 1)
                pipeline(pe, slot, 0, 2, T, T)
                pe.wait_ge(oh_ok, 1)
                nc.tensor.matmul(rank_bank[:, 0:V * E], keep.ustrict[:, :], oh[:, :, :].rearrange("p v e -> p (v e)"), start=True, stop=False)
                pe.wait_ge(pre_ok, 1)
                pe.wait_ge(ones_ok, 1)
                nc.tensor.matmul(rank_bank[:, 0:V * E], keep.ones[:, :], pre[1][:, :, :].rearrange("p v e -> p (v e)"), start=False, stop=True).then_inc(rank_ok, 1)
                nc.tensor.matmul(cnt_bank[:, 0:E], keep.ones[:, :], pre[1][:, V - 1, :], start=True, stop=False)
                nc.tensor.matmul(cnt_bank[:, 0:E], keep.ones[:, :], oh[:, V - 1, :], start=False, stop=True).then_inc(rank_ok, 1)

            @blk.vector
            def _(v):
                done = [0]

                def link(ins):
                    done[0] += 1
                    ins.then_inc(dve, 1)
                    v.wait_ge(dve, done[0])

                def e_cols(a):
                    return a.unsqueeze(2).to_broadcast([P, T, E])

                def over_t(a, n=T):
                    return a.unsqueeze(1).to_broadcast([P, n, E])

                v.memset(keep.ones[:, :], 1.0).then_inc(ones_ok, 1)
                done[0] = norm_from_stats(v, 0, dve, keep.stats, tmp, mean, rstd)
                v.wait_ge(dve, done[0])
                v.sem_inc(var_ok, 1)
                v.wait_ge(std_ok, 1)
                link(v.reciprocal(rstd[:, :], rstd[:, :]))

                def ln(dst, t, ok):
                    v.tensor_scalar(dst, row(keep.x1, t), mean[:, bass.ds(t, 1)], rstd[:, bass.ds(t, 1)], ALU.subtract, ALU.mult).then_inc(ok, 1)

                def slot(t, at):
                    wait(v, xT_ok, t - 1, at - 1)
                    ln(xs[:, at % 2, :], t, xs_ok)
                    ln(row(rows, t), t, rows_ok)
                pipeline(v, slot, 0, 2, T, T - 1)

                v.wait_ge(lg_ok, T)
                v.wait_ge(ld, LOADS)
                logits = lg_bank[:, 0:T * E].rearrange("p (t e) -> p t e", e=E)
                link(v.tensor_tensor(lg[:, :, :], logits, over_t(bg[:, :]), ALU.add) if K == 1 else v.tensor_copy(lg[:, :, :], logits))
                for c in range(K):
                    o = oh[:, c * T:(c + 1) * T, :]
                    link(v.reduce_max(lmax[:, c, :], lg[:, :, :], AX))
                    link(v.tensor_tensor(o, lg[:, :, :], e_cols(lmax[:, c, :]), ALU.is_equal))
                    link(v.tensor_tensor(o, o, over_t(iota[:, 0, :]), ALU.mult))
                    link(v.tensor_reduce(first[:, :], o, AX, ALU.min))
                    link(v.tensor_tensor(o, e_cols(first[:, :]), over_t(iota[:, 0, :]), ALU.is_equal))
                    if c == 0:
                        if K == 1:
                            v.tensor_tensor(ex[:, :, :], lg[:, :, :], e_cols(lmax[:, 0, :]), ALU.subtract).then_inc(shift_ok, 1)
                        else:
                            link(v.scalar_tensor_tensor(lg[:, :, :], o, LOWEST, lg[:, :, :], ALU.mult, ALU.add))
                if K == 2:
                    v.tensor_tensor(ex[:, :, 0], lmax[:, 1, :], lmax[:, 0, :], ALU.subtract).then_inc(shift_ok, 1)
                v.sem_inc(oh_ok, 1)
                cur, w, n = oh, 1, 0
                while w < V:
                    dst = pre[n % 2]
                    v.tensor_copy(dst[:, 0:w, :], cur[:, 0:w, :]).then_inc(dve, 1)
                    v.tensor_tensor(dst[:, w:V, :], cur[:, w:V, :], cur[:, 0:V - w, :], ALU.add).then_inc(dve, 1)
                    done[0] += 2
                    v.wait_ge(dve, done[0])
                    cur = dst
                    w *= 2
                    n += 1
                other = pre[n % 2]
                link(v.tensor_tensor(other[:, :, :], cur[:, :, :], oh[:, :, :], ALU.subtract))
                if other is not pre[1]:
                    link(v.tensor_copy(pre[1][:, :, :], other[:, :, :]))
                v.sem_inc(pre_ok, 1)
                v.wait_ge(ex_ok, 1)
                gate = keep.gate[:, gate_col:gate_col + 1]
                if K == 1:
                    link(v.reduce_sum(first[:, :], ex[:, :, :], AX))
                    link(v.reciprocal(first[:, :], first[:, :]))
                    v.tensor_scalar(prob[:, 0:T], first[:, :], gate, None, ALU.mult).then_inc(dve, 1)
                    done[0] += 1
                else:
                    link(v.tensor_scalar(first[:, :], ex[:, :, 0], 1.0, None, ALU.add))
                    link(v.reciprocal(first[:, :], first[:, :]))
                    link(v.tensor_scalar(prob[:, 0:T], first[:, :], gate, None, ALU.mult))
                    v.tensor_tensor(prob[:, T:2 * T], prob[:, 0:T], ex[:, :, 0], ALU.mult).then_inc(dve, 1)
                    done[0] += 1
                v.wait_ge(rank_ok, 2)
                link(v.tensor_scalar(cnt[:, :], cnt_bank[:, 0:E], float(P - 1), None, ALU.add))
                link(v.tensor_copy(cnti[:, :], cnt[:, :]))
                link(v.tensor_scalar(cnti[:, :], cnti[:, :], 7, None, ALU.arith_shift_right))
                link(v.tensor_copy(cnt[:, :], cnti[:, :]))
                cur, w, n = cnt, 1, 0
                while w < E:
                    dst = ends[n % 2]
                    v.tensor_copy(dst[:, 0:w], cur[:, 0:w]).then_inc(dve, 1)
                    v.tensor_tensor(dst[:, w:E], cur[:, w:E], cur[:, 0:E - w], ALU.add).then_inc(dve, 1)
                    done[0] += 2
                    v.wait_ge(dve, done[0])
                    cur, w, n = dst, 2 * w, n + 1
                tends = cur
                link(v.tensor_tensor(base[:, :], tends[:, :], cnt[:, :], ALU.subtract))
                link(v.tensor_scalar(base[:, :], base[:, :], float(P), None, ALU.mult))
                link(v.tensor_tensor(pre[0][:, :, :], rank_bank[:, 0:V * E].rearrange("p (v e) -> p v e", e=E), over_t(base[:, :], V), ALU.add))
                link(v.tensor_tensor(pre[0][:, :, :], pre[0][:, :, :], oh[:, :, :], ALU.mult))
                link(v.reduce_sum(slotf[:, :], pre[0][:, :, :], AX))
                v.tensor_copy(picks[:, :], slotf[:, :]).then_inc(pick_ok, 1)
                link(v.tensor_tensor(past[:, :, :], iota_t[:, :].unsqueeze(2).to_broadcast([P, NT, E]), over_t(tends[:, :], NT), ALU.is_ge))
                link(v.reduce_sum(tef[:, :], past[:, :, :], AX))
                link(v.tensor_scalar(tef[:, :], tef[:, :], float(E - 1), None, ALU.min))
                v.tensor_copy(tile_expert[:, :], tef[:, :]).then_inc(dve, 1)
                v.tensor_scalar(hot[:, :, :], tef[0:3 * E, :].unsqueeze(2).to_broadcast([3 * E, NT, P]), part[:, 3:4], None, ALU.is_equal).then_inc(dve, 1)
                v.wait_ge(dve, done[0] + 2)

        with ExitStack() as ectx:
            def eb(name, shape, dt=F32):
                return ectx.enter_context(nc.sbuf_tensor(f"{name}{tag}", shape, dt))

            def esem(name):
                return keep.sems.new(f"{name}{tag}")

            xb, xT = eb("slot_rows", [P, 2, D]), eb("slotT", [P, 2, KD, P])
            hid, hT = eb("hidden", [P, 2, F]), eb("hiddenT", [P, KF, P])
            ys = eb("y_rows", [P, 2, D])
            h_ps = [ectx.enter_context(nc.psum_tensor(f"h_ps{tag}{i}", [P, HB, 512], F32)) for i in range(2)]
            hT_ps = [ectx.enter_context(nc.psum_tensor(f"hT_ps{tag}{i}", [P, 512], F32)) for i in range(2)]
            x_ps = ectx.enter_context(nc.psum_tensor(f"x_ps{tag}", [P, 512], F32))
            y_ps = ectx.enter_context(nc.psum_tensor(f"y_ps{tag}", [P, 512], F32))
            ld = [esem(f"slot_rows_{i}") for i in range(2)]
            stored = [esem(f"y_stored_{i}") for i in range(2)]
            xT_ok, xTs_ok, h_ok, act_ok = esem("x_in_psum"), esem("slotT_ready"), esem("h_in_psum"), esem("hidden_ready")
            hT_ok, hTa_ok, hTd_ok, y_ok, ys_ok = (esem(n) for n in ("hT_in_psum", "hT_act_half", "hT_dve_half", "y_in_psum", "y_ready"))
            ALL = NT
            EVEN = NT - NT % 2
            LASTF = EVEN - 2 if EVEN == NT else EVEN - 1
            TPB = KF // 2

            blk = ectx.enter_context(nc.Block())

            @blk.sync
            def _(sp):
                def slot(t, at):
                    u = at % 2
                    if at < ALL:
                        wait(sp, xT_ok, t - 1, at - 1)
                        sp.dma_start(xb[:, u, :], xslots[bass.ds(t * P, P), :]).then_inc(ld[u], 16)
                pipeline(sp, slot, 0, 2, EVEN, ALL - 1)

            @blk.gpsimd
            def _(gp):
                def slot(t, at):
                    u = at % 2
                    gp.wait_ge(ys_ok, t + 1)
                    gp.dma_start(yslots[bass.ds(t * P, P), :], ys[:, u, :]).then_inc(stored[u], 16)
                pipeline(gp, slot, 0, 2, EVEN, ALL - 1)
                gp.wait_ge(stored[0], 16 * ((ALL + 1) // 2))
                gp.wait_ge(stored[1], 16 * (ALL // 2))

            @blk.scalar
            def _(act):
                def slot(t, at):
                    if at + 1 < ALL:
                        act.wait_ge(xT_ok, t + 2)
                        wait(act, h_ok, t, at)
                        nc.scalar.activation(xT[:, (at + 1) % 2, :, :], x_ps[:, 0:D].rearrange("p (k n) -> p k n", k=KD), ACT.Copy).then_inc(xTs_ok, 1)
                    if 1 <= at <= ALL:
                        act.wait_ge(hT_ok, t)
                        wait(act, y_ok, t - 1, at - 1)
                        nc.scalar.activation(hT[:, 0:TPB, :], hT_ps[0][:, 0:TPB * P].rearrange("p (k n) -> p k n", n=P), ACT.Copy).then_inc(hTa_ok, 1)
                    if 0 <= at < ALL:
                        act.wait_ge(h_ok, t + 1)
                        wait(act, hT_ok, t - 1, at - 1)
                        nc.scalar.activation(hid[:, at % 2, :], h_ps[at % 2][:, :, :].rearrange("p b n -> p (b n)"), act_fn).then_inc(act_ok, 1)
                pipeline(act, slot, -1, 3, LASTF, ALL)

            @blk.tensor
            def _(pe):
                if K == 1:
                    pe.wait_ge(keep.ld_w1, 16 * E)
                else:
                    pe.wait_ge(keep.ld_w1, 16 * 2 * E)
                    pe.wait_ge(keep.ld_w2, 16 * 2 * E)

                def expert(t):
                    return pe.value_load(tile_expert[0:1, bass.ds(t, 1)], min_val=0, max_val=E - 1)

                def slot(t, at):
                    if at + 1 < ALL:
                        u = (at + 1) % 2
                        pe.wait_ge(ld[u], ((t + 1) // 2 + 1) * 16)
                        wait(pe, xTs_ok, t + 1, at + 1)
                        for k in range(KD):
                            mm = nc.tensor.transpose(x_ps[:, k * P:(k + 1) * P], xb[:, u, k * P:(k + 1) * P], keep.ident[:, :])
                        mm.then_inc(xT_ok, 1)
                    if 1 <= at <= ALL:
                        u = (at - 1) % 2
                        pe.wait_ge(act_ok, t)
                        wait(pe, hTa_ok, t - 1, at - 1)
                        wait(pe, hTd_ok, t - 1, at - 1)
                        for k in range(KF):
                            mm = nc.tensor.transpose(hT_ps[k // TPB][:, (k % TPB) * P:(k % TPB + 1) * P], hid[:, u, k * P:(k + 1) * P], keep.ident[:, :])
                        mm.then_inc(hT_ok, 1)
                    if 0 <= at < ALL:
                        u = at % 2
                        e = expert(t)
                        pe.wait_ge(xTs_ok, t + 1)
                        wait(pe, act_ok, t - 1, at - 1)
                        for n in range(HB):
                            for k in range(KD):
                                nc.tensor.matmul(h_ps[u][:, n, :], xT[:, u, k, :], keep.w1[:, bass.ds(e, 1), k, n * 512:(n + 1) * 512].rearrange("p a n -> p (a n)"),
                                                 start=(k == 0), stop=False)
                            mm = nc.tensor.matmul(h_ps[u][:, n, :], hot[:, bass.ds(t, 1), :].rearrange("p a n -> p (a n)"), b1x[:, n * 512:(n + 1) * 512],
                                                  start=False, stop=True)
                        mm.then_inc(h_ok, 1)
                    if 1 <= at <= ALL:
                        e = expert(t - 1)
                        if at == 1 and K == 1:
                            pe.wait_ge(keep.ld_w2, 16 * E)
                        pe.wait_ge(hTa_ok, t)
                        pe.wait_ge(hTd_ok, t)
                        wait(pe, ys_ok, t - 1, at - 1)
                        for k in range(KF):
                            nc.tensor.matmul(y_ps[:, 0:D], hT[:, k, :], keep.w2[:, bass.ds(e, 1), k, :].rearrange("p a n -> p (a n)"),
                                             start=(k == 0), stop=False)
                        mm = nc.tensor.matmul(y_ps[:, 0:D], hot[:, bass.ds(t - 1, 1), :].rearrange("p a n -> p (a n)"), b2x[:, :], start=False, stop=True)
                        mm.then_inc(y_ok, 1)
                pipeline(pe, slot, -1, 3, LASTF, ALL)

            @blk.vector
            def _(v):
                def slot(t, at):
                    v.wait_ge(hT_ok, t + 1)
                    wait(v, y_ok, t, at)
                    v.tensor_copy(hT[:, TPB:KF, :], hT_ps[1][:, 0:TPB * P].rearrange("p (k n) -> p k n", n=P)).then_inc(hTd_ok, 1)
                    v.wait_ge(y_ok, t + 1)
                    if at >= 2:
                        v.wait_ge(stored[at % 2], (t // 2) * 16)
                    v.tensor_copy(ys[:, at % 2, :], y_ps[:, 0:D]).then_inc(ys_ok, 1)
                pipeline(v, slot, 0, 2, EVEN, ALL - 1)

        with ExitStack() as gctx:
            more = [gctx.enter_context(nc.sbuf_tensor(f"second{tag}", [P, T, D], F32))] if K == 2 else []
            got = [rows, *more]
            new = keep.sems.new
            gathered = [new(f"gathered{tag}_{c}") for c in range(V)]
            added, stat = new(f"added{tag}"), new(f"row_stats{tag}")
            blk = gctx.enter_context(nc.Block())

            @blk.gpsimd
            def _(gp):
                for t in range(T):
                    for c in range(K):
                        gp.indirect_dma_start(got[c][:, t, :], None, yslots,
                                              bass.IndirectOffsetOnAxis(ap=picks[:, c * T + t:c * T + t + 1], axis=0),
                                              bounds_check=NT * P - 1, oob_is_err=False).then_inc(gathered[c * T + t], 16)

            @blk.vector
            def _(v):
                for t in range(T):
                    for c in range(K):
                        v.wait_ge(gathered[c * T + t], 16)
                        wait(v, added, K * t + c, K * t + c if c else 0)
                        v.scalar_tensor_tensor(keep.x1[:, t, :], got[c][:, t, :], prob[:, c * T + t:c * T + t + 1], keep.x1[:, t, :],
                                               ALU.mult, ALU.add).then_inc(added, 1)
                    if K == 1:
                        v.wait_ge(added, t + 1)
                        v.bn_stats(keep.stats[:, t, :], keep.x1[:, t, :]).then_inc(stat, 1)


H1 = 4
DQ = 128
DH1 = DQ // H1
TOP = 32
MOVED = -3.0e38


def layer1_attention(nc, io, keep, c):
    with ExitStack() as ctx:
        def sb(name, shape, dt=F32):
            return ctx.enter_context(nc.sbuf_tensor(name, shape, dt))

        def bank(name):
            return ctx.enter_context(nc.psum_tensor(name, [P, 512], F32))

        sem = keep.sems.new

        NF = 4 * D
        ctxT = sb("ctxT1", [KC, 2, B * SK])
        wq, wk, wv = sb("wq1", [P, KD, DQ]), sb("wk1", [KC, 2, DQ]), sb("wv1", [KC, 2, D])
        wf = sb("w_film", [P, KD, NF])
        mask4 = sb("headmask32", [P, H1])
        kbd = sb("k1_blockdiag", [P, B, H1, SK])
        vT = sb("v1T", [P, KD, B * SK])
        vw = sb("v_film", [SK + 1, B, NF])
        modg = sb("mod_gate", [P, 1])
        g_in, b_in = sb("g_norm_in", [P, D]), sb("b_norm_in", [P, D])
        key_u8, key_bias = sb("key_mask_u8", [P, B * SK], U8), sb("key_bias", [P, B, SK])
        tok_u8, tok = sb("token_mask_u8", [P, T], U8), sb("token_mask", [P, T])
        tmp, mean, rstd, rstd2 = sb("tmp_c", [P, 4, T]), sb("mean_c", [P, T]), sb("rstd_c", [P, T]), sb("rstd2_c", [P, T])
        xs, xsT, qT = sb("xs_c", [P, 2, D]), sb("xsT_c", [P, 2, KD, P]), sb("qT_c", [P, 2, P])
        s, work = sb("s_c", [P, 2, H1, SK]), sb("work_c", [P, 2, H1, SK])
        best = sb("best8", [P, 2, H1, 8])
        later = sb("later8", [P, H1, 8])
        e = sb("e_c", [P, 2, H1, SK])
        den = sb("den_c", [P, H1])
        am, aT = sb("attn_mean", [P, P]), sb("attn_meanT", [SK + 1, 2, P])
        xl = sb("xl_c", [P, 2, D])
        s_ps = [bank(f"s1_{i}") for i in range(2)]
        m0, m1 = bank("c_m0"), bank("c_m1")
        f_ps = [ctx.enter_context(nc.psum_tensor(f"film_ps{i}", [P, 2, 512], F32)) for i in range(2)]

        ld = sem("ld_c")
        dve, pool, mm_ok = sem("dve_c"), sem("pool_c"), sem("setup_c")
        var_ok, std_ok, var2_ok, std2_ok = sem("var_c"), sem("std_c"), sem("var2_c"), sem("std2_c")
        kbd_ok, vT_ok, vw_ok = sem("kbd_c"), sem("vT_c"), sem("vw_c")
        xs_ok, rows_ok, xT_ok, xTs_ok, q_ok, qT_ok, s_ok, ssb_ok = (sem(n + "_c1") for n in ("xs", "rows", "xT", "xTs", "q", "qT", "s", "ssb"))
        top_ok, best_ok, sub_ok, e_ok, em_ok, den_ok, rden_ok, er_ok, am_ok = (sem(n + "_c1") for n in ("top", "best", "sub", "e", "em", "den", "rden", "er", "am"))
        aT_ok, aTs_ok, f_ok, fo_ok, xl_ok, xlb_ok, xg_ok, xm_ok = (sem(n + "_c1") for n in ("aT", "aTs", "film", "film_out", "xl", "xlb", "xg", "xm"))

        gate_ok = sem("top_steps")
        blk = ctx.enter_context(nc.Block())

        @blk.sync
        def _(sp):
            for dst, src in ((ctxT[:, :, :], io["ctxT"].rearrange("(k c) n -> c k n", k=2)),
                             (wk[:, :, :], io["wk1"].rearrange("(k c) n -> c k n", k=2)),
                             (wv[:, :, :], io["wv1"].rearrange("(k c) n -> c k n", k=2)),
                             (wf[:, :, 0:2 * D], io["w_film_in"].rearrange("(k c) n -> c k n", k=KD)),
                             (wf[:, :, 2 * D:NF], io["w_film_out"].rearrange("(k c) n -> c k n", k=KD)),
                             (wq[:, :, :], io["wq1"].rearrange("(k c) n -> c k n", k=KD)),
                             (vw[SK:SK + 1, 0, 0:2 * D], io["b_film_in"].unsqueeze(0)),
                             (vw[SK:SK + 1, 0, 2 * D:NF], io["b_film_out"].unsqueeze(0)),
                             (mask4[:, :], io["headmask32"]),
                             (modg[:, :], io["mod_gate"].partition_broadcast(P)),
                             (g_in[:, :], io["g_norm_in"].partition_broadcast(P)),
                             (b_in[:, :], io["b_norm_in"].partition_broadcast(P)),
                             (key_u8[:, :], io["key_mask"].partition_broadcast(P)),
                             (tok_u8[:, :], io["token_mask"])):
                sp.dma_start(dst, src).then_inc(ld, 16)
            for x in range(E):
                sp.dma_start(keep.w1[:, x, :, :], io["w1_1"][x].rearrange("(k c) n -> c k n", k=KD)).then_inc(keep.ld_w1, 16)
                sp.dma_start(keep.w2[:, x, :, :], io["w2_1"][x].rearrange("(k c) n -> c k n", k=F1 // P)).then_inc(keep.ld_w2, 16)

        LOADS = 16 * 14

        @blk.gpsimd
        def _(gp):
            gp.wait_ge(ld, LOADS)

            def slot(t, at):
                u = at % 2
                if at < T:
                    gp.wait_ge(best_ok, t + 1)
                    wait(gp, er_ok, t - 1, at - 1)
                    gp.tensor_tensor(e[:, u, :, :], s[:, u, :, :], best[:, u, :, 0:1].to_broadcast([P, H1, SK]), ALU.subtract).then_inc(sub_ok, 1)
                    gp.wait_ge(xl_ok, t + 1)
                    gp.tensor_tensor(xl[:, u, :], xl[:, u, :], b_in[:, :], ALU.add).then_inc(xlb_ok, 1)
                    gp.wait_ge(rden_ok, t + 1)
                    gp.tensor_tensor(e[:, u, :, :], e[:, u, :, :], den[:, :].unsqueeze(2).to_broadcast([P, H1, SK]), ALU.mult).then_inc(er_ok, 1)
            pipeline(gp, slot, 0, 2, T, T - 1)

        @blk.scalar
        def _(act):
            act.wait_ge(var_ok, 1)
            nc.scalar.activation(rstd[:, :], tmp[:, 0, :], ACT.Sqrt).then_inc(std_ok, 1)
            act.wait_ge(var2_ok, 1)
            nc.scalar.activation(rstd2[:, :], tmp[:, 1, :], ACT.Sqrt).then_inc(std2_ok, 1)

            def slot(t, at):
                if 0 <= at + 1 < T:
                    u = (at + 1) % 2
                    act.wait_ge(xT_ok, t + 2)
                    nc.scalar.activation(xsT[:, u, :, :], m0[:, 0:D].rearrange("p (k n) -> p k n", k=KD), ACT.Copy).then_inc(xTs_ok, 1)
                    act.wait_ge(q_ok, t + 2)
                    wait(act, s_ok, t, at)
                    nc.scalar.activation(qT[:, u, :], m0[:, 0:P], ACT.Copy).then_inc(qT_ok, 1)
                if 0 <= at < T:
                    act.wait_ge(sub_ok, t + 1)
                    nc.scalar.activation(e[:, at % 2, :, :], e[:, at % 2, :, :], ACT.Exp).then_inc(e_ok, 1)
                if 0 <= at - 1 < T:
                    u = (at - 1) % 2
                    act.wait_ge(aT_ok, t)
                    nc.scalar.activation(aT[0:SK, u, :], m1[0:SK, 0:P], ACT.Copy).then_inc(aTs_ok, 1)
                    act.wait_ge(f_ok, t)
                    nc.scalar.activation(row(c.film, t - 1), f_ps[u][:, 1, :], ACT.Copy).then_inc(fo_ok, 1)
            pipeline(act, slot, -1, 3, T - 1, T)

        @blk.tensor
        def _(pe):
            pe.wait_ge(ld, LOADS)
            for k in range(2):
                mm = nc.tensor.matmul(s_ps[0][:, 0:B * SK], wk[:, k, :], ctxT[:, k, :], start=(k == 0), stop=(k == 1))
            mm.then_inc(mm_ok, 1)
            for m in range(KD):
                for k in range(2):
                    mm = nc.tensor.matmul((m0, m1)[m][:, 0:B * SK], wv[:, k, m * P:(m + 1) * P], ctxT[:, k, :], start=(k == 0), stop=(k == 1))
                mm.then_inc(mm_ok, 1)
            pe.wait_ge(vT_ok, 2)
            for b in range(B):
                wait(pe, vw_ok, 2 * (b - 1), 2 * (b - 1))
                for n in range(2):
                    for k in range(KD):
                        mm = nc.tensor.matmul(f_ps[b % 2][0:SK, n, :], vT[:, k, b * SK:(b + 1) * SK], wf[:, k, n * 512:(n + 1) * 512],
                                              start=(k == 0), stop=(k == KD - 1))
                    mm.then_inc(mm_ok, 1)
            pe.wait_ge(vw_ok, 2 * B + 3)
            pe.wait_ge(kbd_ok, B)

            def slot(t, at):
                if 0 <= at + 1 < T:
                    u = (at + 1) % 2
                    pe.wait_ge(xs_ok, t + 2)
                    wait(pe, qT_ok, t + 1, at + 1)
                    for k in range(KD):
                        mm = nc.tensor.transpose(m0[:, k * P:(k + 1) * P], xs[:, u, k * P:(k + 1) * P], keep.ident[:, :])
                    mm.then_inc(xT_ok, 1)
                    pe.wait_ge(xTs_ok, t + 2)
                    for k in range(KD):
                        mm = nc.tensor.matmul(m0[:, 0:P], wq[:, k, :], xsT[:, u, k, :], start=(k == 0), stop=(k == KD - 1))
                    mm.then_inc(q_ok, 1)
                    pe.wait_ge(qT_ok, t + 2)
                    wait(pe, ssb_ok, t, at)
                    nc.tensor.matmul(s_ps[u][:, 0:H1 * SK], qT[:, u, :], kbd[:, bass.ds((t + 1) // TB, 1), :, :].rearrange("p a h s -> p (a h s)"),
                                     start=True, stop=True).then_inc(s_ok, 1)
                if 0 <= at - 1 < T:
                    u = (at - 1) % 2
                    pe.wait_ge(am_ok, t)
                    wait(pe, aTs_ok, t - 1, at - 1)
                    nc.tensor.transpose(m1[:, 0:P], am[:, :], keep.ident[:, :]).then_inc(aT_ok, 1)
                    pe.wait_ge(aTs_ok, t)
                    wait(pe, fo_ok, t - 2, at - 2)
                    wait(pe, xm_ok, t - 2, at - 2)
                    for n in range(2):
                        mm = nc.tensor.matmul(f_ps[u][:, n, :], aT[:, u, :], vw[:, bass.ds((t - 1) // TB, 1), n * 512:(n + 1) * 512].rearrange("p a n -> p (a n)"),
                                              start=True, stop=True)
                    mm.then_inc(f_ok, 1)
            pipeline(pe, slot, -1, 3, T - 1, T)

        @blk.vector
        def _(v):
            done = [0]

            def link(ins):
                done[0] += 1
                ins.then_inc(dve, 1)
                v.wait_ge(dve, done[0])

            done[0] = norm_from_stats(v, 0, dve, keep.stats, tmp, mean, rstd)
            v.wait_ge(dve, done[0])
            v.sem_inc(var_ok, 1)
            v.wait_ge(std_ok, 1)
            link(v.reciprocal(rstd[:, :], rstd[:, :]))
            link(v.tensor_tensor(tmp[:, 1, :], rstd[:, :], rstd[:, :], ALU.mult))
            link(v.tensor_scalar(tmp[:, 1, :], tmp[:, 1, :], -EPS, 1.0 + EPS, ALU.mult, ALU.add))
            v.sem_inc(var2_ok, 1)
            v.wait_ge(ld, LOADS)
            v.wait_ge(std2_ok, 1)
            link(v.reciprocal(rstd2[:, :], rstd2[:, :]))
            link(v.tensor_copy(key_bias[:, :, :].rearrange("p b s -> p (b s)"), key_u8[:, :]))
            link(v.tensor_scalar(key_bias[:, :, :], key_bias[:, :, :], 1.0, 3.0e38, ALU.subtract, ALU.mult))
            link(v.tensor_scalar(key_bias[:, :, :], key_bias[:, :, :], 10.0, None, ALU.mult))
            link(v.tensor_copy(tok[:, :], tok_u8[:, :]))
            link(v.tensor_scalar(tok[:, :], tok[:, :], 1.0 / H1, None, ALU.mult))
            v.wait_ge(mm_ok, 1)
            link(v.tensor_copy(vT[:, 0, :], s_ps[0][:, 0:B * SK]))
            for b in range(B):
                v.tensor_tensor(kbd[:, b, :, :], vT[:, 0, b * SK:(b + 1) * SK].unsqueeze(1).to_broadcast([P, H1, SK]),
                                mask4[:, :].unsqueeze(2).to_broadcast([P, H1, SK]), ALU.mult).then_inc(kbd_ok, 1)
            v.wait_ge(kbd_ok, B)
            for m in range(KD):
                v.wait_ge(mm_ok, 2 + m)
                v.tensor_copy(vT[:, m, :], (m0, m1)[m][:, 0:B * SK]).then_inc(vT_ok, 1)
            for n in range(4):
                v.tensor_scalar(vw[SK:SK + 1, 0, n * D:(n + 1) * D], vw[SK:SK + 1, 0, n * D:(n + 1) * D], modg[SK:SK + 1, 0:1],
                                1.0 - n % 2, ALU.mult, ALU.add).then_inc(dve, 1)
            done[0] += 4
            v.wait_ge(dve, done[0])
            for b in range(1, B):
                v.tensor_copy(vw[SK:SK + 1, b, :], vw[SK:SK + 1, 0, :]).then_inc(dve, 1)
            v.memset(aT[SK:SK + 1, :, :], 1.0).then_inc(dve, 1)
            v.memset(am[:, SK:P], 0.0).then_inc(dve, 1)
            done[0] += B + 1
            for b in range(B):
                for n in range(2):
                    v.wait_ge(mm_ok, 3 + 2 * b + n + 1)
                    v.tensor_scalar(vw[0:SK, b, n * 512:(n + 1) * 512], f_ps[b % 2][0:SK, n, :], modg[0:SK, 0:1], None, ALU.mult).then_inc(vw_ok, 1)
            v.wait_ge(dve, done[0])
            v.sem_inc(vw_ok, 3)
            D0 = done[0]
            PER = 7

            def slot(t, at):
                if 0 <= at + 1 < T:
                    u = (at + 1) % 2
                    wait(v, xT_ok, t, at)
                    if at >= 1:
                        v.wait_ge(xl_ok, t)
                    v.tensor_scalar(xs[:, u, :], row(keep.x1, t + 1), mean[:, bass.ds(t + 1, 1)], rstd[:, bass.ds(t + 1, 1)], ALU.subtract, ALU.mult).then_inc(xs_ok, 1)
                    v.tensor_scalar(row(c.rows, t + 1), row(keep.x1, t + 1), mean[:, bass.ds(t + 1, 1)], rstd[:, bass.ds(t + 1, 1)], ALU.subtract, ALU.mult).then_inc(rows_ok, 1)
                if 0 <= at < T:
                    u = at % 2
                    v.wait_ge(s_ok, t + 1)
                    v.scalar_tensor_tensor(s[:, u, :, :], s_ps[u][:, 0:H1 * SK].rearrange("p (h s) -> p h s", h=H1), 1.0 / DH1 ** 0.5,
                                           key_bias[:, bass.ds(t // TB, 1), :].to_broadcast([P, H1, SK]), ALU.mult, ALU.add).then_inc(ssb_ok, 1)
                    v.wait_ge(ssb_ok, t + 1)
                    v.sem_inc(gate_ok, 1)
                    for r in range(TOP // 8):
                        src = s if r == 0 else work
                        for h in range(H1):
                            mx = best[:, u, h, :] if r == 0 else later[:, h, :]
                            ins = v.max(mx, src[:, u, h, :])
                        if r == 0:
                            ins.then_inc(best_ok, 1)
                            v.wait_ge(best_ok, t + 1)
                            v.sem_inc(gate_ok, 1)
                        else:
                            ins.then_inc(dve, 1)
                            v.wait_ge(dve, t * PER + (D0 + 2 * r))
                            v.sem_inc(gate_ok, 1)
                        for h in range(H1):
                            mx = best[:, u, h, :] if r == 0 else later[:, h, :]
                            ins = v.match_replace(work[:, u, h, :], mx, src[:, u, h, :], MOVED)
                        ins.then_inc(dve, 1)
                        v.wait_ge(dve, t * PER + (D0 + 2 * r + 1))
                        v.sem_inc(gate_ok, 1)
                    v.wait_ge(e_ok, t + 1)
                    v.scalar_tensor_tensor(e[:, u, :, :], work[:, u, :, :], MOVED, e[:, u, :, :], ALU.is_equal, ALU.mult).then_inc(em_ok, 1)
                    wait(v, xm_ok, t - 1, at - 1)
                    v.scalar_tensor_tensor(xl[:, u, :], xs[:, u, :], rstd2[:, bass.ds(t, 1)], g_in[:, :], ALU.mult, ALU.mult).then_inc(xl_ok, 1)
                    v.wait_ge(em_ok, t + 1)
                    wait(v, er_ok, t, at)
                    v.reduce_sum(den[:, :], e[:, u, :, :], AX).then_inc(den_ok, 1)
                    v.wait_ge(den_ok, t + 1)
                    v.reciprocal(later[:, 0, 0:H1], den[:, :]).then_inc(top_ok, 1)
                    v.wait_ge(top_ok, t + 1)
                    v.tensor_scalar(den[:, :], later[:, 0, 0:H1], tok[:, bass.ds(t, 1)], None, ALU.mult).then_inc(rden_ok, 1)
                if 0 <= at - 1 < T:
                    u = (at - 1) % 2
                    v.wait_ge(f_ok, t)
                    v.wait_ge(fo_ok, t)
                    v.wait_ge(xlb_ok, t)
                    v.tensor_tensor(xl[:, u, :], xl[:, u, :], f_ps[u][:, 0, 0:D], ALU.mult).then_inc(xg_ok, 1)
                    v.wait_ge(xg_ok, t)
                    v.tensor_tensor(row(c.xm, t - 1), xl[:, u, :], f_ps[u][:, 0, D:2 * D], ALU.add).then_inc(xm_ok, 1)
                if 0 <= at < T:
                    u = at % 2
                    v.wait_ge(er_ok, t + 1)
                    wait(v, aT_ok, t, at)
                    v.reduce_sum(am[:, 0:SK], e[:, u, :, :].rearrange("p h s -> p s h"), AX).then_inc(am_ok, 1)
            pipeline(v, slot, -1, 3, T - 1, T)
            v.wait_ge(xm_ok, T)


def ssm_kernel(nc, io, keep, c):
    N = 64
    DL = P
    CH = 32
    NB, NA = 32, 16
    L = S
    W = L // 2
    with ExitStack() as ctx:
        def sb(name, shape, dt=F32):
            return ctx.enter_context(nc.sbuf_tensor(name, shape, dt))

        sem = keep.sems.new

        ar, ai, cr, ci = (sb(n, [P, DL]) for n in ("a_re", "a_im", "c_re", "c_im"))
        dt = sb("dt_rows", [P, DL])
        t = [sb(f"k_tmp{i}", [P, DL]) for i in range(6)]
        ki = sb("k_int", [P, DL], I32)
        ur, ui, pr, pi = (sb(n, [P, DL]) for n in ("u_re", "u_im", "p_re", "p_im"))
        zr, zi = sb("z_re", [P, 9, DL]), sb("z_im", [P, 9, DL])
        gr, gi = sb("dc_re", [P, DL]), sb("dc_im", [P, DL])
        tabr, tabi = sb("tab_re", [P, CH, NB]), sb("tab_im", [P, CH, NB])
        gar, gai = sb("ga_re", [P, CH, NA]), sb("ga_im", [P, CH, NA])
        gneg = sb("ga_im_neg", [P, CH, NA])
        w = [sb(f"tab_tmp{i}", [P, CH, NB // 2]) for i in range(4)]
        kout = sb("k_out", [NA, 2, CH, NB])
        k_ps = ctx.enter_context(nc.psum_tensor("k_ps", [P, 2, CH, NB], F32))
        ld, dve, mm_ok, out_ok, stored = sem("ld_k"), sem("dve_k"), sem("mm_k"), sem("out_k"), sem("stored_k")
        tab_ok, turn_ok = sem("tab_k"), sem("turn_k")
        kd = c.kernel_dram
        blk = ctx.enter_context(nc.Block())

        @blk.sync
        def _(sp):
            for h in range(2):
                q = slice(N * h, N * h + N)
                for buf, name in ((ar, "a_reT"), (ai, "a_imT"), (cr, "c_reT"), (ci, "c_imT")):
                    sp.dma_start(buf[q, :], io[name][:, h * DL:(h + 1) * DL]).then_inc(ld, 16)
                sp.dma_start(dt[q, :], io["log_dt"][h * DL:(h + 1) * DL].partition_broadcast(N)).then_inc(ld, 16)
            with sp.Fori(0, DL // CH) as i:
                sp.wait_ge(out_ok, i + 1)
                for h in range(2):
                    sp.dma_start(kd[bass.ds(i * CH + h * DL, CH), :].rearrange("d (a b) -> a d b", a=NA), kout[:, h, :, :]).then_inc(stored, 16)
            sp.wait_ge(stored, 16 * 2 * (DL // CH) + 1)

        @blk.tensor
        def _(pe):
            with pe.Fori(0, DL // CH) as i:
                pe.wait_ge(tab_ok, i + 1)
                pe.sem_inc(turn_ok, 1)
                for d in range(CH):
                    for h in range(2):
                        q = slice(N * h, N * h + N)
                        nc.tensor.matmul(k_ps[0:NA, h, d, :], gar[q, d, :], tabr[q, d, :], start=True, stop=False)
                        mm = nc.tensor.matmul(k_ps[0:NA, h, d, :], gneg[q, d, :], tabi[q, d, :], start=False, stop=True)
                mm.then_inc(mm_ok, 1)

        @blk.vector
        def _(v):
            n = 0

            def link(*ins):
                nonlocal n
                for x in ins:
                    x.then_inc(dve, 1)
                n += len(ins)
                v.wait_ge(dve, n)

            def tt(o, a, b, op):
                return v.tensor_tensor(o, a, b, op)

            v.wait_ge(ld, 160)
            A = slice(None)
            x = dt[:, :]
            k, r, q, f = t[0][:, :], t[1][:, :], t[2][:, :], t[3][:, :]
            MAGIC = 12582912.0
            link(v.tensor_scalar(k, x, 1.4426950408889634, MAGIC, ALU.mult, ALU.add))
            link(v.tensor_scalar(k, k, MAGIC, None, ALU.subtract))
            link(v.scalar_tensor_tensor(r, k, -0.693359375, x, ALU.mult, ALU.add))
            link(v.scalar_tensor_tensor(r, k, 2.12194440e-4, r, ALU.mult, ALU.add))
            link(v.tensor_scalar(q, r, 1.0 / 5040, None, ALU.mult))
            for co in (1 / 720, 1 / 120, 1 / 24, 1 / 6, 0.5, 1.0):
                link(v.scalar_tensor_tensor(q, q, co, r, ALU.add, ALU.mult))
            link(v.tensor_scalar(f, k, 127.0, 8388608.0, ALU.add, ALU.mult))
            link(v.tensor_copy(ki[:, :], f))
            link(v.scalar_tensor_tensor(x, q, 1.0, ki[:, :].bitcast(F32), ALU.add, ALU.mult))
            link(tt(t[4][:, :], x, ar[:, :], ALU.mult), tt(t[5][:, :], x, ai[:, :], ALU.mult))
            wr, wi = t[4][:, :], t[5][:, :]
            link(v.tensor_scalar(k, wi, 0.15915494309189535, MAGIC, ALU.mult, ALU.add))
            link(v.tensor_scalar(k, k, MAGIC, None, ALU.subtract))
            for part in (6.28125, 1.93500518798828125e-3, 3.01991598196e-7):
                link(v.scalar_tensor_tensor(wi, k, -part, wi, ALU.mult, ALU.add))
            u_r, u_i, p_r, p_i = ur[:, :], ui[:, :], pr[:, :], pi[:, :]
            a, b, cc, dd = (t[i][:, :] for i in range(4))
            link(v.tensor_scalar(u_r, wr, 1 / 256, None, ALU.mult), v.tensor_scalar(u_i, wi, 1 / 256, None, ALU.mult))
            link(v.tensor_scalar(p_r, u_r, 0.2, None, ALU.mult), v.tensor_scalar(p_i, u_i, 0.2, None, ALU.mult))
            for co in (1 / 4, 1 / 3, 1 / 2, 1.0):
                link(v.scalar_tensor_tensor(a, p_r, 1.0, u_r, ALU.add, ALU.mult), tt(b, p_i, u_i, ALU.mult),
                     v.scalar_tensor_tensor(cc, p_r, 1.0, u_i, ALU.add, ALU.mult), tt(dd, p_i, u_r, ALU.mult))
                link(tt(p_r, a, b, ALU.subtract), tt(p_i, cc, dd, ALU.add))
                if co != 1.0:
                    link(v.tensor_scalar(p_r, p_r, co, None, ALU.mult), v.tensor_scalar(p_i, p_i, co, None, ALU.mult))

            def double():
                link(v.scalar_tensor_tensor(a, p_r, 2.0, p_r, ALU.add, ALU.mult), tt(b, p_i, p_i, ALU.mult),
                     v.scalar_tensor_tensor(cc, p_r, 1.0, p_i, ALU.add, ALU.mult))
                link(tt(p_r, a, b, ALU.subtract), v.tensor_scalar(p_i, cc, 2.0, None, ALU.mult))

            for _ in range(8):
                double()
            link(tt(a, cr[:, :], p_r, ALU.mult), tt(b, ci[:, :], p_i, ALU.mult), tt(cc, cr[:, :], p_i, ALU.mult), tt(dd, ci[:, :], p_r, ALU.mult))
            link(tt(u_r, a, b, ALU.subtract), tt(u_i, cc, dd, ALU.add))
            link(tt(a, ar[:, :], ar[:, :], ALU.mult), tt(b, ai[:, :], ai[:, :], ALU.mult))
            link(tt(a, a, b, ALU.add))
            link(v.reciprocal(t[4][:, :], a))
            link(tt(a, u_r, ar[:, :], ALU.mult), tt(b, u_i, ai[:, :], ALU.mult), tt(cc, u_i, ar[:, :], ALU.mult), tt(dd, u_r, ai[:, :], ALU.mult))
            link(tt(u_r, a, b, ALU.add), tt(u_i, cc, dd, ALU.subtract))
            link(v.scalar_tensor_tensor(gr[:, :], u_r, 2.0, t[4][:, :], ALU.mult, ALU.mult), v.scalar_tensor_tensor(gi[:, :], u_i, 2.0, t[4][:, :], ALU.mult, ALU.mult))
            for j in range(9):
                link(v.tensor_scalar(zr[:, j, :], p_r, 1.0, None, ALU.add), v.tensor_copy(zi[:, j, :], p_i))
                if j < 8:
                    double()
            v.memset(tabr[:, :, 0:1], 1.0).then_inc(dve, 1)
            v.memset(tabi[:, :, 0:1], 0.0).then_inc(dve, 1)
            n += 2
            v.wait_ge(dve, n)
            v.sem_inc(stored, 1)
            N0 = n
            PER = 6 * 9 + 2 + 1 + 2
            with v.Fori(0, DL // CH) as i:
                m = 0

                def step(*ins):
                    nonlocal m
                    for y in ins:
                        y.then_inc(dve, 1)
                    m += len(ins)
                    v.wait_ge(dve, i * PER + (N0 + m))

                sl = bass.ds(i * CH, CH)
                step(v.tensor_copy(gar[:, :, 0], gr[:, sl]), v.tensor_copy(gai[:, :, 0], gi[:, sl]))

                def grow(tr, ti, width, j0):
                    x, j = 1, j0
                    while x < width:
                        br = zr[:, j, sl].unsqueeze(2).to_broadcast([P, CH, x])
                        bi = zi[:, j, sl].unsqueeze(2).to_broadcast([P, CH, x])
                        s0, s1 = tr[:, :, 0:x], ti[:, :, 0:x]
                        q = [y[:, :, 0:x] for y in w]
                        step(tt(q[0], s0, br, ALU.mult), tt(q[1], s1, bi, ALU.mult), tt(q[2], s0, bi, ALU.mult), tt(q[3], s1, br, ALU.mult))
                        step(tt(tr[:, :, x:2 * x], q[0], q[1], ALU.subtract), tt(ti[:, :, x:2 * x], q[2], q[3], ALU.add))
                        x, j = 2 * x, j + 1

                grow(tabr, tabi, NB, 0)
                grow(gar, gai, NA, 5)
                step(v.tensor_scalar(gneg[:, :, :], gai[:, :, :], -1.0, None, ALU.mult))
                v.sem_inc(tab_ok, 1)
                v.wait_ge(mm_ok, i + 1)
                v.wait_ge(stored, i * 32 + 1)
                step(v.tensor_copy(kout[:, 0, :, :], k_ps[0:NA, 0, :, :]), v.tensor_copy(kout[:, 1, :, :], k_ps[0:NA, 1, :, :]))
                assert m == PER
                v.sem_inc(out_ok, 1)


W = S // 2
X_TILES = (0, 1, 2, 3)
K_TILES = (0, 1, 4, 3, 5, 1)


def kernel_transform(nc, io, keep, c):
    with ExitStack() as ctx:
        k_rows = ctx.enter_context(nc.sbuf_tensor("k_rows", [P, 2, S], F32))
        kT = ctx.enter_context(nc.sbuf_tensor("k_T", [P, 4, D], F32))
        t_ps = ctx.enter_context(nc.psum_tensor("kt_ps", [P, 2, 512], F32))
        f_ps = ctx.enter_context(nc.psum_tensor("kf_ps", [P, 6, 512], F32))
        sem = keep.sems.new
        ld, tr, ev, mm = (sem(n) for n in ("ld_kt", "kT_in_psum", "kT_ready", "kf_in_psum"))
        blk = ctx.enter_context(nc.Block())

        @blk.sync
        def _(sp):
            sp.dma_start(k_rows[:, :, :], c.kernel_dram.rearrange("(h p) l -> p h l", p=P)).then_inc(ld, 16)
            sp.dma_start(c.fwd[:, :, :], io["dft"].rearrange("(k p) f -> p k f", k=2)).then_inc(ld, 16)
            sp.dma_start(c.inv[:, :, :], io["idft"].rearrange("(k p) t -> p k t", p=P)).then_inc(ld, 16)
            sp.dma_start(c.sign[:, :], io["sign"]).then_inc(ld, 16)
            sp.dma_start(c.dskip[:, :], io["d_skip"].partition_broadcast(P)).then_inc(ld, 16)

        @blk.tensor
        def _(pe):
            pe.wait_ge(ld, 80)
            for lc in range(4):
                for h in range(2):
                    x = nc.tensor.transpose(t_ps[:, lc // 2, (lc % 2) * D + h * P:(lc % 2) * D + h * P + P], k_rows[:, h, lc * P:(lc + 1) * P], keep.ident[:, :])
                if lc % 2:
                    x.then_inc(tr, 1)
            pe.wait_ge(ev, 2)
            kv = kT[:, :, :].rearrange("p (w k) d -> p w k d", k=2)
            for j, f in enumerate(K_TILES):
                for k in range(2):
                    x = nc.tensor.matmul(f_ps[:, j, :], c.fwd[:, k, f * P:(f + 1) * P], kv[:, :, k, :], start=(k == 0), stop=(k == 1))
                x.then_inc(mm, 1)

        @blk.vector
        def _(v):
            for i in range(2):
                v.wait_ge(tr, i + 1)
                v.tensor_copy(kT[:, 2 * i:2 * i + 2, :], t_ps[:, i, :].rearrange("p (a d) -> p a d", a=2)).then_inc(ev, 1)
            for j in range(6):
                v.wait_ge(mm, j + 1)
                v.tensor_copy(c.kf[:, j, :, :], f_ps[:, j, :].rearrange("p (w d) -> p w d", w=2)).then_inc(ev, 1)
            v.wait_ge(ev, 8)


def convolution(nc, io, keep, c):
    with ExitStack() as ctx:
        def sb(name, shape, dt=F32):
            return ctx.enter_context(nc.sbuf_tensor(name, shape, dt))

        sem = keep.sems.new

        xz = sb("x_hat", [P, 4, 2, D])
        yh = sb("y_hat", [P, 4, 2, D])
        t = [sb(f"prod{i}", [P, 2, 2, D]) for i in range(4)]
        xf_ps = ctx.enter_context(nc.psum_tensor("xf_ps", [P, 4, 512], F32))
        y_ps = [ctx.enter_context(nc.psum_tensor(f"yt_ps{i}", [P, 512], F32)) for i in range(2)]
        fwd_ok, x0_ok, xz_ok, prod, ppool, yh_ok = (sem(n) for n in ("fwd_done", "x0_ready", "xz_ready", "dve_products", "pool_products", "yhat_ready"))
        inv_ok, y_ok, skip_ok, base_ok, st_ok = (sem(n) for n in ("inv_done", "y_added", "skip_ready", "base_ready", "stats_conv"))
        blk = ctx.enter_context(nc.Block())

        def win(buf, b, k):
            return buf[:, :, :].rearrange("p (b q k) d -> p b q k d", b=B, q=2)[:, b, :, k, :]

        UA = c.kf[:, 0:2, 0, :].unsqueeze(2).to_broadcast([P, 2, 2, D])
        UB = c.kf[:, 2:4, 0, :].unsqueeze(2).to_broadcast([P, 2, 2, D])
        UD = c.kf[:, 4:6, 0, :].unsqueeze(2).to_broadcast([P, 2, 2, D])
        VA, VB, VD = (c.kf[:, j:j + 2, 1, :] for j in (0, 2, 4))

        @blk.tensor
        def _(pe):
            for b in range(B + 1):
                if b < B:
                    for j, f in enumerate(X_TILES):
                        wait(pe, xz_ok, b, b)
                        for k in range(2):
                            x = nc.tensor.matmul(xf_ps[:, j, :], c.fwd[:, k, f * P:(f + 1) * P], win(c.xm, b, k), start=(k == 0), stop=(k == 1))
                    x.then_inc(fwd_ok, 1)
                if b >= 1:
                    pe.wait_ge(yh_ok, b)
                    for k in range(2):
                        wait(pe, y_ok, 2 * (b - 2) + k + 1, 2 * (b - 2) + k + 1)
                        for j in range(4):
                            x = nc.tensor.matmul(y_ps[k][:, :], c.inv[:, j, k * P:(k + 1) * P], yh[:, j, :, :].rearrange("p q d -> p (q d)"),
                                                 start=(j == 0), stop=(j == 3))
                        x.then_inc(inv_ok, 1)

        @blk.scalar
        def _(act):
            for b in range(B):
                act.wait_ge(fwd_ok, b + 1)
                wait(act, yh_ok, b, b)
                nc.scalar.activation(xz[:, :, 0, :], xf_ps[:, :, 0:D], ACT.Copy).then_inc(x0_ok, 1)

        @blk.gpsimd
        def _(gp):
            n = 0
            for b in range(B):
                xr, xi = xz[:, 0:2, :, :], xz[:, 2:4, :, :]
                gp.wait_ge(xz_ok, b + 1)
                wait(gp, yh_ok, b, b)
                gp.tensor_tensor(t[2][:, :, :, :], xr, UB, ALU.mult).then_inc(ppool, 1)
                gp.tensor_tensor(t[3][:, :, :, :], xi, UD, ALU.mult).then_inc(ppool, 1)
                gp.wait_ge(fwd_ok, b + 1)
                for k in range(2):
                    xm, rows = win(c.xm, b, k), win(c.rows, b, k)
                    gp.tensor_tensor(xm, xm, c.dskip[:, :].unsqueeze(1).to_broadcast([P, 2, D]), ALU.mult).then_inc(skip_ok, 1)
                    gp.tensor_tensor(rows, rows, win(c.film, b, k)[:, :, D:2 * D], ALU.add).then_inc(base_ok, 1)

        @blk.vector
        def _(v):
            n = 0

            def link(*ins):
                nonlocal n
                for x in ins:
                    x.then_inc(prod, 1)
                n += len(ins)
                v.wait_ge(prod, n)

            def tt(o, a, b, op):
                return v.tensor_tensor(o, a, b, op)

            def products(b):
                v.wait_ge(x0_ok, b + 1)
                v.scalar_tensor_tensor(xz[:, :, 1, :], xz[:, :, 0, :], c.sign[:, 0:1], xf_ps[:, :, D:2 * D], ALU.mult, ALU.add).then_inc(xz_ok, 1)
                v.wait_ge(xz_ok, b + 1)
                xr, xi = xz[:, 0:2, :, :], xz[:, 2:4, :, :]
                r0, i0 = xr[:, :, 0, :], xi[:, :, 0, :]
                yr, yi = yh[:, 0:2, :, :], yh[:, 2:4, :, :]
                link(tt(t[0][:, :, :, :], xr, UA, ALU.mult), tt(t[1][:, :, :, :], xi, UB, ALU.mult))
                wait(v, inv_ok, 2 * b, 2 * b)
                link(tt(yr, t[0][:, :, :, :], t[1][:, :, :, :], ALU.subtract))
                v.wait_ge(ppool, 2 * b + 2)
                link(tt(yi, t[2][:, :, :, :], t[3][:, :, :, :], ALU.add), tt(t[0][:, :, 0, :], r0, VA, ALU.mult), tt(t[0][:, :, 1, :], i0, VB, ALU.mult),
                     tt(t[1][:, :, 0, :], r0, VB, ALU.mult), tt(t[1][:, :, 1, :], i0, VD, ALU.mult))
                link(tt(yr[:, :, 1, :], yr[:, :, 1, :], t[0][:, :, 0, :], ALU.add), tt(yi[:, :, 1, :], yi[:, :, 1, :], t[1][:, :, 0, :], ALU.add))
                link(tt(yr[:, :, 1, :], yr[:, :, 1, :], t[0][:, :, 1, :], ALU.subtract), tt(yi[:, :, 1, :], yi[:, :, 1, :], t[1][:, :, 1, :], ALU.add))
                v.sem_inc(yh_ok, 1)

            def outer(b):
                for k in range(2):
                    xm, rows = win(c.xm, b, k), win(c.rows, b, k)
                    v.wait_ge(inv_ok, 2 * b + k + 1)
                    v.wait_ge(skip_ok, 2 * b + k + 1)
                    v.tensor_tensor(xm, xm, y_ps[k][:, :].rearrange("p (q d) -> p q d", q=2), ALU.add).then_inc(y_ok, 1)
                    v.wait_ge(y_ok, 2 * b + k + 1)
                    link(tt(xm, xm, win(c.film, b, k)[:, :, 0:D], ALU.mult))
                    v.wait_ge(base_ok, 2 * b + k + 1)
                    link(tt(rows, rows, xm, ALU.add))
                for i in range(TB * b, TB * b + TB):
                    v.bn_stats(keep.stats[:, i, :], c.rows[:, i, :]).then_inc(st_ok, 1)

            for b in range(B):
                products(b)
                if b >= 1:
                    outer(b - 1)
            outer(B - 1)
            v.wait_ge(st_ok, T)


def dense_ffn(nc, io, keep, c):
    FH = 4 * D
    MH = FH // P
    with ExitStack() as ctx:
        def sb(name, shape, dt=F32):
            return ctx.enter_context(nc.sbuf_tensor(name, shape, dt))

        sem = keep.sems.new

        w1, w1g = sb("ffn_w1", [P, KD, FH]), sb("ffn_w1_gain", [P, KD, FH])
        w2 = sb("ffn_w2", [P, MH, D])
        gT, bT, b1T, b1s = sb("g_ffnT", [P, KD]), sb("b_ffnT", [P, KD]), sb("ffn_b1T", [P, MH]), sb("ffn_b1_sum", [P, MH])
        b2 = sb("ffn_b2", [P, D])
        g_out, b_out = sb("g_norm_out", [P, D]), sb("b_norm_out", [P, D])
        tmp, mean, rstd = sb("tmp_f", [P, 4, T]), sb("mean_f", [P, T]), sb("rstd_f", [P, T])
        xs, xT = sb("xs_f", [P, TB, D]), sb("xT_f", [P, 2, KD, S])
        hid = sb("hid_f", [P, MH, S])
        t_ps = ctx.enter_context(nc.psum_tensor("ft_ps", [P, KD, 512], F32))
        h_ps = [ctx.enter_context(nc.psum_tensor(f"fh_ps{i}", [P, 512], F32)) for i in range(3)]
        o_ps = [ctx.enter_context(nc.psum_tensor(f"fo_ps{i}", [P, 512], F32)) for i in range(2)]
        ld, dve, var_ok, std_ok, w1_ok, bias_ok = (sem(n) for n in ("ld_f", "dve_f", "var_f", "std_f", "w1_gain_ready", "bias_in_psum"))
        xs_ok, xT_ok, xTs_ok, h_ok, act_ok, o_ok, x5_ok, rb_ok, st_ok = (sem(n + "_f") for n in ("xs", "xT", "xTs", "h", "act", "o", "x5", "rb", "stats"))
        fin, finp, dve_bias = sem("final_dve"), sem("final_pool"), sem("bias_ready")
        blk = ctx.enter_context(nc.Block())

        @blk.sync
        def _(sp):
            for dst, src in ((w1[:, :, :], io["ffn_w1"].rearrange("(k c) n -> c k n", k=KD)), (gT[:, :], io["g_ffnT"]), (bT[:, :], io["b_ffnT"]),
                             (b1T[:, :], io["ffn_b1T"]), (b2[:, :], io["ffn_b2"].partition_broadcast(P)),
                             (w2[:, :, :], io["ffn_w2"].rearrange("(k c) n -> c k n", k=MH)),
                             (g_out[:, :], io["g_norm_out"].partition_broadcast(P)), (b_out[:, :], io["b_norm_out"].partition_broadcast(P))):
                sp.dma_start(dst, src).then_inc(ld, 16)

        LOADS = 16 * 8

        @blk.gpsimd
        def _(gp):
            gp.wait_ge(ld, LOADS)
            gate = keep.gate[:, 1:2]
            gp.tensor_scalar(g_out[:, :], g_out[:, :], gate, None, ALU.mult).then_inc(finp, 1)
            gp.tensor_scalar(b_out[:, :], b_out[:, :], gate, None, ALU.mult).then_inc(finp, 1)
            gp.wait_ge(finp, 2)
            for b in range(B):
                sl = slice(TB * b, TB * b + TB)
                wide = [P, TB, D]
                gp.wait_ge(xs_ok, TB * (b + 1))
                gp.tensor_tensor(c.rows[:, sl, :], c.rows[:, sl, :], b2[:, :].unsqueeze(1).to_broadcast(wide), ALU.add).then_inc(rb_ok, 1)
                gp.tensor_tensor(keep.x1[:, sl, :], keep.x1[:, sl, :], b_out[:, :].unsqueeze(1).to_broadcast(wide), ALU.add).then_inc(finp, 1)
            with gp.Fori(0, T) as t:
                gp.wait_ge(fin, t + 1)
                r = row(c.rows, t)
                gp.tensor_tensor(r, r, g_out[:, :], ALU.mult).then_inc(finp, 1)

        @blk.scalar
        def _(act):
            act.wait_ge(var_ok, 1)
            nc.scalar.activation(rstd[:, :], tmp[:, 0, :], ACT.Sqrt).then_inc(std_ok, 1)
            for b in range(B):
                for m in range(MH):
                    n = MH * b + m
                    act.wait_ge(h_ok, n + 1)
                    if m == 0:
                        act.wait_ge(dve_bias, 1)
                        wait(act, o_ok, TB * b, TB * b)
                    nc.scalar.activation(hid[:, m, :], h_ps[n % 3][:, :], ACT.Gelu, bias=b1s[:, m:m + 1]).then_inc(act_ok, 1)
            act.wait_ge(var_ok, 2)
            nc.scalar.activation(rstd[:, :], tmp[:, 0, :], ACT.Sqrt).then_inc(std_ok, 1)

        @blk.tensor
        def _(pe):
            pe.wait_ge(ld, LOADS)
            for m in range(MH):
                for k in range(KD):
                    x = nc.tensor.matmul(o_ps[0][:, m:m + 1], w1[:, k, m * P:(m + 1) * P], bT[:, k:k + 1], start=(k == 0), stop=(k == KD - 1))
            x.then_inc(bias_ok, 1)

            def turn(b):
                for i in range(TB):
                    pe.wait_ge(xs_ok, TB * b + i + 1)
                    if i == 0:
                        wait(pe, xTs_ok, 2 * b, 2 * b)
                    for k in range(KD):
                        x = nc.tensor.transpose(t_ps[:, k, i * P:(i + 1) * P], xs[:, i, k * P:(k + 1) * P], keep.ident[:, :])
                    x.then_inc(xT_ok, 1)

            turn(0)
            pe.wait_ge(w1_ok, 2)
            for b in range(B):
                pe.wait_ge(xTs_ok, 2 * b + 2)
                for m in range(MH):
                    n = MH * b + m
                    wait(pe, act_ok, n - 2, n - 2)
                    for k in range(KD):
                        x = nc.tensor.matmul(h_ps[n % 3][:, :], w1g[:, k, m * P:(m + 1) * P], xT[:, b % 2, k, :], start=(k == 0), stop=(k == KD - 1))
                    x.then_inc(h_ok, 1)
                if b + 1 < B:
                    turn(b + 1)
                pe.wait_ge(act_ok, MH * (b + 1))
                for i in range(TB):
                    n = TB * b + i
                    if n == 0:
                        pe.wait_ge(dve_bias, 1)
                    wait(pe, x5_ok, n - 1, n - 1)
                    for k in range(MH):
                        x = nc.tensor.matmul(o_ps[n % 2][:, 0:D], hid[:, k, i * P:(i + 1) * P], w2[:, k, :], start=(k == 0), stop=(k == MH - 1))
                    x.then_inc(o_ok, 1)

        @blk.vector
        def _(v):
            n = norm_from_stats(v, 0, dve, keep.stats, tmp, mean, rstd)
            v.wait_ge(dve, n)
            v.sem_inc(var_ok, 1)
            v.wait_ge(ld, LOADS)
            for k in range(KD):
                v.tensor_scalar(w1g[:, k, :], w1[:, k, :], gT[:, k:k + 1], None, ALU.mult).then_inc(w1_ok, 1)
            v.wait_ge(std_ok, 1)
            v.reciprocal(rstd[:, :], rstd[:, :]).then_inc(dve, 1)
            n += 1
            v.wait_ge(dve, n)

            def ln(b):
                for i in range(TB):
                    t = TB * b + i
                    wait(v, xT_ok, TB * (b - 1) + i + 1, TB * (b - 1) + i + 1)
                    v.tensor_scalar(xs[:, i, :], c.rows[:, t, :], mean[:, t:t + 1], rstd[:, t:t + 1], ALU.subtract, ALU.mult).then_inc(xs_ok, 1)
                v.wait_ge(xT_ok, TB * (b + 1))
                wait(v, h_ok, MH * (b - 1), MH * (b - 1))
                for k in range(KD):
                    v.tensor_copy(xT[:, b % 2, k, :], t_ps[:, k, :]).then_inc(xTs_ok, 1)

            ln(0)
            v.wait_ge(bias_ok, 1)
            v.tensor_tensor(b1s[:, :], o_ps[0][:, 0:MH], b1T[:, :], ALU.add).then_inc(dve_bias, 1)
            for b in range(B):
                if b + 1 < B:
                    ln(b + 1)
                v.wait_ge(rb_ok, b + 1)
                for i in range(TB):
                    t = TB * b + i
                    v.wait_ge(o_ok, t + 1)
                    v.tensor_tensor(c.rows[:, t, :], c.rows[:, t, :], o_ps[t % 2][:, 0:D], ALU.add).then_inc(x5_ok, 1)
                    v.wait_ge(x5_ok, t + 1)
                    v.bn_stats(keep.stats[:, t, :], c.rows[:, t, :]).then_inc(st_ok, 1)
            v.wait_ge(st_ok, T)
            n = norm_from_stats(v, n, dve, keep.stats, tmp, mean, rstd)
            v.wait_ge(dve, n)
            v.sem_inc(var_ok, 1)
            v.wait_ge(std_ok, 2)
            v.reciprocal(rstd[:, :], rstd[:, :]).then_inc(dve, 1)
            v.wait_ge(dve, n + 1)
            with v.Fori(0, T) as t:
                v.tensor_scalar(row(c.rows, t), row(c.rows, t), mean[:, bass.ds(t, 1)], rstd[:, bass.ds(t, 1)], ALU.subtract, ALU.mult).then_inc(fin, 1)
            with v.Fori(0, T) as t:
                v.wait_ge(finp, t + (2 + B + 1))
                v.tensor_tensor(row(keep.x1, t), row(keep.x1, t), row(c.rows, t), ALU.add).then_inc(x5_ok, 1)
                v.wait_ge(x5_ok, t + (T + 1))
                v.bn_stats(row(keep.stats, t), row(keep.x1, t)).then_inc(st_ok, 1)
            v.wait_ge(st_ok, 2 * T)


class Kept:
    pass


def store_x(nc, x1, out):
    with ExitStack() as ctx:
        written = ctx.enter_context(nc.semaphore("written"))
        blk = ctx.enter_context(nc.Block())

        @blk.sync
        def _(sp):
            sp.dma_start(out.rearrange("(n p) d -> p n d", p=P), x1[:, :, :]).then_inc(written, 16)
            sp.wait_ge(written, 16)


def build(nc, io, out):
    with ExitStack() as ctx:
        def sb(name, shape, dt=F32):
            return ctx.enter_context(nc.sbuf_tensor(name, shape, dt))

        keep = Kept()
        keep.x1 = sb("x1", [P, T, D])
        keep.stats = sb("stats", [P, T, 6])
        keep.gate = sb("gate", [P, 4])
        keep.ident, keep.ustrict = sb("ident", [P, P]), sb("ustrict", [P, P])
        keep.ones = sb("ones_", [P, P])
        keep.xslots, keep.yslots, keep.zeroed, keep.zero_loads = {}, {}, {}, {}
        for tag, k in (("0", 1), ("1", 2)):
            n = k * T + E - 1
            keep.xslots[tag] = nc.dram_tensor(f"xslots{tag}", (n * P, D), F32, kind="Internal").ap()
            keep.yslots[tag] = nc.dram_tensor(f"yslots{tag}", (n * P, D), F32, kind="Internal").ap()
            keep.zeroed[tag] = ctx.enter_context(nc.semaphore(f"zeroed{tag}"))
            keep.zero_loads[tag] = 1
        keep.ld_w2 = ctx.enter_context(nc.semaphore("ld_expert_w2"))
        keep.ld_w1 = ctx.enter_context(nc.semaphore("ld_expert_w1"))
        with ExitStack() as w0:
            keep.sems = w0.enter_context(LayerSemaphores(nc))
            keep.w1 = w0.enter_context(nc.sbuf_tensor("w1_0", [P, E, KD, F0], F32))
            layer0_attention(nc, io, keep)
            keep.w2 = w0.enter_context(nc.sbuf_tensor("w2_0", [P, E, F0 // P, D], F32))
            routed_experts(nc, io, keep, 1, F0, ACT.Silu, 2, "0")
        with ExitStack() as w1:
            keep.w1 = w1.enter_context(nc.sbuf_tensor("w1_1", [P, E, KD, F1], F32))
            keep.w2 = w1.enter_context(nc.sbuf_tensor("w2_1", [P, E, F1 // P, D], F32))
            with ExitStack() as lc:
                keep.sems = lc.enter_context(LayerSemaphores(nc))
                c = Kept()

                def cb(name, shape):
                    return lc.enter_context(nc.sbuf_tensor(name, shape, F32))

                c.rows = cb("xt_rows", [P, T, D])
                c.kernel_dram = nc.dram_tensor("conv_kernel", (D, S), F32, kind="Internal").ap()
                with ExitStack() as lx:
                    c.xm = lx.enter_context(nc.sbuf_tensor("xm", [P, T, D], F32))
                    c.film = lx.enter_context(nc.sbuf_tensor("film", [P, T, 2 * D], F32))
                    layer1_attention(nc, io, keep, c)
                    ssm_kernel(nc, io, keep, c)
                    c.fwd = lx.enter_context(nc.sbuf_tensor("dft_table", [P, 2, 6 * P], F32))
                    c.inv = lx.enter_context(nc.sbuf_tensor("idft_table", [P, 4, W], F32))
                    c.sign = lx.enter_context(nc.sbuf_tensor("sign", [P, 1], F32))
                    c.dskip = lx.enter_context(nc.sbuf_tensor("d_skip", [P, D], F32))
                    c.kf = lx.enter_context(nc.sbuf_tensor("kernel_hat", [P, 6, 2, D], F32))
                    kernel_transform(nc, io, keep, c)
                    convolution(nc, io, keep, c)
                dense_ffn(nc, io, keep, c)
            keep.sems = w1.enter_context(LayerSemaphores(nc))
            routed_experts(nc, io, keep, 2, F1, ACT.Gelu, 3, "1")
            store_x(nc, keep.x1, out)


def constants():
    import numpy as np

    c = {"ident": np.eye(P, dtype=np.float32), "ustrict": np.triu(np.ones((P, P), np.float32), 1)}
    ch = np.arange(P)
    c["headmask16"] = np.where(ch[:, None] // DH0 == np.arange(8)[None], np.float32(DH0 ** -0.5), np.float32(0)).astype(np.float32)
    c["headmask32"] = (ch[:, None] // DH1 == np.arange(H1)[None]).astype(np.float32)
    f, t = np.arange(W)[None], np.arange(W)[:, None]
    turn = 2 * np.pi * ((f * t) % (2 * W)) / (2 * W)
    cos, sin = np.cos(turn), -np.sin(turn)
    nyquist = np.where(t % 2, -1.0, 1.0)
    ca, cb, sa, sb = cos[:, :P], cos[:, P:], sin[:, :P], sin[:, P:]
    c["dft"] = np.concatenate([ca, cb, np.hstack([nyquist, sa[:, 1:]]), sb, sa, np.hstack([nyquist, ca[:, 1:]])], 1).astype(np.float32)
    back = np.concatenate([ca, cb, np.hstack([nyquist, sa[:, 1:]]), sb], 1).T / W
    back[[0, 2 * P]] /= 2
    c["idft"] = back.astype(np.float32)
    c["sign"] = np.where(ch % 2, -1.0, 1.0).astype(np.float32)[:, None]
    e = np.arange(E, dtype=np.float32)
    c["iota_e"] = np.stack([e - 100, e])
    c["iota_t"] = np.arange(2 * T + E - 1, dtype=np.float32)
    c["part"] = np.concatenate([np.repeat(np.eye(3, dtype=np.float32), E, 0), np.tile(e, 3)[:, None]], 1)
    return c


def kernel(**inputs):
    import numpy as np
    import concourse.bacc as bacc
    from concourse.bass_utils import run_bass_kernel_spmd

    g = {k: np.asarray(v) for k, v in inputs.items()}

    def col(name, k):
        return g[name].reshape(k, -1).T

    arrays = {
        "x": g["x"].reshape(B * S, D),
        "ctxT": g["ctx_768"].reshape(B * SK, DC).T,
        "g_xattn": g["g_xattn"], "g_ffn": g["g_ffn"],
        "wq0": g["L0_xattn_Wq"], "wk0": g["L0_xattn_Wk"], "wv0": g["L0_xattn_Wv"], "wo0": g["L0_xattn_Wo"],
        "bq0T": col("L0_xattn_bq", KD), "bk0T": col("L0_xattn_bk", KD), "bv0T": col("L0_xattn_bv", KD),
        "bv0": g["L0_xattn_bv"], "bo0": g["L0_xattn_bo"],
        "w1_0": g["L0_ffn_W1"], "w2_0": g["L0_ffn_W2"], "b1_0": g["L0_ffn_b1"], "b2_0": g["L0_ffn_b2"],
        "wg0": g["L0_ffn_Wg"], "bg0": g["L0_ffn_bg"],
        "wq1": g["L1_xattn_Wq"], "wk1": g["L1_xattn_Wk"], "wv1": g["L1_xattn_Wv"],
        "w_film_in": g["L1_xattn_W_film_in"], "w_film_out": g["L1_xattn_W_film_out"],
        "b_film_in": g["L1_xattn_b_film_in"], "b_film_out": g["L1_xattn_b_film_out"],
        "mod_gate": g["L1_xattn_mod_gate"].reshape(1),
        "g_norm_in": g["L1_xattn_g_norm_in"], "b_norm_in": g["L1_xattn_b_norm_in"],
        "key_mask": g["mask_BxS2_bf1"].reshape(B * SK).view(np.uint8), "token_mask": g["mask_BxS_bf1"].reshape(T, P).T.copy().view(np.uint8),
        "a_reT": g["L1_xattn_A_re"].T, "a_imT": g["L1_xattn_A_im"].T, "c_reT": g["L1_xattn_C_re"].T, "c_imT": g["L1_xattn_C_im"].T,
        "log_dt": g["L1_xattn_log_dt"], "d_skip": g["L1_xattn_D_skip"],
        "ffn_w1": g["L1_xattn_W1"], "ffn_w2": g["L1_xattn_W2"], "ffn_b1T": col("L1_xattn_b1", 8), "ffn_b2": g["L1_xattn_b2"],
        "g_ffnT": col("L1_xattn_g_ffn", KD), "b_ffnT": col("L1_xattn_b_ffn", KD),
        "g_norm_out": g["L1_xattn_g_norm_out"], "b_norm_out": g["L1_xattn_b_norm_out"],
        "w1_1": g["L1_ffn_w1"].transpose(0, 2, 1), "w2_1": g["L1_ffn_w2"].transpose(0, 2, 1),
        "b1_1": g["L1_ffn_b1"], "b2_1": g["L1_ffn_b2"], "wg1": g["L1_ffn_router_w"].T,
        **constants(),
    }
    nc = bacc.Bacc("TRN2", target_bir_lowering=False, num_devices=1)
    arrays = {f"in_{k}": np.ascontiguousarray(a) for k, a in arrays.items()}
    io = {k[3:]: nc.dram_tensor(k, a.shape, mybir.dt.from_np(a.dtype), kind="ExternalInput").ap() for k, a in arrays.items()}
    out = nc.dram_tensor("x_out", (B * S, D), F32, kind="ExternalOutput").ap()
    build(nc, io, out)
    got = run_bass_kernel_spmd(nc, [arrays], core_ids=[0])
    return got.results[0]["x_out"].reshape(B, S, D)
```

```python
from contextlib import ExitStack

import concourse.bass as bass
from concourse import mybir

ALU = mybir.AluOpType
ACT = mybir.ActivationFunctionType
F32 = mybir.dt.float32
BF16 = mybir.dt.bfloat16
I32 = mybir.dt.int32
U32 = mybir.dt.uint32
U8 = mybir.dt.uint8
AX = mybir.AxisListType.X

P = 128
B, S, D = 4, 512, 256
SK, DC = 64, 192
T = B * S // P
TB = S // P
KD = D // P
KC = 96
H0 = 16
DH0 = D // H0
HP0 = H0 // 2
CLAMP = 10000.0
EPS = 1e-5
E = 8
F0, F1 = 1024, 512
LOWEST = -3.0e38


def static(v):
    return isinstance(v, int)


def wait(eng, sem, value, at):
    if at >= 1:
        eng.wait_ge(sem, value)


def pipeline(eng, slot, first, steady, stop, last):
    for t in range(first, steady):
        slot(t, t)
    with eng.Fori(0, (stop - steady) // 2) as i:
        for u in range(2):
            slot(i * 2 + (steady + u), steady + u)
    for t in range(stop, last + 1):
        slot(t, t)


def row(buf, t):
    return buf[:, bass.ds(t, 1), :].rearrange("p a n -> p (a n)")


def halves(stats):
    return stats[:, :, 1], stats[:, :, 2], stats[:, :, 4], stats[:, :, 5]


def norm_from_stats(v, act_done, sem, stats, tmp, mean, rstd, var_only=None):
    m0, q0, m1, q1 = halves(stats)
    v.tensor_tensor(tmp[:, 1, :], m0, m1, ALU.subtract).then_inc(sem, 1)
    v.tensor_tensor(tmp[:, 2, :], q0, q1, ALU.add).then_inc(sem, 1)
    v.tensor_tensor(mean[:, :], m0, m1, ALU.add).then_inc(sem, 1)
    v.wait_ge(sem, act_done + 3)
    v.tensor_tensor(tmp[:, 3, :], tmp[:, 1, :], tmp[:, 1, :], ALU.mult).then_inc(sem, 1)
    v.tensor_scalar(tmp[:, 2, :], tmp[:, 2, :], 1.0 / D, EPS, ALU.mult, ALU.add).then_inc(sem, 1)
    v.tensor_scalar(mean[:, :], mean[:, :], 0.5, None, ALU.mult).then_inc(sem, 1)
    v.wait_ge(sem, act_done + 6)
    v.scalar_tensor_tensor(tmp[:, 0, :], tmp[:, 3, :], 0.25, tmp[:, 2, :], ALU.mult, ALU.add).then_inc(sem, 1)
    return act_done + 7


class LayerSemaphores:

    def __init__(self, nc):
        self.nc, self.held = nc, []

    def __enter__(self):
        return self

    def new(self, name):
        self.held.append(self.nc.alloc_semaphore(name))
        return self.held[-1]

    def __exit__(self, *failed):
        if failed[0] is None:
            self.nc.clear_and_free_semaphores(self.held)
            self.nc.all_engine_barrier()


def layer0_attention(nc, io, keep):
    with ExitStack() as ctx:
        def sb(name, shape, dt=F32):
            return ctx.enter_context(nc.sbuf_tensor(name, shape, dt))

        def bank(name):
            return ctx.enter_context(nc.psum_tensor(name, [P, 512], F32))

        sem = keep.sems.new

        x = sb("x_in", [P, T, D])
        ctxT = sb("ctxT", [KC, 2, B, 2, SK])
        wq, wo = sb("wq0", [P, KD, D]), sb("wo0", [P, KD, D])
        wk, wv = sb("wk0", [KC, 2, D]), sb("wv0", [KC, 2, D])
        bqT, bkT, bvT = sb("bqT", [P, KD]), sb("bkT", [P, KD]), sb("bvT", [P, KD])
        bv, bo = sb("bv_rows", [P, D]), sb("bo_rows", [P, D])
        headmask = sb("headmask", [P, 8])
        kT = sb("kT", [P, KD, B, SK])
        kbd = sb("k_blockdiag", [P, B, KD, 8, SK])
        vbd = sb("v_blockdiag", [P, B, HP0, 2 * (DH0 + 1)])
        csum = sb("ctx_sum", [KC, 2, B])
        vmT = sb("vmeanT", [P, KD, B])
        vmTw = sb("vmeanT_wide", [P, KD, B, P])
        gv = sb("guard_rows", [P, B, D])
        stats = sb("stats_x", [P, T, 6])
        gstats = sb("stats_guard", [P, T, 6])
        tmp, mean, rstd = sb("tmp_x", [P, 4, T]), sb("mean_x", [P, T]), sb("rstd_x", [P, T])
        xn = sb("xn", [P, 2, D])
        xnT, qT = sb("xnT", [P, KD, P]), sb("qT", [P, 2, KD, P])
        sc = sb("scores", [P, 2, H0, SK])
        top = sb("rowmax", [P, 2, H0])
        pT = sb("probsT", [P, HP0, P])
        junk = sb("junk", [P, 2, 512], BF16)
        nanp, nans, nanm = sb("nan_part", [P, 4]), sb("nan_sum", [P, 1]), sb("nan_mask", [P, 1])
        ones = sb("ones", [P, P])
        nanw = sb("nan_wide", [P, D], I32)
        zeros = sb("zeros", [P, 2 * D])
        rden, oN, oT = sb("rden", [P, H0]), sb("oN", [P, D]), sb("oT", [P, KD, P])

        s0 = [ctx.enter_context(nc.psum_tensor(f"S{i}", [P, 2, 512], F32)) for i in range(2)]
        pt0 = ctx.enter_context(nc.psum_tensor("PT", [P, 2, 512], F32))
        m0, m1 = bank("M0"), bank("M1")

        ld_x = [sem(f"ld_x{b}") for b in range(B)]
        ld_w = sem("ld_w")
        ld_ctx = sem("ld_ctx")
        gates = sem("gates_done")
        dve = sem("dve_chain")
        pool = sem("pool_chain")
        setup_mm = sem("setup_matmuls")
        kbd_ok, vbd_ok = sem("kbd_ready"), sem("vbd_ready")
        std_ok, rstd_ok = sem("std_ready"), sem("rstd_ready")
        xn_ok, xT_ok, xnT_ok, q_ok, qT_ok = (sem(n) for n in ("xn_ready", "xT_in_psum", "xnT_ready", "q_in_psum", "qT_ready"))
        s_ok, max_ok, cmax_ok, clip_ok, abs_ok = (sem(n) for n in ("scores_ready", "max_ready", "cmax_ready", "clip_ready", "abs_done"))
        sub_ok, exp_ok = sem("shifted_ready"), sem("probs_ready")
        pT_ok, pTa_ok, pTd_ok = sem("probsT_in_psum"), sem("probsT_act_half"), sem("probsT_dve_half")
        o_ok, rden_ok, oN_ok, oT_ok, oTs_ok, wo_ok = (sem(n) for n in ("o_in_psum", "rden_ready", "oN_ready", "oT_in_psum", "oT_ready", "proj_ready"))
        res_ok, xb_ok, xg_ok = sem("x1_ready"), sem("xb_ready"), sem("xg_ready")
        gst_ok, st_ok, nan_ok, flag_ok = sem("guard_stats_done"), sem("stats_done"), sem("nan_added"), sem("flag_ready")
        zero_ok = sem("zeros_ready")
        gv_ok, vm_ok = sem("gv_ready"), sem("vm_ready")

        xv = io["x"].rearrange("(n p) d -> p n d", p=P)
        cv = io["ctxT"].rearrange("(k c) (b s) -> c k b s", k=2, b=B)

        N_SMALL = 10
        blk = ctx.enter_context(nc.Block())

        @blk.sync
        def _(sp):
            for k in range(2):
                for dup in range(2):
                    sp.dma_start(ctxT[:, k, :, dup, :], cv[:, k]).then_inc(ld_ctx, 16)
            sp.dma_start(wk[:, :, :], io["wk0"].rearrange("(k c) n -> c k n", k=2)).then_inc(ld_ctx, 16)
            sp.dma_start(wv[:, :, :], io["wv0"].rearrange("(k c) n -> c k n", k=2)).then_inc(ld_ctx, 16)
            for b in range(B):
                sp.dma_start(x[:, TB * b:TB * b + TB, :], xv[:, TB * b:TB * b + TB, :]).then_inc(ld_x[b], 16)
            sp.dma_start(wq[:, :, :], io["wq0"].rearrange("(k c) n -> c k n", k=KD)).then_inc(ld_w, 16)
            sp.dma_start(wo[:, :, :], io["wo0"].rearrange("(k c) n -> c k n", k=KD)).then_inc(ld_w, 16)
            sp.dma_start(keep.gate[:, 0:2], io["g_xattn"].partition_broadcast(P)).then_inc(ld_w, 16)
            sp.dma_start(keep.gate[:, 2:4], io["g_ffn"].partition_broadcast(P)).then_inc(ld_w, 16)
            sp.dma_start(bqT[:, :], io["bq0T"]).then_inc(ld_w, 16)
            sp.dma_start(bkT[:, :], io["bk0T"]).then_inc(ld_w, 16)
            sp.dma_start(bvT[:, :], io["bv0T"]).then_inc(ld_w, 16)
            sp.dma_start(bv[:, :], io["bv0"].partition_broadcast(P)).then_inc(ld_w, 16)
            sp.dma_start(bo[:, :], io["bo0"].partition_broadcast(P)).then_inc(ld_w, 16)
            sp.dma_start(headmask[:, :], io["headmask16"]).then_inc(ld_w, 16)
            sp.dma_start(keep.ident[:, :], io["ident"]).then_inc(ld_w, 16)
            sp.dma_start(keep.ustrict[:, :], io["ustrict"]).then_inc(ld_w, 16)
            sp.wait_ge(zero_ok, 1)
            for tag, slots in keep.xslots.items():
                sp.dma_start(slots.rearrange("(n p) d -> p n d", p=P),
                             zeros[:, 0:D].unsqueeze(1).to_broadcast([P, slots.shape[0] // P, D])).then_inc(keep.zeroed[tag], 16)
            for e in range(E):
                sp.dma_start(keep.w1[:, e, :, :], io["w1_0"][e].rearrange("(k c) n -> c k n", k=KD)).then_inc(keep.ld_w1, 16)


        @blk.gpsimd
        def _(gp):
            gp.memset(zeros[:, :], 0.0).then_inc(zero_ok, 1)
            gp.memset(ones[:, :], 1.0).then_inc(pool, 1)
            gp.memset(vbd[:, :, :, :], 0.0).then_inc(pool, 1)
            gp.wait_ge(gates, 1)
            gp.tensor_scalar(bo[:, :], bo[:, :], keep.gate[:, 0:1], None, ALU.mult).then_inc(pool, 1)
            gp.wait_ge(pool, 3)
            def slot(t, at):
                if 0 <= at < T:
                    gp.wait_ge(clip_ok, t + 1)
                    gp.wait_ge(cmax_ok, t + 1)
                    b = sc[:, at % 2, :, :]
                    gp.tensor_tensor(b, b, top[:, at % 2, :].unsqueeze(2).to_broadcast([P, H0, SK]), ALU.subtract).then_inc(sub_ok, 1)
                    gp.tensor_tensor(row(x, t), row(x, t), bo[:, :], ALU.add).then_inc(xb_ok, 1)
                if 0 <= at - 4 < T:
                    gp.wait_ge(res_ok, t - 3)
                    gp.tensor_tensor(row(x, t - 4), row(x, t - 4), row(gv, (t - 4) // TB), ALU.add).then_inc(xg_ok, 1)
            for b in range(B):
                gp.wait_ge(ld_x[b], 16)
            gp.wait_ge(rstd_ok, 1)
            gp.wait_ge(xn_ok, 1)
            gp.wait_ge(gv_ok, B)
            pipeline(gp, slot, 0, 4, T, T + 3)

        @blk.scalar
        def _(act):
            act.wait_ge(ld_w, 16 * (N_SMALL + 2))
            nc.scalar.activation(keep.gate[:, :], keep.gate[:, :], ACT.Tanh).then_inc(gates, 1)
            act.wait_ge(rstd_ok, 1)
            nc.scalar.activation(rstd[:, :], tmp[:, 0, :], ACT.Sqrt).then_inc(std_ok, 1)

            def slot(t, at):
                if 0 <= at - 2 < T:
                    act.wait_ge(pT_ok, t - 1)
                    wait(act, o_ok, t - 2, at - 2)
                    nc.scalar.activation(pT[:, 0:4, :], pt0[:, 0, :].rearrange("p (a n) -> p a n", n=P), ACT.Copy).then_inc(pTa_ok, 1)
                if 0 <= at - 3 < T:
                    act.wait_ge(oT_ok, t - 2)
                    wait(act, wo_ok, t - 3, at - 3)
                    nc.scalar.activation(oT[:, :, :], m1[:, 0:KD * P].rearrange("p (k n) -> p k n", k=KD), ACT.Copy).then_inc(oTs_ok, 1)
                if 0 <= at + 1 < T:
                    act.wait_ge(xT_ok, t + 2)
                    wait(act, q_ok, t + 1, at + 1)
                    nc.scalar.activation(xnT[:, :, :], m0[:, 0:KD * P].rearrange("p (k n) -> p k n", k=KD), ACT.Copy).then_inc(xnT_ok, 1)
                if 0 <= at - 1 < T:
                    u = (at - 1) % 2
                    act.wait_ge(sub_ok, t)
                    nc.scalar.activation(sc[:, u, :, :], sc[:, u, :, :], ACT.Exp).then_inc(exp_ok, 1)
                    act.wait_ge(clip_ok, t)
                    wait(act, nan_ok, t - 2, at - 2)
                    wait(act, abs_ok, 2 * t - 2, 2 * at - 2)
                    for h in range(2):
                        nc.scalar.activation(junk[:, h, :], s0[u][:, h, :], ACT.Abs,
                                             accum_out=nanp[:, 2 * u + h:2 * u + h + 1]).then_inc(abs_ok, 1)
            pipeline(act, slot, -1, 4, T - 2, T + 2)

        @blk.tensor
        def _(pe):
            pe.wait_ge(ld_ctx, 16 * 6)
            for m in range(KD):
                for k in range(2):
                    mm = nc.tensor.matmul(s0[0][:, m, 0:B * SK], wk[:, k, m * P:(m + 1) * P], ctxT[:, k, :, 0, :],
                                          start=(k == 0), stop=(k == 1))
                mm.then_inc(setup_mm, 1)
            for b in range(B):
                for k in range(2):
                    mm = nc.tensor.matmul((s0[1], pt0)[b // 2][:, b % 2, 0:D], ctxT[:, k, b, :, :].rearrange("c u s -> c (u s)"), wv[:, k, :],
                                          start=(k == 0), stop=(k == 1))
                mm.then_inc(setup_mm, 1)
            pe.wait_ge(vm_ok, 1)
            for m in range(KD):
                for k in range(2):
                    mm = nc.tensor.matmul(m1[:, m * B:(m + 1) * B], wv[:, k, m * P:(m + 1) * P], csum[:, k, :],
                                          start=(k == 0), stop=(k == 1))
            mm.then_inc(setup_mm, 1)
            pe.wait_ge(vm_ok, 3)
            pe.wait_ge(ld_w, 16 * (N_SMALL + 2))
            for b in range(B):
                pe.wait_ge(vbd_ok, 2 * B + 2)
                for k in range(KD):
                    mm = nc.tensor.matmul((s0[1], pt0)[b // 2][:, b % 2, 0:D], vmTw[:, k, b, :], wo[:, k, :],
                                          start=(k == 0), stop=(k == KD - 1))
                mm.then_inc(setup_mm, 1)
            pe.wait_ge(gv_ok, B)
            pe.wait_ge(kbd_ok, B * KD)

            def slot(t, at):
                def scores(m):
                    return nc.tensor.matmul(s0[at % 2][:, m, :], qT[:, at % 2, m, :],
                                            kbd[:, bass.ds(t // TB, 1), m, :, :].rearrange("p a h s -> p (a h s)"),
                                            start=True, stop=True)

                if 0 <= at - 2 < T:
                    u = at % 2
                    pe.wait_ge(exp_ok, t - 1)
                    wait(pe, pTa_ok, t - 2, at - 2)
                    wait(pe, pTd_ok, t - 2, at - 2)
                    for a in range(HP0):
                        mm = nc.tensor.transpose(pt0[:, a // 4, (a % 4) * P:(a % 4 + 1) * P],
                                                 sc[:, u, 2 * a:2 * a + 2, :].rearrange("p h s -> p (h s)"), keep.ident[:, :])
                    mm.then_inc(pT_ok, 1)
                if 0 <= at - 3 < T:
                    pe.wait_ge(oN_ok, t - 2)
                    for k in range(KD):
                        mm = nc.tensor.transpose(m1[:, k * P:(k + 1) * P], oN[:, k * P:(k + 1) * P], keep.ident[:, :])
                    mm.then_inc(oT_ok, 1)
                if 0 <= at + 1 < T:
                    u = (at + 1) % 2
                    pe.wait_ge(xn_ok, t + 2)
                    wait(pe, qT_ok, t + 1, at + 1)
                    for k in range(KD):
                        mm = nc.tensor.transpose(m0[:, k * P:(k + 1) * P], xn[:, u, k * P:(k + 1) * P], keep.ident[:, :])
                    mm.then_inc(xT_ok, 1)
                if 0 <= at < T:
                    pe.wait_ge(qT_ok, t + 1)
                    wait(pe, abs_ok, 2 * t - 2, 2 * at - 2)
                    scores(0)
                if 0 <= at - 3 < T:
                    pe.wait_ge(oTs_ok, t - 2)
                    for k in range(KD):
                        mm = nc.tensor.matmul(m1[:, 0:D], oT[:, k, :], wo[:, k, :], start=(k == 0), stop=(k == KD - 1))
                    mm.then_inc(wo_ok, 1)
                if 0 <= at + 1 < T:
                    pe.wait_ge(xnT_ok, t + 2)
                    for m in range(KD):
                        for k in range(KD):
                            mm = nc.tensor.matmul(m0[:, m * P:(m + 1) * P], wq[:, k, m * P:(m + 1) * P], xnT[:, k, :],
                                                  start=(k == 0), stop=(k == KD - 1))
                    mm.then_inc(q_ok, 1)
                if 0 <= at < T:
                    scores(1).then_inc(s_ok, 1)
                if 0 <= at - 2 < T:
                    pe.wait_ge(pTa_ok, t - 1)
                    pe.wait_ge(pTd_ok, t - 1)
                    wait(pe, res_ok, t - 2, at - 2)
                    for a in range(HP0):
                        mm = nc.tensor.matmul(m1[:, 34 * a:34 * a + 34], pT[:, a, :],
                                              vbd[:, bass.ds((t - 2) // TB, 1), a, :].rearrange("p a n -> p (a n)"), start=True, stop=True)
                    mm.then_inc(o_ok, 1)
            pipeline(pe, slot, -1, 4, T - 2, T + 2)
            pe.wait_ge(flag_ok, 1)
            nc.tensor.matmul(m0[:, 0:1], ones[:, :], nans[:, :], start=True, stop=True).then_inc(setup_mm, 1)

        @blk.vector
        def _(v):
            v.memset(nans[:, :], 0.0).then_inc(dve, 1)
            for b in range(B):
                v.wait_ge(ld_x[b], 16)
                for t in range(TB * b, TB * b + TB):
                    v.bn_stats(stats[:, t, :], x[:, t, :]).then_inc(dve, 1)
            v.wait_ge(dve, 1 + T)
            n = norm_from_stats(v, 1 + T, dve, stats, tmp, mean, rstd)
            v.wait_ge(dve, n)
            v.sem_inc(rstd_ok, 1)
            v.wait_ge(ld_ctx, 16 * 6)
            v.reduce_sum(csum[:, :, :], ctxT[:, :, :, 0, :], AX).then_inc(vm_ok, 1)
            v.wait_ge(ld_w, 16 * (N_SMALL + 2))
            for m in range(KD):
                v.wait_ge(setup_mm, m + 1)
                v.tensor_scalar(kT[:, m, :, :], s0[0][:, m, 0:B * SK].rearrange("p (b s) -> p b s", b=B), bkT[:, m:m + 1], None, ALU.add).then_inc(dve, 1)
            v.wait_ge(dve, n + 2)
            for m in range(KD):
                for b in range(B):
                    v.tensor_tensor(kbd[:, b, m, :, :], kT[:, m, b, :].unsqueeze(1).to_broadcast([P, 8, SK]),
                                    headmask[:, :].unsqueeze(2).to_broadcast([P, 8, SK]), ALU.mult).then_inc(kbd_ok, 1)
            v.wait_ge(pool, 2)
            for u in range(2):
                v.memset(vbd[64 * u:64 * u + 64, :, :, 17 * u + DH0:17 * u + DH0 + 1], 1.0).then_inc(vbd_ok, 1)
            bvv = bv[:, :].rearrange("p (a u j) -> p a u j", u=2, j=DH0)
            for b in range(B):
                v.wait_ge(setup_mm, KD + b + 1)
                vp = (s0[1], pt0)[b // 2][:, b % 2, 0:D].rearrange("p (a u j) -> p a u j", u=2, j=DH0)
                for u in range(2):
                    q = slice(64 * u, 64 * u + 64)
                    v.tensor_tensor(vbd[q, b, :, 17 * u:17 * u + DH0], vp[q, :, u, :], bvv[q, :, u, :], ALU.add).then_inc(vbd_ok, 1)
            v.wait_ge(setup_mm, KD + B + 1)
            for m in range(KD):
                v.tensor_scalar(vmT[:, m, :], m1[:, m * B:(m + 1) * B], 1.0 / SK, bvT[:, m:m + 1], ALU.mult, ALU.add).then_inc(dve, 1)
            v.wait_ge(dve, n + 4)
            for m in range(KD):
                v.tensor_copy(vmTw[:, m, :, :], vmT[:, m, :].unsqueeze(2).to_broadcast([P, B, P])).then_inc(vm_ok, 1)
            v.wait_ge(gates, 1)
            for b in range(B):
                v.wait_ge(setup_mm, KD + B + 2 + b)
                v.tensor_scalar(gv[:, b, :], (s0[1], pt0)[b // 2][:, b % 2, 0:D], keep.gate[:, 0:1], None, ALU.mult).then_inc(gv_ok, 1)
            v.wait_ge(std_ok, 1)
            v.reciprocal(rstd[:, :], rstd[:, :]).then_inc(dve, 1)
            v.wait_ge(dve, n + 5)

            def slot(t, at):
                if 0 <= at - 2 < T:
                    v.wait_ge(pT_ok, t - 1)
                    wait(v, o_ok, t - 2, at - 2)
                    v.tensor_copy(pT[:, 4:8, :], pt0[:, 1, :].rearrange("p (a n) -> p a n", n=P)).then_inc(pTd_ok, 1)
                if 0 <= at + 2 < T:
                    wait(v, xT_ok, t + 1, at + 1)
                    v.tensor_scalar(xn[:, at % 2, :], row(x, t + 2), mean[:, bass.ds(t + 2, 1)], rstd[:, bass.ds(t + 2, 1)],
                                    ALU.subtract, ALU.mult).then_inc(xn_ok, 1)
                if 0 <= at - 3 < T:
                    v.wait_ge(wo_ok, t - 2)
                    v.wait_ge(xb_ok, t - 2)
                    v.scalar_tensor_tensor(row(keep.x1, t - 3), m1[:, 0:D], keep.gate[:, 0:1], row(x, t - 3), ALU.mult, ALU.add).then_inc(res_ok, 1)
                if 0 <= at + 1 < T:
                    u = (at + 1) % 2
                    v.wait_ge(q_ok, t + 2)
                    wait(v, s_ok, t, at)
                    v.tensor_tensor(qT[:, u, :, :], m0[:, 0:KD * P].rearrange("p (k n) -> p k n", k=KD),
                                    bqT[:, :].unsqueeze(2).to_broadcast([P, KD, P]), ALU.add).then_inc(qT_ok, 1)
                if 0 <= at < T:
                    u = at % 2
                    sv = s0[u][:, :, :].rearrange("p m (h s) -> p (m h) s", s=SK)
                    v.wait_ge(s_ok, t + 1)
                    wait(v, sub_ok, t - 1, at - 1)
                    v.reduce_max(top[:, u, :], sv, AX).then_inc(max_ok, 1)
                    wait(v, pT_ok, t - 1, at - 1)
                    v.tensor_scalar(sc[:, u, :, :], sv, CLAMP, -CLAMP, ALU.min, ALU.max).then_inc(clip_ok, 1)
                    v.wait_ge(max_ok, t + 1)
                    v.tensor_scalar(top[:, u, :], top[:, u, :], CLAMP, -CLAMP, ALU.min, ALU.max).then_inc(cmax_ok, 1)
                if 0 <= at - 2 < T:
                    ov = m1[:, 0:34 * HP0].rearrange("p (h j) -> p h j", j=DH0 + 1)
                    v.wait_ge(o_ok, t - 1)
                    v.reciprocal(rden[:, :], ov[:, :, DH0]).then_inc(rden_ok, 1)
                    v.wait_ge(rden_ok, t - 1)
                    wait(v, oT_ok, t - 2, at - 2)
                    v.tensor_tensor(oN[:, :].rearrange("p (h j) -> p h j", j=DH0), ov[:, :, 0:DH0],
                                    rden[:, :].unsqueeze(2).to_broadcast([P, H0, DH0]), ALU.mult).then_inc(oN_ok, 1)
                if 0 <= at - 1 < T:
                    u = (at - 1) % 2
                    v.wait_ge(abs_ok, 2 * t)
                    wait(v, nan_ok, t - 1, at - 1)
                    v.scalar_tensor_tensor(nans[:, :], nanp[:, 2 * u:2 * u + 1], nanp[:, 2 * u + 1:2 * u + 2],
                                           nans[:, :], ALU.add, ALU.add).then_inc(nan_ok, 1)
                if 0 <= at - 4 < T:
                    v.wait_ge(res_ok, t - 3)
                    v.bn_stats(row(keep.stats, t - 4), row(keep.x1, t - 4)).then_inc(st_ok, 1)
                if 0 <= at - 5 < T:
                    v.wait_ge(xg_ok, t - 4)
                    v.bn_stats(row(gstats, t - 5), row(x, t - 5)).then_inc(gst_ok, 1)
            pipeline(v, slot, -2, 6, T - 2, T + 4)
            v.wait_ge(nan_ok, T)
            v.tensor_tensor(nans[:, :], nans[:, :], nans[:, :], ALU.not_equal).then_inc(flag_ok, 1)
            v.wait_ge(setup_mm, KD + B + 1 + B + 1)
            v.tensor_scalar(nanm[:, :], m0[:, 0:1], 0.0, None, ALU.is_gt).then_inc(flag_ok, 1)
            v.wait_ge(flag_ok, 2)
            v.tensor_copy(nanw[:, :], nanm[:, :].to_broadcast([P, D])).then_inc(flag_ok, 1)
            v.wait_ge(flag_ok, 3)
            v.wait_ge(xg_ok, T)
            v.wait_ge(st_ok, T)
            v.wait_ge(gst_ok, T)
            v.copy_predicated(keep.x1[:, :, :], nanw[:, :].unsqueeze(1).to_broadcast([P, T, D]), x[:, :, :]).then_inc(flag_ok, 1)
            v.copy_predicated(keep.stats[:, :, :], nanw[:, 0:6].unsqueeze(1).to_broadcast([P, T, 6]), gstats[:, :, :]).then_inc(flag_ok, 1)
            v.wait_ge(flag_ok, 5)


def routed_experts(nc, io, keep, K, F, act_fn, gate_col, tag):
    V = K * T
    NT = V + E - 1
    KF = F // P
    HB = F // 512
    xslots, yslots = keep.xslots[tag], keep.yslots[tag]

    with ExitStack() as ctx:
        def sb(name, shape, dt=F32):
            return ctx.enter_context(nc.sbuf_tensor(f"{name}{tag}", shape, dt))

        rows = sb("ln_rows", [P, T, D])
        picks = sb("picks", [P, V], U32)
        prob = sb("prob", [P, V])
        tile_expert = sb("tile_expert", [P, NT], I32)
        hot = sb("tile_hot", [3 * E, NT, P], BF16)
        b1x, b2x = sb("b1_parts", [3 * E, F], BF16), sb("b2_parts", [3 * E, D], BF16)

        with ExitStack() as rctx:
            def rb(name, shape, dt=F32):
                return rctx.enter_context(nc.sbuf_tensor(f"{name}{tag}", shape, dt))

            def rsem(name):
                return keep.sems.new(f"{name}{tag}")

            xs, xsT = rb("xs", [P, 2, D]), rb("xsT", [P, 2, KD, P])
            tmp, mean, rstd = rb("tmp", [P, 4, T]), rb("mean", [P, T]), rb("rstd", [P, T])
            wg = rb("wg", [P, KD, E])
            bg = rb("bg", [P, E])
            lg, ex = rb("logits", [P, T, E]), rb("ex", [P, T, E])
            oh = rb("onehot", [P, V, E])
            pre = [rb(f"prefix{i}", [P, V, E]) for i in range(2)]
            lmax = rb("lmax", [P, 2, T])
            first = rb("first", [P, T])
            iota = rb("iota", [P, 2, E])
            iota_t = rb("iota_t", [P, NT])
            cnt, cnti = rb("cnt", [P, E]), rb("cnti", [P, E], I32)
            ends = [rb(f"ends{i}", [P, E]) for i in range(2)]
            base = rb("base", [P, E])
            slotf = rb("slot_f", [P, V])
            past = rb("past", [P, NT, E])
            tef = rb("tile_expert_f", [P, NT])
            part = rb("part", [3 * E, 4])
            bf = rb("b_split", [3 * E, 2, F])
            bh = rb("b_high", [3 * E, 2, F], BF16)
            xT_bank = [rctx.enter_context(nc.psum_tensor(f"xT_ps{tag}{i}", [P, 512], F32)) for i in range(2)]
            lg_bank = rctx.enter_context(nc.psum_tensor(f"lg{tag}", [P, 512], F32))
            rank_bank = rctx.enter_context(nc.psum_tensor(f"rank{tag}", [P, 512], F32))
            cnt_bank = rctx.enter_context(nc.psum_tensor(f"count_ps{tag}", [P, 512], F32))

            ld, dve, pool = rsem("ld_route"), rsem("dve_chain"), rsem("pool_chain")
            var_ok, std_ok, ones_ok = rsem("var_ready"), rsem("std_ready"), rsem("ones_ready")
            xs_ok, xT_ok, xsT_ok, lg_ok = rsem("xs_ready"), rsem("xT_in_psum"), rsem("xsT_ready"), rsem("logits_ready")
            rows_ok, shift_ok, ex_ok = rsem("rows_ready"), rsem("shifted_ready"), rsem("exp_ready")
            oh_ok, pre_ok, rank_ok = rsem("onehot_ready"), rsem("prefix_ready"), rsem("rank_ready")
            pick_ok, scattered = rsem("picks_ready"), rsem("scattered")

            blk = rctx.enter_context(nc.Block())

            @blk.sync
            def _(sp):
                sp.dma_start(wg[:, :, :], io["wg" + tag].rearrange("(k c) e -> c k e", k=KD)).then_inc(ld, 16)
                if K == 1:
                    sp.dma_start(bg[:, :], io["bg" + tag].partition_broadcast(P)).then_inc(ld, 16)
                sp.dma_start(iota[:, :, :], io["iota_e"].partition_broadcast(P)).then_inc(ld, 16)
                sp.dma_start(iota_t[:, :], io["iota_t"][0:NT].partition_broadcast(P)).then_inc(ld, 16)
                sp.dma_start(part[:, :], io["part"]).then_inc(ld, 16)
                for q in range(3):
                    sp.dma_start(bf[E * q:E * q + E, 0, :], io["b1_" + tag]).then_inc(ld, 16)
                    sp.dma_start(bf[E * q:E * q + E, 1, 0:D], io["b2_" + tag]).then_inc(ld, 16)
                if K == 1:
                    for e in range(E):
                        sp.dma_start(keep.w2[:, e, :, :], io["w2_" + tag][e].rearrange("(k c) n -> c k n", k=KF)).then_inc(keep.ld_w2, 16)

            LOADS = 16 * (11 if K == 1 else 10)

            @blk.gpsimd
            def _(gp):
                gp.wait_ge(ld, LOADS)
                n = 0
                def link(ins):
                    nonlocal n
                    n += 1
                    ins.then_inc(pool, 1)
                    gp.wait_ge(pool, n)
                for j, w, dst in ((0, F, b1x), (1, D, b2x)):
                    r = bf[:, j, 0:w]
                    hi = bh[:, 0, 0:w]
                    acc = bh[:, 1, 0:w]
                    for q in range(3):
                        link(gp.tensor_copy(hi, r))
                        if q == 0:
                            link(gp.tensor_scalar(dst[:, :], hi, part[:, 0:1], None, ALU.mult))
                        else:
                            link(gp.tensor_scalar(acc, hi, part[:, q:q + 1], None, ALU.mult))
                            link(gp.tensor_tensor(dst[:, :], dst[:, :], acc, ALU.add))
                        if q < 2:
                            link(gp.tensor_tensor(r, r, hi, ALU.subtract))
                gp.wait_ge(pick_ok, 1)
                gp.wait_ge(rows_ok, T)
                gp.wait_ge(keep.zeroed[tag], 16 * keep.zero_loads[tag])
                for c in range(V):
                    gp.indirect_dma_start(xslots, bass.IndirectOffsetOnAxis(ap=picks[:, c:c + 1], axis=0), rows[:, c % T, :], None,
                                          bounds_check=NT * P - 1, oob_is_err=False).then_inc(scattered, 16)
                gp.wait_ge(scattered, 16 * V)

            @blk.scalar
            def _(act):
                act.wait_ge(var_ok, 1)
                nc.scalar.activation(rstd[:, :], tmp[:, 0, :], ACT.Sqrt).then_inc(std_ok, 1)
                with act.Fori(0, T // 2) as i:
                    for u in range(2):
                        act.wait_ge(xT_ok, i * 2 + (u + 1))
                        nc.scalar.activation(xsT[:, u, :, :], xT_bank[u][:, 0:D].rearrange("p (k n) -> p k n", k=KD), ACT.Copy).then_inc(xsT_ok, 1)
                act.wait_ge(shift_ok, 1)
                shifted = ex[:, :, :] if K == 1 else ex[:, :, 0]
                nc.scalar.activation(shifted, shifted, ACT.Exp).then_inc(ex_ok, 1)

            @blk.tensor
            def _(pe):
                pe.wait_ge(ld, LOADS)

                def slot(t, at):
                    u = at % 2
                    if at < T:
                        pe.wait_ge(xs_ok, t + 1)
                        wait(pe, xsT_ok, t - 1, at - 1)
                        for k in range(KD):
                            mm = nc.tensor.transpose(xT_bank[u][:, k * P:(k + 1) * P], xs[:, u, k * P:(k + 1) * P], keep.ident[:, :])
                        mm.then_inc(xT_ok, 1)
                    if at >= 1:
                        pe.wait_ge(xsT_ok, t)
                        for k in range(KD):
                            mm = nc.tensor.matmul(lg_bank[:, bass.ds((t - 1) * E, E)], xsT[:, 1 - u, k, :], wg[:, k, :],
                                                  start=(k == 0), stop=(k == KD - 1))
                        mm.then_inc(lg_ok, 1)
                pipeline(pe, slot, 0, 2, T, T)
                pe.wait_ge(oh_ok, 1)
                nc.tensor.matmul(rank_bank[:, 0:V * E], keep.ustrict[:, :], oh[:, :, :].rearrange("p v e -> p (v e)"), start=True, stop=False)
                pe.wait_ge(pre_ok, 1)
                pe.wait_ge(ones_ok, 1)
                nc.tensor.matmul(rank_bank[:, 0:V * E], keep.ones[:, :], pre[1][:, :, :].rearrange("p v e -> p (v e)"), start=False, stop=True).then_inc(rank_ok, 1)
                nc.tensor.matmul(cnt_bank[:, 0:E], keep.ones[:, :], pre[1][:, V - 1, :], start=True, stop=False)
                nc.tensor.matmul(cnt_bank[:, 0:E], keep.ones[:, :], oh[:, V - 1, :], start=False, stop=True).then_inc(rank_ok, 1)

            @blk.vector
            def _(v):
                done = [0]

                def link(ins):
                    done[0] += 1
                    ins.then_inc(dve, 1)
                    v.wait_ge(dve, done[0])

                def e_cols(a):
                    return a.unsqueeze(2).to_broadcast([P, T, E])

                def over_t(a, n=T):
                    return a.unsqueeze(1).to_broadcast([P, n, E])

                v.memset(keep.ones[:, :], 1.0).then_inc(ones_ok, 1)
                done[0] = norm_from_stats(v, 0, dve, keep.stats, tmp, mean, rstd)
                v.wait_ge(dve, done[0])
                v.sem_inc(var_ok, 1)
                v.wait_ge(std_ok, 1)
                link(v.reciprocal(rstd[:, :], rstd[:, :]))

                def ln(dst, t, ok):
                    v.tensor_scalar(dst, row(keep.x1, t), mean[:, bass.ds(t, 1)], rstd[:, bass.ds(t, 1)], ALU.subtract, ALU.mult).then_inc(ok, 1)

                def slot(t, at):
                    wait(v, xT_ok, t - 1, at - 1)
                    ln(xs[:, at % 2, :], t, xs_ok)
                    ln(row(rows, t), t, rows_ok)
                pipeline(v, slot, 0, 2, T, T - 1)

                v.wait_ge(lg_ok, T)
                v.wait_ge(ld, LOADS)
                logits = lg_bank[:, 0:T * E].rearrange("p (t e) -> p t e", e=E)
                link(v.tensor_tensor(lg[:, :, :], logits, over_t(bg[:, :]), ALU.add) if K == 1 else v.tensor_copy(lg[:, :, :], logits))
                for c in range(K):
                    o = oh[:, c * T:(c + 1) * T, :]
                    link(v.reduce_max(lmax[:, c, :], lg[:, :, :], AX))
                    link(v.tensor_tensor(o, lg[:, :, :], e_cols(lmax[:, c, :]), ALU.is_equal))
                    link(v.tensor_tensor(o, o, over_t(iota[:, 0, :]), ALU.mult))
                    link(v.tensor_reduce(first[:, :], o, AX, ALU.min))
                    link(v.tensor_tensor(o, e_cols(first[:, :]), over_t(iota[:, 0, :]), ALU.is_equal))
                    if c == 0:
                        if K == 1:
                            v.tensor_tensor(ex[:, :, :], lg[:, :, :], e_cols(lmax[:, 0, :]), ALU.subtract).then_inc(shift_ok, 1)
                        else:
                            link(v.scalar_tensor_tensor(lg[:, :, :], o, LOWEST, lg[:, :, :], ALU.mult, ALU.add))
                if K == 2:
                    v.tensor_tensor(ex[:, :, 0], lmax[:, 1, :], lmax[:, 0, :], ALU.subtract).then_inc(shift_ok, 1)
                v.sem_inc(oh_ok, 1)
                cur, w, n = oh, 1, 0
                while w < V:
                    dst = pre[n % 2]
                    v.tensor_copy(dst[:, 0:w, :], cur[:, 0:w, :]).then_inc(dve, 1)
                    v.tensor_tensor(dst[:, w:V, :], cur[:, w:V, :], cur[:, 0:V - w, :], ALU.add).then_inc(dve, 1)
                    done[0] += 2
                    v.wait_ge(dve, done[0])
                    cur = dst
                    w *= 2
                    n += 1
                other = pre[n % 2]
                link(v.tensor_tensor(other[:, :, :], cur[:, :, :], oh[:, :, :], ALU.subtract))
                if other is not pre[1]:
                    link(v.tensor_copy(pre[1][:, :, :], other[:, :, :]))
                v.sem_inc(pre_ok, 1)
                v.wait_ge(ex_ok, 1)
                gate = keep.gate[:, gate_col:gate_col + 1]
                if K == 1:
                    link(v.reduce_sum(first[:, :], ex[:, :, :], AX))
                    link(v.reciprocal(first[:, :], first[:, :]))
                    v.tensor_scalar(prob[:, 0:T], first[:, :], gate, None, ALU.mult).then_inc(dve, 1)
                    done[0] += 1
                else:
                    link(v.tensor_scalar(first[:, :], ex[:, :, 0], 1.0, None, ALU.add))
                    link(v.reciprocal(first[:, :], first[:, :]))
                    link(v.tensor_scalar(prob[:, 0:T], first[:, :], gate, None, ALU.mult))
                    v.tensor_tensor(prob[:, T:2 * T], prob[:, 0:T], ex[:, :, 0], ALU.mult).then_inc(dve, 1)
                    done[0] += 1
                v.wait_ge(rank_ok, 2)
                link(v.tensor_scalar(cnt[:, :], cnt_bank[:, 0:E], float(P - 1), None, ALU.add))
                link(v.tensor_copy(cnti[:, :], cnt[:, :]))
                link(v.tensor_scalar(cnti[:, :], cnti[:, :], 7, None, ALU.arith_shift_right))
                link(v.tensor_copy(cnt[:, :], cnti[:, :]))
                cur, w, n = cnt, 1, 0
                while w < E:
                    dst = ends[n % 2]
                    v.tensor_copy(dst[:, 0:w], cur[:, 0:w]).then_inc(dve, 1)
                    v.tensor_tensor(dst[:, w:E], cur[:, w:E], cur[:, 0:E - w], ALU.add).then_inc(dve, 1)
                    done[0] += 2
                    v.wait_ge(dve, done[0])
                    cur, w, n = dst, 2 * w, n + 1
                tends = cur
                link(v.tensor_tensor(base[:, :], tends[:, :], cnt[:, :], ALU.subtract))
                link(v.tensor_scalar(base[:, :], base[:, :], float(P), None, ALU.mult))
                link(v.tensor_tensor(pre[0][:, :, :], rank_bank[:, 0:V * E].rearrange("p (v e) -> p v e", e=E), over_t(base[:, :], V), ALU.add))
                link(v.tensor_tensor(pre[0][:, :, :], pre[0][:, :, :], oh[:, :, :], ALU.mult))
                link(v.reduce_sum(slotf[:, :], pre[0][:, :, :], AX))
                v.tensor_copy(picks[:, :], slotf[:, :]).then_inc(pick_ok, 1)
                link(v.tensor_tensor(past[:, :, :], iota_t[:, :].unsqueeze(2).to_broadcast([P, NT, E]), over_t(tends[:, :], NT), ALU.is_ge))
                link(v.reduce_sum(tef[:, :], past[:, :, :], AX))
                link(v.tensor_scalar(tef[:, :], tef[:, :], float(E - 1), None, ALU.min))
                v.tensor_copy(tile_expert[:, :], tef[:, :]).then_inc(dve, 1)
                v.tensor_scalar(hot[:, :, :], tef[0:3 * E, :].unsqueeze(2).to_broadcast([3 * E, NT, P]), part[:, 3:4], None, ALU.is_equal).then_inc(dve, 1)
                v.wait_ge(dve, done[0] + 2)

        with ExitStack() as ectx:
            def eb(name, shape, dt=F32):
                return ectx.enter_context(nc.sbuf_tensor(f"{name}{tag}", shape, dt))

            def esem(name):
                return keep.sems.new(f"{name}{tag}")

            xb, xT = eb("slot_rows", [P, 2, D]), eb("slotT", [P, 2, KD, P])
            hid, hT = eb("hidden", [P, 2, F]), eb("hiddenT", [P, KF, P])
            ys = eb("y_rows", [P, 2, D])
            h_ps = [ectx.enter_context(nc.psum_tensor(f"h_ps{tag}{i}", [P, HB, 512], F32)) for i in range(2)]
            hT_ps = [ectx.enter_context(nc.psum_tensor(f"hT_ps{tag}{i}", [P, 512], F32)) for i in range(2)]
            x_ps = ectx.enter_context(nc.psum_tensor(f"x_ps{tag}", [P, 512], F32))
            y_ps = ectx.enter_context(nc.psum_tensor(f"y_ps{tag}", [P, 512], F32))
            ld = [esem(f"slot_rows_{i}") for i in range(2)]
            stored = [esem(f"y_stored_{i}") for i in range(2)]
            xT_ok, xTs_ok, h_ok, act_ok = esem("x_in_psum"), esem("slotT_ready"), esem("h_in_psum"), esem("hidden_ready")
            hT_ok, hTa_ok, hTd_ok, y_ok, ys_ok = (esem(n) for n in ("hT_in_psum", "hT_act_half", "hT_dve_half", "y_in_psum", "y_ready"))
            ALL = NT
            EVEN = NT - NT % 2
            LASTF = EVEN - 2 if EVEN == NT else EVEN - 1
            TPB = KF // 2

            side = StatePowers(nc, keep, rows) if K == 1 else None
            blk = ectx.enter_context(nc.Block())

            @blk.sync
            def _(sp):
                if side:
                    side.load(sp, io)

                def slot(t, at):
                    u = at % 2
                    if at >= 4:
                        sp.wait_ge(ys_ok, t - 3)
                        sp.dma_start(yslots[bass.ds(t * P - 4 * P, P), :], ys[:, u, :]).then_inc(stored[u], 16)
                    if at < ALL:
                        wait(sp, xT_ok, t - 1, at - 1)
                        sp.dma_start(xb[:, u, :], xslots[bass.ds(t * P, P), :]).then_inc(ld[u], 16)
                pipeline(sp, slot, 0, 4, EVEN, ALL + 3)
                sp.wait_ge(stored[0], 16 * ((ALL + 1) // 2))
                sp.wait_ge(stored[1], 16 * (ALL // 2))

            @blk.gpsimd
            def _(gp):
                if side:
                    side.powers(gp)

            @blk.scalar
            def _(act):
                def slot(t, at):
                    if at + 1 < ALL:
                        act.wait_ge(xT_ok, t + 2)
                        wait(act, h_ok, t, at)
                        nc.scalar.activation(xT[:, (at + 1) % 2, :, :], x_ps[:, 0:D].rearrange("p (k n) -> p k n", k=KD), ACT.Copy).then_inc(xTs_ok, 1)
                    if 1 <= at <= ALL:
                        act.wait_ge(hT_ok, t)
                        wait(act, y_ok, t - 1, at - 1)
                        nc.scalar.activation(hT[:, 0:TPB, :], hT_ps[0][:, 0:TPB * P].rearrange("p (k n) -> p k n", n=P), ACT.Copy).then_inc(hTa_ok, 1)
                    if 0 <= at < ALL:
                        act.wait_ge(h_ok, t + 1)
                        wait(act, hT_ok, t - 1, at - 1)
                        nc.scalar.activation(hid[:, at % 2, :], h_ps[at % 2][:, :, :].rearrange("p b n -> p (b n)"), act_fn).then_inc(act_ok, 1)
                pipeline(act, slot, -1, 3, LASTF, ALL)

            @blk.tensor
            def _(pe):
                if K == 1:
                    pe.wait_ge(keep.ld_w1, 16 * E)
                else:
                    pe.wait_ge(keep.ld_w1, 16 * 2 * E)
                    pe.wait_ge(keep.ld_w2, 16 * 2 * E)

                def expert(t):
                    return pe.value_load(tile_expert[0:1, bass.ds(t, 1)], min_val=0, max_val=E - 1)

                def slot(t, at):
                    if at + 1 < ALL:
                        u = (at + 1) % 2
                        pe.wait_ge(ld[u], ((t + 1) // 2 + 1) * 16)
                        wait(pe, xTs_ok, t + 1, at + 1)
                        for k in range(KD):
                            mm = nc.tensor.transpose(x_ps[:, k * P:(k + 1) * P], xb[:, u, k * P:(k + 1) * P], keep.ident[:, :])
                        mm.then_inc(xT_ok, 1)
                    if 1 <= at <= ALL:
                        u = (at - 1) % 2
                        pe.wait_ge(act_ok, t)
                        wait(pe, hTa_ok, t - 1, at - 1)
                        wait(pe, hTd_ok, t - 1, at - 1)
                        for k in range(KF):
                            mm = nc.tensor.transpose(hT_ps[k // TPB][:, (k % TPB) * P:(k % TPB + 1) * P], hid[:, u, k * P:(k + 1) * P], keep.ident[:, :])
                        mm.then_inc(hT_ok, 1)
                    if 0 <= at < ALL:
                        u = at % 2
                        e = expert(t)
                        pe.wait_ge(xTs_ok, t + 1)
                        wait(pe, act_ok, t - 1, at - 1)
                        for n in range(HB):
                            for k in range(KD):
                                nc.tensor.matmul(h_ps[u][:, n, :], xT[:, u, k, :], keep.w1[:, bass.ds(e, 1), k, n * 512:(n + 1) * 512].rearrange("p a n -> p (a n)"),
                                                 start=(k == 0), stop=False)
                            mm = nc.tensor.matmul(h_ps[u][:, n, :], hot[:, bass.ds(t, 1), :].rearrange("p a n -> p (a n)"), b1x[:, n * 512:(n + 1) * 512],
                                                  start=False, stop=True)
                        mm.then_inc(h_ok, 1)
                    if 1 <= at <= ALL:
                        e = expert(t - 1)
                        if at == 1 and K == 1:
                            pe.wait_ge(keep.ld_w2, 16 * E)
                        pe.wait_ge(hTa_ok, t)
                        pe.wait_ge(hTd_ok, t)
                        wait(pe, ys_ok, t - 1, at - 1)
                        for k in range(KF):
                            nc.tensor.matmul(y_ps[:, 0:D], hT[:, k, :], keep.w2[:, bass.ds(e, 1), k, :].rearrange("p a n -> p (a n)"),
                                             start=(k == 0), stop=False)
                        mm = nc.tensor.matmul(y_ps[:, 0:D], hot[:, bass.ds(t - 1, 1), :].rearrange("p a n -> p (a n)"), b2x[:, :], start=False, stop=True)
                        mm.then_inc(y_ok, 1)
                pipeline(pe, slot, -1, 3, LASTF, ALL)

            @blk.vector
            def _(v):
                if side:
                    side.inverse_square(v)

                def slot(t, at):
                    v.wait_ge(hT_ok, t + 1)
                    wait(v, y_ok, t, at)
                    v.tensor_copy(hT[:, TPB:KF, :], hT_ps[1][:, 0:TPB * P].rearrange("p (k n) -> p k n", n=P)).then_inc(hTd_ok, 1)
                    v.wait_ge(y_ok, t + 1)
                    if at >= 2:
                        v.wait_ge(stored[at % 2], (t // 2) * 16)
                    v.tensor_copy(ys[:, at % 2, :], y_ps[:, 0:D]).then_inc(ys_ok, 1)
                pipeline(v, slot, 0, 2, EVEN, ALL - 1)

        with ExitStack() as gctx:
            more = [gctx.enter_context(nc.sbuf_tensor(f"second{tag}", [P, T, D], F32))] if K == 2 else []
            got = [rows, *more]
            new = keep.sems.new
            gathered = [new(f"gathered{tag}_{c}") for c in range(V)]
            added, stat = new(f"added{tag}"), new(f"row_stats{tag}")
            blk = gctx.enter_context(nc.Block())

            @blk.gpsimd
            def _(gp):
                for t in range(T):
                    for c in range(K):
                        gp.indirect_dma_start(got[c][:, t, :], None, yslots,
                                              bass.IndirectOffsetOnAxis(ap=picks[:, c * T + t:c * T + t + 1], axis=0),
                                              bounds_check=NT * P - 1, oob_is_err=False).then_inc(gathered[c * T + t], 16)

            @blk.vector
            def _(v):
                for t in range(T):
                    for c in range(K):
                        v.wait_ge(gathered[c * T + t], 16)
                        wait(v, added, K * t + c, K * t + c if c else 0)
                        v.scalar_tensor_tensor(keep.x1[:, t, :], got[c][:, t, :], prob[:, c * T + t:c * T + t + 1], keep.x1[:, t, :],
                                               ALU.mult, ALU.add).then_inc(added, 1)
                    if K == 1:
                        v.wait_ge(added, t + 1)
                        v.bn_stats(keep.stats[:, t, :], keep.x1[:, t, :]).then_inc(stat, 1)


H1 = 4
DQ = 128
DH1 = DQ // H1
TOP = 32
MOVED = -3.0e38


class ConvKernel:

    CH, PART = 32, 8
    NB, NA = 32, S // 32
    SLOTS = P // 8

    def __init__(self, nc, io, keep, c, sb):
        CH, PART, NB, NA = self.CH, self.PART, self.NB, self.NA
        self.nc, self.keep, self.dram = nc, keep, c.kernel_dram
        self.low, self.high = sb("z_low", [P, 2, 2 * CH, NB]), sb("z_high", [P, 2, 2 * CH, NA])
        self.prod = [sb(f"z_products{i}", [P, 2, CH, NB // 2]) for i in range(2)]
        self.mov = [sb(f"z_low_part{i}", [P, 2, PART, NB]) for i in range(2)]
        self.sta = [sb(f"z_high_part{i}", [P, 3, PART, NA]) for i in range(2)]
        self.kout = [sb(f"k_out{i}", [NA, 2, PART, NB]) for i in range(2)]
        self.chain, self.tab_ok, self.staged, self.mm_ok = (keep.sems.new(n) for n in ("table_chain", "table_ready", "part_laid_out", "k_in_psum"))
        self.turn_ok = keep.sems.new("product_turns")
        self.out_ok = [keep.sems.new(f"k_half{h}_ready") for h in range(2)]
        self.stored = [keep.sems.new(f"k_stored{i}") for i in range(2)]

    def tables(self, gp):
        CH, NB, NA = self.CH, self.NB, self.NA
        n = 0
        for turn in range(P // CH):
            sl = slice(turn * CH, turn * CH + CH)
            at = (turn % 2) * CH
            low, high = self.low[:, :, at:at + CH, :], self.high[:, :, at:at + CH, :]

            def step(*ins):
                nonlocal n
                for y in ins:
                    y.then_inc(self.chain, 1)
                n += len(ins)
                gp.wait_ge(self.chain, n)

            def grow(tab, width, j0):
                x, j = 1, j0
                while x < width:
                    re, im = (self.keep.z[:, i, j, sl].unsqueeze(1).unsqueeze(3).to_broadcast([P, 2, CH, x]) for i in range(2))
                    by_re, by_im = (q[:, :, :, 0:x] for q in self.prod)
                    have = tab[:, :, :, 0:x]
                    step(gp.tensor_tensor(by_re, have, re, ALU.mult), gp.tensor_tensor(by_im, have, im, ALU.mult))
                    step(gp.tensor_tensor(tab[:, 0, :, x:2 * x], by_re[:, 0], by_im[:, 1], ALU.subtract),
                         gp.tensor_tensor(tab[:, 1, :, x:2 * x], by_re[:, 1], by_im[:, 0], ALU.add))
                    x, j = 2 * x, j + 1

            if turn >= 2:
                gp.wait_ge(self.staged, (turn - 1) * (CH // self.PART))
            step(gp.memset(low[:, 0, :, 0:1], 1.0), gp.memset(low[:, 1, :, 0:1], 0.0), gp.tensor_copy(high[:, :, :, 0], self.keep.dc[:, :, sl]))
            grow(low, NB, 0)
            grow(high, NA, 5)
            gp.sem_inc(self.tab_ok, 1)

    def stage(self, act, k, at):
        u = at % 2
        a = self.nc.scalar.activation
        ring = bass.ds((k % (2 * self.CH // self.PART)) * self.PART, self.PART)
        act.wait_ge(self.tab_ok, k // 4 + 1)
        wait(act, self.mm_ok, k * 2 - 2, at * 2 - 2)
        a(self.mov[u][:, :, :, :], self.low[:, :, ring, :], ACT.Copy)
        a(self.sta[u][:, 0:2, :, :], self.high[:, :, ring, :], ACT.Copy)
        a(self.sta[u][:, 2, :, :], self.high[:, 1, ring, :], ACT.Copy, scale=-1.0).then_inc(self.staged, 1)

    def product(self, pe, k, at, h):
        u = at % 2
        q = slice(64 * h, 64 * h + 64)
        pe.wait_ge(self.staged, k + 1)
        wait(pe, self.out_ok[h], k, at)
        pe.sem_inc(self.turn_ok, 1)
        for d in range(self.PART):
            o = self.banks[h][0:self.NA, D + d * self.NB:D + (d + 1) * self.NB]
            self.nc.tensor.matmul(o, self.sta[u][q, 0, d, :], self.mov[u][q, 0, d, :], start=True, stop=False)
            mm = self.nc.tensor.matmul(o, self.sta[u][q, 2, d, :], self.mov[u][q, 1, d, :], start=False, stop=True)
        mm.then_inc(self.mm_ok, 1)

    def wait_evacuated(self, eng, k, at, h):
        eng.wait_ge(self.out_ok[h], k + 1)

    def evacuate(self, act, k, at, h):
        u = at % 2
        act.wait_ge(self.mm_ok, k * 2 + (h + 1))
        if at >= 2:
            act.wait_ge(self.stored[u], (k // 2) * 32)
        self.nc.scalar.activation(self.kout[u][:, h, :, :], self.banks[h][0:self.NA, D:2 * D].rearrange("p (d b) -> p d b", d=self.PART),
                                  ACT.Copy).then_inc(self.out_ok[h], 1)

    def store(self, sp):
        def slot(k, at):
            for h in range(2):
                sp.wait_ge(self.out_ok[h], k + 1)
                sp.dma_start(self.dram[bass.ds(k * self.PART + h * P, self.PART), :].rearrange("d (a b) -> a d b", a=self.NA),
                             self.kout[at % 2][:, h, :, :]).then_inc(self.stored[at % 2], 16)
        pipeline(sp, slot, 0, 2, self.SLOTS, self.SLOTS - 1)
        for u in range(2):
            sp.wait_ge(self.stored[u], 16 * self.SLOTS)


def layer1_attention(nc, io, keep, c):
    with ExitStack() as ctx:
        def sb(name, shape, dt=F32):
            return ctx.enter_context(nc.sbuf_tensor(name, shape, dt))

        def bank(name):
            return ctx.enter_context(nc.psum_tensor(name, [P, 512], F32))

        sem = keep.sems.new

        NF = 4 * D
        ctxT = sb("ctxT1", [KC, 2, B * SK])
        wq, wk, wv = sb("wq1", [P, KD, DQ]), sb("wk1", [KC, 2, DQ]), sb("wv1", [KC, 2, D])
        wf = sb("w_film", [P, KD, NF])
        mask4 = sb("headmask32", [P, H1])
        kbd = sb("k1_blockdiag", [P, B, H1, SK])
        vT = sb("v1T", [P, KD, B * SK])
        vw = sb("v_film", [SK + 1, B, NF])
        modg = sb("mod_gate", [P, 1])
        g_in, b_in = sb("g_norm_in", [P, D]), sb("b_norm_in", [P, D])
        key_u8, key_bias = sb("key_mask_u8", [P, B * SK], U8), sb("key_bias", [P, B, SK])
        tok_u8, tok = sb("token_mask_u8", [P, T], U8), sb("token_mask", [P, T])
        tmp, mean, rstd, rstd2 = sb("tmp_c", [P, 4, T]), sb("mean_c", [P, T]), sb("rstd_c", [P, T]), sb("rstd2_c", [P, T])
        xs, xsT, qT = sb("xs_c", [P, 2, D]), sb("xsT_c", [P, KD, P]), sb("qT_c", [P, P])
        s, work = sb("s_c", [P, 2, H1, SK]), sb("work_c", [P, 2, H1, SK])
        best, neg = sb("best8", [P, 2, H1, 8]), sb("minus_max", [P, 2, H1])
        later = sb("later8", [P, H1, 8])
        e = sb("e_c", [P, 2, H1, SK])
        den, rden = sb("den_c", [P, H1]), sb("rden_c", [P, 2, H1])
        am, aT = sb("attn_mean", [P, P]), sb("attn_meanT", [SK + 1, P])
        xl = sb("xl_c", [P, D])
        vw_b = sb("film_offset", [SK + 1, B, D])
        ssm = ConvKernel(nc, io, keep, c, sb)
        s_ps = [bank(f"s1_{i}") for i in range(2)]
        m0, m1 = bank("c_m0"), bank("c_m1")
        f_ps = [ctx.enter_context(nc.psum_tensor(f"film_ps{i}", [P, 2, 512], F32)) for i in range(2)]

        ld = sem("ld_c")
        dve, pool, mm_ok = sem("dve_c"), sem("pool_c"), sem("setup_c")
        var_ok, std_ok, var2_ok, std2_ok = sem("var_c"), sem("std_c"), sem("var2_c"), sem("std2_c")
        kbd_ok, vT_ok, vw_ok = sem("kbd_c"), sem("vT_c"), sem("vw_c")
        xs_ok, rows_ok, xT_ok, xTs_ok, q_ok, qT_ok, s_ok, ssb_ok = (sem(n + "_c1") for n in ("xs", "rows", "xT", "xTs", "q", "qT", "s", "ssb"))
        best_ok, neg_ok, e_ok, em_ok, den_ok, inv_ok, rden_ok, er_ok, am_ok = (sem(n + "_c1") for n in ("best", "neg", "e", "em", "den", "inv", "rden", "er", "am"))
        aT_ok, aTs_ok, f_ok, fo_ok, xg_ok, xm_ok = (sem(n + "_c1") for n in ("aT", "aTs", "film", "film_out", "xg", "xm"))

        gate_ok = sem("top_steps")
        ssm.banks = (m0, m1)
        KS = ssm.SLOTS
        blk = ctx.enter_context(nc.Block())

        @blk.sync
        def _(sp):
            for dst, src in ((ctxT[:, :, :], io["ctxT"].rearrange("(k c) n -> c k n", k=2)),
                             (wk[:, :, :], io["wk1"].rearrange("(k c) n -> c k n", k=2)),
                             (wv[:, :, :], io["wv1"].rearrange("(k c) n -> c k n", k=2)),
                             (wf[:, :, 0:2 * D], io["w_film_in"].rearrange("(k c) n -> c k n", k=KD)),
                             (wf[:, :, 2 * D:NF], io["w_film_out"].rearrange("(k c) n -> c k n", k=KD)),
                             (wq[:, :, :], io["wq1"].rearrange("(k c) n -> c k n", k=KD)),
                             (vw[SK:SK + 1, 0, 0:2 * D], io["b_film_in"].unsqueeze(0)),
                             (vw[SK:SK + 1, 0, 2 * D:NF], io["b_film_out"].unsqueeze(0)),
                             (mask4[:, :], io["headmask32"]),
                             (modg[:, :], io["mod_gate"].partition_broadcast(P)),
                             (g_in[:, :], io["g_norm_in"].partition_broadcast(P)),
                             (b_in[:, :], io["b_norm_in"].partition_broadcast(P)),
                             (key_u8[:, :], io["key_mask"].partition_broadcast(P)),
                             (tok_u8[:, :], io["token_mask"])):
                sp.dma_start(dst, src).then_inc(ld, 16)
            ssm.store(sp)

        LOADS = 16 * 14

        @blk.gpsimd
        def _(gp):
            ssm.tables(gp)

        @blk.scalar
        def _(act):
            act.wait_ge(var_ok, 1)
            nc.scalar.activation(rstd[:, :], tmp[:, 0, :], ACT.Sqrt).then_inc(std_ok, 1)
            act.wait_ge(var2_ok, 1)
            nc.scalar.activation(rstd2[:, :], tmp[:, 1, :], ACT.Sqrt).then_inc(std2_ok, 1)

            def slot(t, at):
                if 0 <= at - 1 < KS:
                    ssm.stage(act, t - 1, at - 1)
                if 0 <= at + 1 < T:
                    act.wait_ge(xT_ok, t + 2)
                    wait(act, q_ok, t + 1, at + 1)
                    nc.scalar.activation(xsT[:, :, :], m0[:, 0:D].rearrange("p (k n) -> p k n", k=KD), ACT.Copy).then_inc(xTs_ok, 1)
                if 0 <= at - 2 < KS:
                    ssm.evacuate(act, t - 2, at - 2, 0)
                if 0 <= at - 2 < T:
                    act.wait_ge(aT_ok, t - 1)
                    wait(act, f_ok, t - 2, at - 2)
                    nc.scalar.activation(aT[0:SK, :], m1[0:SK, 0:P], ACT.Copy).then_inc(aTs_ok, 1)
                if 0 <= at - 2 < KS:
                    ssm.evacuate(act, t - 2, at - 2, 1)
                if 0 <= at + 1 < T:
                    act.wait_ge(q_ok, t + 2)
                    wait(act, s_ok, t + 1, at + 1)
                    nc.scalar.activation(qT[:, :], m0[:, 0:P], ACT.Copy).then_inc(qT_ok, 1)
                if 0 <= at < T:
                    u = at % 2
                    act.wait_ge(neg_ok, t + 1)
                    wait(act, er_ok, t - 1, at - 1)
                    wait(act, am_ok, t - 1, at - 1)
                    for h in range(H1):
                        x = nc.scalar.activation(e[:, u, h, :], s[:, u, h, :], ACT.Exp, bias=neg[:, u, h:h + 1])
                    x.then_inc(e_ok, 1)
                if 0 <= at - 2 < T:
                    act.wait_ge(f_ok, t - 1)
                    nc.scalar.activation(row(c.film, t - 2), f_ps[at % 2][:, 1, :], ACT.Copy).then_inc(fo_ok, 1)
            pipeline(act, slot, -1, 5, T - 1, T + 2)

        @blk.tensor
        def _(pe):
            pe.wait_ge(ld, LOADS)
            for k in range(2):
                mm = nc.tensor.matmul(s_ps[0][:, 0:B * SK], wk[:, k, :], ctxT[:, k, :], start=(k == 0), stop=(k == 1))
            mm.then_inc(mm_ok, 1)
            for m in range(KD):
                for k in range(2):
                    mm = nc.tensor.matmul((m0, m1)[m][:, 0:B * SK], wv[:, k, m * P:(m + 1) * P], ctxT[:, k, :], start=(k == 0), stop=(k == 1))
                mm.then_inc(mm_ok, 1)
            pe.wait_ge(vT_ok, 2)
            for b in range(B):
                wait(pe, vw_ok, 2 * (b - 1), 2 * (b - 1))
                for n in range(2):
                    for k in range(KD):
                        mm = nc.tensor.matmul(f_ps[b % 2][0:SK, n, :], vT[:, k, b * SK:(b + 1) * SK], wf[:, k, n * 512:(n + 1) * 512],
                                              start=(k == 0), stop=(k == KD - 1))
                    mm.then_inc(mm_ok, 1)
            pe.wait_ge(vw_ok, 2 * B + 3)
            pe.wait_ge(kbd_ok, B)

            def slot(t, at):
                if 0 <= at - 2 < KS:
                    wait(pe, qT_ok, t + 1 if at < T else T, at + 1)
                    ssm.product(pe, t - 2, at - 2, 0)
                if 0 <= at + 1 < T:
                    u = (at + 1) % 2
                    pe.wait_ge(xs_ok, t + 2)
                    wait(pe, qT_ok, t + 1, at + 1)
                    for k in range(KD):
                        mm = nc.tensor.transpose(m0[:, k * P:(k + 1) * P], xs[:, u, k * P:(k + 1) * P], keep.ident[:, :])
                    mm.then_inc(xT_ok, 1)
                if 0 <= at - 2 < KS:
                    wait(pe, aTs_ok, t - 2, at - 2)
                    ssm.product(pe, t - 2, at - 2, 1)
                if 0 <= at - 2 < T:
                    pe.wait_ge(am_ok, t - 1)
                    wait(pe, aTs_ok, t - 2, at - 2)
                    nc.tensor.transpose(m1[:, 0:P], am[:, :], keep.ident[:, :]).then_inc(aT_ok, 1)
                if 0 <= at + 1 < T:
                    pe.wait_ge(xTs_ok, t + 2)
                    if 0 <= at - 2 < KS:
                        ssm.wait_evacuated(pe, t - 2, at - 2, 0)
                    for k in range(KD):
                        mm = nc.tensor.matmul(m0[:, 0:P], wq[:, k, :], xsT[:, k, :], start=(k == 0), stop=(k == KD - 1))
                    mm.then_inc(q_ok, 1)
                if 0 <= at - 2 < T:
                    pe.wait_ge(aTs_ok, t - 1)
                    wait(pe, fo_ok, t - 3, at - 3)
                    wait(pe, xm_ok, t - 3, at - 3)
                    for n in range(2):
                        mm = nc.tensor.matmul(f_ps[at % 2][:, n, :], aT[:, :], vw[:, bass.ds((t - 2) // TB, 1), n * 512:(n + 1) * 512].rearrange("p a n -> p (a n)"),
                                              start=True, stop=True)
                    mm.then_inc(f_ok, 1)
                if 0 <= at + 1 < T:
                    pe.wait_ge(qT_ok, t + 2)
                    wait(pe, ssb_ok, t, at)
                    nc.tensor.matmul(s_ps[(at + 1) % 2][:, 0:H1 * SK], qT[:, :], kbd[:, bass.ds((t + 1) // TB, 1), :, :].rearrange("p a h s -> p (a h s)"),
                                     start=True, stop=True).then_inc(s_ok, 1)
            pipeline(pe, slot, -1, 5, T - 1, T + 2)

        @blk.vector
        def _(v):
            done = [0]

            def link(ins):
                done[0] += 1
                ins.then_inc(dve, 1)
                v.wait_ge(dve, done[0])

            done[0] = norm_from_stats(v, 0, dve, keep.stats, tmp, mean, rstd)
            v.wait_ge(dve, done[0])
            v.sem_inc(var_ok, 1)
            v.wait_ge(std_ok, 1)
            link(v.reciprocal(rstd[:, :], rstd[:, :]))
            link(v.tensor_tensor(tmp[:, 1, :], rstd[:, :], rstd[:, :], ALU.mult))
            link(v.tensor_scalar(tmp[:, 1, :], tmp[:, 1, :], -EPS, 1.0 + EPS, ALU.mult, ALU.add))
            v.sem_inc(var2_ok, 1)
            v.wait_ge(ld, LOADS)
            v.wait_ge(std2_ok, 1)
            link(v.reciprocal(rstd2[:, :], rstd2[:, :]))
            link(v.tensor_copy(key_bias[:, :, :].rearrange("p b s -> p (b s)"), key_u8[:, :]))
            link(v.tensor_scalar(key_bias[:, :, :], key_bias[:, :, :], 1.0, 3.0e38, ALU.subtract, ALU.mult))
            link(v.tensor_scalar(key_bias[:, :, :], key_bias[:, :, :], 10.0, None, ALU.mult))
            link(v.tensor_copy(tok[:, :], tok_u8[:, :]))
            link(v.tensor_scalar(tok[:, :], tok[:, :], 1.0 / H1, None, ALU.mult))
            v.wait_ge(mm_ok, 1)
            link(v.tensor_copy(vT[:, 0, :], s_ps[0][:, 0:B * SK]))
            for b in range(B):
                v.tensor_tensor(kbd[:, b, :, :], vT[:, 0, b * SK:(b + 1) * SK].unsqueeze(1).to_broadcast([P, H1, SK]),
                                mask4[:, :].unsqueeze(2).to_broadcast([P, H1, SK]), ALU.mult).then_inc(kbd_ok, 1)
            v.wait_ge(kbd_ok, B)
            for m in range(KD):
                v.wait_ge(mm_ok, 2 + m)
                v.tensor_copy(vT[:, m, :], (m0, m1)[m][:, 0:B * SK]).then_inc(vT_ok, 1)
            for n in range(4):
                v.tensor_scalar(vw[SK:SK + 1, 0, n * D:(n + 1) * D], vw[SK:SK + 1, 0, n * D:(n + 1) * D], modg[SK:SK + 1, 0:1],
                                1.0 - n % 2, ALU.mult, ALU.add).then_inc(dve, 1)
            done[0] += 4
            v.wait_ge(dve, done[0])
            for b in range(1, B):
                v.tensor_copy(vw[SK:SK + 1, b, :], vw[SK:SK + 1, 0, :]).then_inc(dve, 1)
            v.memset(aT[SK:SK + 1, :], 1.0).then_inc(dve, 1)
            v.memset(am[:, SK:P], 0.0).then_inc(dve, 1)
            done[0] += B + 1
            for b in range(B):
                for n in range(2):
                    v.wait_ge(mm_ok, 3 + 2 * b + n + 1)
                    v.tensor_scalar(vw[0:SK, b, n * 512:(n + 1) * 512], f_ps[b % 2][0:SK, n, :], modg[0:SK, 0:1], None, ALU.mult).then_inc(vw_ok, 1)
            v.wait_ge(dve, done[0])
            v.wait_ge(vw_ok, 2 * B)
            def g_rows(a):
                return a[0:SK + 1, :].unsqueeze(1).to_broadcast([SK + 1, B, D])
            link(v.tensor_tensor(vw_b[:, :, :], vw[:, :, 0:D], g_rows(b_in), ALU.mult))
            link(v.tensor_tensor(vw[:, :, D:2 * D], vw[:, :, D:2 * D], vw_b[:, :, :], ALU.add))
            link(v.tensor_tensor(vw[:, :, 0:D], vw[:, :, 0:D], g_rows(g_in), ALU.mult))
            v.sem_inc(vw_ok, 3)
            D0 = done[0]
            PER = 7

            def slot(t, at):
                if 0 <= at + 1 < T:
                    wait(v, xT_ok, t, at)
                    v.tensor_scalar(xs[:, (at + 1) % 2, :], row(keep.x1, t + 1), mean[:, bass.ds(t + 1, 1)], rstd[:, bass.ds(t + 1, 1)], ALU.subtract, ALU.mult).then_inc(xs_ok, 1)
                    v.tensor_scalar(row(c.rows, t + 1), row(keep.x1, t + 1), mean[:, bass.ds(t + 1, 1)], rstd[:, bass.ds(t + 1, 1)], ALU.subtract, ALU.mult).then_inc(rows_ok, 1)

                p = (at - 1) % 2
                prev, mod = 0 <= at - 1 < T, 0 <= at - 3 < T
                film = f_ps[(at - 3) % 2]

                def taken():
                    v.wait_ge(e_ok, t)
                    v.scalar_tensor_tensor(e[:, p, :, :], work[:, p, :, :], MOVED, e[:, p, :, :], ALU.is_equal, ALU.mult).then_inc(em_ok, 1)

                def sums():
                    v.wait_ge(em_ok, t)
                    v.reduce_sum(den[:, :], e[:, p, :, :], AX).then_inc(den_ok, 1)

                def inverses():
                    v.wait_ge(den_ok, t)
                    v.reciprocal(rden[:, 0, :], den[:, :]).then_inc(inv_ok, 1)

                def mean_weights():
                    v.wait_ge(inv_ok, t)
                    v.tensor_scalar(rden[:, 1, :], rden[:, 0, :], tok[:, bass.ds(t - 1, 1)], None, ALU.mult).then_inc(rden_ok, 1)

                def weigh():
                    v.wait_ge(rden_ok, t)
                    v.tensor_tensor(e[:, p, :, :], e[:, p, :, :], rden[:, 1, :].unsqueeze(2).to_broadcast([P, H1, SK]), ALU.mult).then_inc(er_ok, 1)

                def head_mean():
                    v.wait_ge(er_ok, t)
                    wait(v, aT_ok, t - 1, at - 1)
                    v.reduce_sum(am[:, 0:SK], e[:, p, :, :].rearrange("p h s -> p s h"), AX).then_inc(am_ok, 1)

                def modulate():
                    v.wait_ge(f_ok, t - 2)
                    v.wait_ge(fo_ok, t - 2)
                    wait(v, xm_ok, t - 3, at - 3)
                    v.scalar_tensor_tensor(xl[:, :], row(c.rows, t - 3), rstd2[:, bass.ds(t - 3, 1)], film[:, 0, 0:D], ALU.mult, ALU.mult).then_inc(xg_ok, 1)

                def shift():
                    v.wait_ge(xg_ok, t - 2)
                    v.tensor_tensor(row(c.xm, t - 3), xl[:, :], film[:, 0, D:2 * D], ALU.add).then_inc(xm_ok, 1)

                fill = [(prev, taken), (mod, modulate), (prev, sums), (mod, shift), (prev, inverses), (prev, mean_weights), (prev, weigh), (prev, head_mean)]
                fill = [f if there else None for there, f in fill]

                def next_fill():
                    f = fill.pop(0)
                    if f:
                        f()

                if 0 <= at < T:
                    u = at % 2
                    v.wait_ge(s_ok, t + 1)
                    v.scalar_tensor_tensor(s[:, u, :, :], s_ps[u][:, 0:H1 * SK].rearrange("p (h s) -> p h s", h=H1), 1.0 / DH1 ** 0.5,
                                           key_bias[:, bass.ds(t // TB, 1), :].to_broadcast([P, H1, SK]), ALU.mult, ALU.add).then_inc(ssb_ok, 1)
                    v.wait_ge(ssb_ok, t + 1)
                    v.sem_inc(gate_ok, 1)
                    for r in range(TOP // 8):
                        src = s if r == 0 else work
                        for h in range(H1):
                            mx = best[:, u, h, :] if r == 0 else later[:, h, :]
                            ins = v.max(mx, src[:, u, h, :])
                        if r == 0:
                            ins.then_inc(best_ok, 1)
                            next_fill()
                            v.wait_ge(best_ok, t + 1)
                            v.tensor_scalar(neg[:, u, :], best[:, u, :, 0], -1.0, None, ALU.mult).then_inc(neg_ok, 1)
                        else:
                            ins.then_inc(dve, 1)
                            next_fill()
                            v.wait_ge(dve, t * PER + (D0 + 2 * r))
                            v.sem_inc(gate_ok, 1)
                        for h in range(H1):
                            mx = best[:, u, h, :] if r == 0 else later[:, h, :]
                            ins = v.match_replace(work[:, u, h, :], mx, src[:, u, h, :], MOVED)
                        ins.then_inc(dve, 1)
                        next_fill()
                        v.wait_ge(dve, t * PER + (D0 + 2 * r + 1))
                        v.sem_inc(gate_ok, 1)
                while fill:
                    next_fill()
            pipeline(v, slot, -1, 5, T - 1, T + 2)
            v.wait_ge(xm_ok, T)


class StatePowers:

    N = 64
    DL = P

    def __init__(self, nc, keep, rows):
        room = [rows[:, i // 2, (i % 2) * P:(i % 2) * P + P] for i in range(17)]
        self.ar, self.ai, self.cr, self.ci, self.dt = room[0:5]
        self.t = room[5:11]
        self.ki, self.inv = room[11].bitcast(I32), room[12]
        self.ur, self.ui, self.pr, self.pi = room[13:17]
        self.keep = keep
        self.ld, self.chain, self.inv_ok, self.inv_steps = (keep.sems.new(n) for n in ("ld_state", "state_chain", "inverse_ready", "inverse_steps"))

    def load(self, sp, io):
        for h in range(2):
            q = slice(self.N * h, self.N * h + self.N)
            for buf, name in ((self.ar, "a_reT"), (self.ai, "a_imT"), (self.cr, "c_reT"), (self.ci, "c_imT")):
                sp.dma_start(buf[q], io[name][:, h * self.DL:(h + 1) * self.DL]).then_inc(self.ld, 16)
            sp.dma_start(self.dt[q], io["log_dt"][h * self.DL:(h + 1) * self.DL].partition_broadcast(self.N)).then_inc(self.ld, 16)

    def inverse_square(self, v):
        sq = self.t[5]
        v.wait_ge(self.ld, 160)
        v.tensor_tensor(self.inv, self.ar, self.ar, ALU.mult).then_inc(self.inv_steps, 1)
        v.tensor_tensor(sq, self.ai, self.ai, ALU.mult).then_inc(self.inv_steps, 1)
        v.wait_ge(self.inv_steps, 2)
        v.tensor_tensor(sq, self.inv, sq, ALU.add).then_inc(self.inv_steps, 1)
        v.wait_ge(self.inv_steps, 3)
        v.reciprocal(self.inv, sq).then_inc(self.inv_ok, 1)

    def powers(self, gp):
        n = 0

        def link(*ins):
            nonlocal n
            for x in ins:
                x.then_inc(self.chain, 1)
            n += len(ins)
            gp.wait_ge(self.chain, n)

        def tt(o, a, b, op):
            return gp.tensor_tensor(o, a, b, op)

        def ts(o, a, s0, s1, op0, op1=None):
            return gp.tensor_scalar(o, a, s0, s1, op0, *([op1] if op1 else []))

        gp.wait_ge(self.ld, 160)
        gp.wait_ge(self.inv_ok, 1)
        keep, x = self.keep, self.dt
        k, r, q, f = self.t[0:4]
        MAGIC = 12582912.0
        link(ts(k, x, 1.4426950408889634, MAGIC, ALU.mult, ALU.add))
        link(ts(k, k, MAGIC, None, ALU.subtract))
        for part in (-0.693359375, 2.12194440e-4):
            link(ts(f, k, part, None, ALU.mult))
            link(tt(x if part < 0 else r, x, f, ALU.add))
        link(ts(q, r, 1.0 / 5040, None, ALU.mult))
        for co in (1 / 720, 1 / 120, 1 / 24, 1 / 6, 0.5, 1.0):
            link(ts(q, q, co, None, ALU.add))
            link(tt(q, q, r, ALU.mult))
        link(ts(f, k, 127.0, 8388608.0, ALU.add, ALU.mult), ts(q, q, 1.0, None, ALU.add))
        link(gp.tensor_copy(self.ki, f))
        link(tt(x, q, self.ki.bitcast(F32), ALU.mult))
        wr, wi = self.t[4], self.t[5]
        link(tt(wr, x, self.ar, ALU.mult), tt(wi, x, self.ai, ALU.mult))
        link(ts(k, wi, 0.15915494309189535, MAGIC, ALU.mult, ALU.add))
        link(ts(k, k, MAGIC, None, ALU.subtract))
        for part in (6.28125, 1.93500518798828125e-3, 3.01991598196e-7):
            link(ts(f, k, part, None, ALU.mult))
            link(tt(wi, wi, f, ALU.subtract))
        ur, ui, pr, pi = self.ur, self.ui, self.pr, self.pi
        a, b, c, d = self.t[0:4]
        link(ts(ur, wr, 1 / 256, None, ALU.mult), ts(ui, wi, 1 / 256, None, ALU.mult))
        link(ts(pr, ur, 0.2, None, ALU.mult), ts(pi, ui, 0.2, None, ALU.mult))
        for co in (1 / 4, 1 / 3, 1 / 2, 1.0):
            link(ts(pr, pr, 1.0, None, ALU.add), tt(b, pi, ui, ALU.mult), tt(d, pi, ur, ALU.mult))
            link(tt(a, pr, ur, ALU.mult), tt(c, pr, ui, ALU.mult))
            link(tt(pr, a, b, ALU.subtract), tt(pi, c, d, ALU.add))
            if co != 1.0:
                link(ts(pr, pr, co, None, ALU.mult), ts(pi, pi, co, None, ALU.mult))

        def double():
            link(ts(a, pr, 2.0, None, ALU.add), ts(c, pr, 1.0, 2.0, ALU.add, ALU.mult), tt(b, pi, pi, ALU.mult))
            link(tt(a, a, pr, ALU.mult), tt(pi, c, pi, ALU.mult))
            link(tt(pr, a, b, ALU.subtract))

        for _ in range(8):
            double()
        link(tt(a, self.cr, pr, ALU.mult), tt(b, self.ci, pi, ALU.mult), tt(c, self.cr, pi, ALU.mult), tt(d, self.ci, pr, ALU.mult))
        link(tt(ur, a, b, ALU.subtract), tt(ui, c, d, ALU.add))
        link(tt(a, ur, self.ar, ALU.mult), tt(b, ui, self.ai, ALU.mult), tt(c, ui, self.ar, ALU.mult), tt(d, ur, self.ai, ALU.mult))
        link(tt(ur, a, b, ALU.add), tt(ui, c, d, ALU.subtract), ts(self.inv, self.inv, 2.0, None, ALU.mult))
        link(tt(keep.dc[:, 0, :], ur, self.inv, ALU.mult), tt(keep.dc[:, 1, :], ui, self.inv, ALU.mult))
        for j in range(9):
            link(ts(keep.z[:, 0, j, :], pr, 1.0, None, ALU.add), gp.tensor_copy(keep.z[:, 1, j, :], pi))
            if j < 8:
                double()


W = S // 2
X_TILES = (0, 1, 2, 3)
K_TILES = (0, 1, 4, 3, 5, 1)


def kernel_transform(nc, io, keep, c):
    with ExitStack() as ctx:
        k_rows = ctx.enter_context(nc.sbuf_tensor("k_rows", [P, 2, S], F32))
        kT = ctx.enter_context(nc.sbuf_tensor("k_T", [P, 4, D], F32))
        t_ps = ctx.enter_context(nc.psum_tensor("kt_ps", [P, 2, 512], F32))
        f_ps = ctx.enter_context(nc.psum_tensor("kf_ps", [P, 6, 512], F32))
        sem = keep.sems.new
        ld, tr, ev, mm = (sem(n) for n in ("ld_kt", "kT_in_psum", "kT_ready", "kf_in_psum"))
        blk = ctx.enter_context(nc.Block())

        @blk.sync
        def _(sp):
            sp.dma_start(k_rows[:, :, :], c.kernel_dram.rearrange("(h p) l -> p h l", p=P)).then_inc(ld, 16)
            sp.dma_start(c.fwd[:, :, :], io["dft"].rearrange("(k p) f -> p k f", k=2)).then_inc(ld, 16)
            sp.dma_start(c.inv[:, :, :], io["idft"].rearrange("(k p) t -> p k t", p=P)).then_inc(ld, 16)
            sp.dma_start(c.sign[:, :], io["sign"]).then_inc(ld, 16)
            sp.dma_start(c.dskip[:, :], io["d_skip"].partition_broadcast(P)).then_inc(ld, 16)

        @blk.tensor
        def _(pe):
            pe.wait_ge(ld, 80)
            for lc in range(4):
                for h in range(2):
                    x = nc.tensor.transpose(t_ps[:, lc // 2, (lc % 2) * D + h * P:(lc % 2) * D + h * P + P], k_rows[:, h, lc * P:(lc + 1) * P], keep.ident[:, :])
                if lc % 2:
                    x.then_inc(tr, 1)
            pe.wait_ge(ev, 2)
            kv = kT[:, :, :].rearrange("p (w k) d -> p w k d", k=2)
            for j, f in enumerate(K_TILES):
                for k in range(2):
                    x = nc.tensor.matmul(f_ps[:, j, :], c.fwd[:, k, f * P:(f + 1) * P], kv[:, :, k, :], start=(k == 0), stop=(k == 1))
                x.then_inc(mm, 1)

        @blk.vector
        def _(v):
            for i in range(2):
                v.wait_ge(tr, i + 1)
                v.tensor_copy(kT[:, 2 * i:2 * i + 2, :], t_ps[:, i, :].rearrange("p (a d) -> p a d", a=2)).then_inc(ev, 1)
            for j in range(6):
                v.wait_ge(mm, j + 1)
                v.tensor_copy(c.kf[:, j, :, :], f_ps[:, j, :].rearrange("p (w d) -> p w d", w=2)).then_inc(ev, 1)
            v.wait_ge(ev, 8)


def convolution(nc, io, keep, c):
    with ExitStack() as ctx:
        def sb(name, shape, dt=F32):
            return ctx.enter_context(nc.sbuf_tensor(name, shape, dt))

        sem = keep.sems.new

        xz = sb("x_hat", [P, 4, 2, D])
        yh = sb("y_hat", [P, 4, 2, D])
        t = [sb(f"prod{i}", [P, 2, 2, D]) for i in range(4)]
        xf_ps = ctx.enter_context(nc.psum_tensor("xf_ps", [P, 4, 512], F32))
        y_ps = [ctx.enter_context(nc.psum_tensor(f"yt_ps{i}", [P, 512], F32)) for i in range(2)]
        fwd_ok, x0_ok, xz_ok, prod, ppool, yh_ok = (sem(n) for n in ("fwd_done", "x0_ready", "xz_ready", "dve_products", "pool_products", "yhat_ready"))
        inv_ok, y_ok, skip_ok, base_ok, st_ok = (sem(n) for n in ("inv_done", "y_added", "skip_ready", "base_ready", "stats_conv"))
        blk = ctx.enter_context(nc.Block())

        def win(buf, b, k):
            return buf[:, :, :].rearrange("p (b q k) d -> p b q k d", b=B, q=2)[:, b, :, k, :]

        UA = c.kf[:, 0:2, 0, :].unsqueeze(2).to_broadcast([P, 2, 2, D])
        UB = c.kf[:, 2:4, 0, :].unsqueeze(2).to_broadcast([P, 2, 2, D])
        UD = c.kf[:, 4:6, 0, :].unsqueeze(2).to_broadcast([P, 2, 2, D])
        VA, VB, VD = (c.kf[:, j:j + 2, 1, :] for j in (0, 2, 4))

        @blk.tensor
        def _(pe):
            for b in range(B + 1):
                if b < B:
                    for j, f in enumerate(X_TILES):
                        wait(pe, xz_ok, b, b)
                        for k in range(2):
                            x = nc.tensor.matmul(xf_ps[:, j, :], c.fwd[:, k, f * P:(f + 1) * P], win(c.xm, b, k), start=(k == 0), stop=(k == 1))
                    x.then_inc(fwd_ok, 1)
                if b >= 1:
                    pe.wait_ge(yh_ok, b)
                    for k in range(2):
                        wait(pe, y_ok, 2 * (b - 2) + k + 1, 2 * (b - 2) + k + 1)
                        for j in range(4):
                            x = nc.tensor.matmul(y_ps[k][:, :], c.inv[:, j, k * P:(k + 1) * P], yh[:, j, :, :].rearrange("p q d -> p (q d)"),
                                                 start=(j == 0), stop=(j == 3))
                        x.then_inc(inv_ok, 1)

        @blk.scalar
        def _(act):
            for b in range(B):
                act.wait_ge(fwd_ok, b + 1)
                wait(act, yh_ok, b, b)
                nc.scalar.activation(xz[:, :, 0, :], xf_ps[:, :, 0:D], ACT.Copy).then_inc(x0_ok, 1)

        @blk.gpsimd
        def _(gp):
            n = 0
            for b in range(B):
                xr, xi = xz[:, 0:2, :, :], xz[:, 2:4, :, :]
                gp.wait_ge(xz_ok, b + 1)
                wait(gp, yh_ok, b, b)
                gp.tensor_tensor(t[2][:, :, :, :], xr, UB, ALU.mult).then_inc(ppool, 1)
                gp.tensor_tensor(t[3][:, :, :, :], xi, UD, ALU.mult).then_inc(ppool, 1)
                gp.wait_ge(fwd_ok, b + 1)
                for k in range(2):
                    xm, rows = win(c.xm, b, k), win(c.rows, b, k)
                    gp.tensor_tensor(xm, xm, c.dskip[:, :].unsqueeze(1).to_broadcast([P, 2, D]), ALU.mult).then_inc(skip_ok, 1)
                    gp.tensor_tensor(rows, rows, win(c.film, b, k)[:, :, D:2 * D], ALU.add).then_inc(base_ok, 1)

        @blk.vector
        def _(v):
            n = 0

            def link(*ins):
                nonlocal n
                for x in ins:
                    x.then_inc(prod, 1)
                n += len(ins)
                v.wait_ge(prod, n)

            def tt(o, a, b, op):
                return v.tensor_tensor(o, a, b, op)

            def products(b):
                v.wait_ge(x0_ok, b + 1)
                v.scalar_tensor_tensor(xz[:, :, 1, :], xz[:, :, 0, :], c.sign[:, 0:1], xf_ps[:, :, D:2 * D], ALU.mult, ALU.add).then_inc(xz_ok, 1)
                v.wait_ge(xz_ok, b + 1)
                xr, xi = xz[:, 0:2, :, :], xz[:, 2:4, :, :]
                r0, i0 = xr[:, :, 0, :], xi[:, :, 0, :]
                yr, yi = yh[:, 0:2, :, :], yh[:, 2:4, :, :]
                link(tt(t[0][:, :, :, :], xr, UA, ALU.mult), tt(t[1][:, :, :, :], xi, UB, ALU.mult))
                wait(v, inv_ok, 2 * b, 2 * b)
                link(tt(yr, t[0][:, :, :, :], t[1][:, :, :, :], ALU.subtract))
                v.wait_ge(ppool, 2 * b + 2)
                link(tt(yi, t[2][:, :, :, :], t[3][:, :, :, :], ALU.add), tt(t[0][:, :, 0, :], r0, VA, ALU.mult), tt(t[0][:, :, 1, :], i0, VB, ALU.mult),
                     tt(t[1][:, :, 0, :], r0, VB, ALU.mult), tt(t[1][:, :, 1, :], i0, VD, ALU.mult))
                link(tt(yr[:, :, 1, :], yr[:, :, 1, :], t[0][:, :, 0, :], ALU.add), tt(yi[:, :, 1, :], yi[:, :, 1, :], t[1][:, :, 0, :], ALU.add))
                link(tt(yr[:, :, 1, :], yr[:, :, 1, :], t[0][:, :, 1, :], ALU.subtract), tt(yi[:, :, 1, :], yi[:, :, 1, :], t[1][:, :, 1, :], ALU.add))
                v.sem_inc(yh_ok, 1)

            def outer(b):
                for k in range(2):
                    xm, rows = win(c.xm, b, k), win(c.rows, b, k)
                    v.wait_ge(inv_ok, 2 * b + k + 1)
                    v.wait_ge(skip_ok, 2 * b + k + 1)
                    v.tensor_tensor(xm, xm, y_ps[k][:, :].rearrange("p (q d) -> p q d", q=2), ALU.add).then_inc(y_ok, 1)
                    v.wait_ge(y_ok, 2 * b + k + 1)
                    link(tt(xm, xm, win(c.film, b, k)[:, :, 0:D], ALU.mult))
                    v.wait_ge(base_ok, 2 * b + k + 1)
                    link(tt(rows, rows, xm, ALU.add))
                for i in range(TB * b, TB * b + TB):
                    v.bn_stats(keep.stats[:, i, :], c.rows[:, i, :]).then_inc(st_ok, 1)

            for b in range(B):
                products(b)
                if b >= 1:
                    outer(b - 1)
            outer(B - 1)
            v.wait_ge(st_ok, T)


def dense_ffn(nc, io, keep, c):
    FH = 4 * D
    MH = FH // P
    with ExitStack() as ctx:
        def sb(name, shape, dt=F32):
            return ctx.enter_context(nc.sbuf_tensor(name, shape, dt))

        sem = keep.sems.new

        w1, w1g = sb("ffn_w1", [P, KD, FH]), sb("ffn_w1_gain", [P, KD, FH])
        w2 = sb("ffn_w2", [P, MH, D])
        gT, bT, b1T, b1s = sb("g_ffnT", [P, KD]), sb("b_ffnT", [P, KD]), sb("ffn_b1T", [P, MH]), sb("ffn_b1_sum", [P, MH])
        b2 = sb("ffn_b2", [P, D])
        g_out, b_out = sb("g_norm_out", [P, D]), sb("b_norm_out", [P, D])
        tmp, mean, rstd = sb("tmp_f", [P, 4, T]), sb("mean_f", [P, T]), sb("rstd_f", [P, T])
        xs, xT = sb("xs_f", [P, TB, D]), sb("xT_f", [P, 2, KD, S])
        hid = sb("hid_f", [P, MH, S])
        t_ps = ctx.enter_context(nc.psum_tensor("ft_ps", [P, KD, 512], F32))
        h_ps = [ctx.enter_context(nc.psum_tensor(f"fh_ps{i}", [P, 512], F32)) for i in range(3)]
        o_ps = [ctx.enter_context(nc.psum_tensor(f"fo_ps{i}", [P, 512], F32)) for i in range(2)]
        ld, dve, var_ok, std_ok, w1_ok, bias_ok = (sem(n) for n in ("ld_f", "dve_f", "var_f", "std_f", "w1_gain_ready", "bias_in_psum"))
        xs_ok, xT_ok, xTs_ok, h_ok, act_ok, o_ok, x5_ok, rb_ok, st_ok = (sem(n + "_f") for n in ("xs", "xT", "xTs", "h", "act", "o", "x5", "rb", "stats"))
        fin, finp, dve_bias = sem("final_dve"), sem("final_pool"), sem("bias_ready")
        blk = ctx.enter_context(nc.Block())

        @blk.sync
        def _(sp):
            for dst, src in ((w1[:, :, :], io["ffn_w1"].rearrange("(k c) n -> c k n", k=KD)), (gT[:, :], io["g_ffnT"]), (bT[:, :], io["b_ffnT"]),
                             (b1T[:, :], io["ffn_b1T"]), (b2[:, :], io["ffn_b2"].partition_broadcast(P)),
                             (w2[:, :, :], io["ffn_w2"].rearrange("(k c) n -> c k n", k=MH)),
                             (g_out[:, :], io["g_norm_out"].partition_broadcast(P)), (b_out[:, :], io["b_norm_out"].partition_broadcast(P))):
                sp.dma_start(dst, src).then_inc(ld, 16)
            for x in range(E):
                sp.dma_start(keep.w1[:, x, :, :], io["w1_1"][x].rearrange("(k c) n -> c k n", k=KD)).then_inc(keep.ld_w1, 16)
                sp.dma_start(keep.w2[:, x, :, :], io["w2_1"][x].rearrange("(k c) n -> c k n", k=F1 // P)).then_inc(keep.ld_w2, 16)

        LOADS = 16 * 8

        @blk.gpsimd
        def _(gp):
            gp.wait_ge(ld, LOADS)
            gate = keep.gate[:, 1:2]
            gp.tensor_scalar(g_out[:, :], g_out[:, :], gate, None, ALU.mult).then_inc(finp, 1)
            gp.tensor_scalar(b_out[:, :], b_out[:, :], gate, None, ALU.mult).then_inc(finp, 1)
            gp.wait_ge(finp, 2)
            for b in range(B):
                sl = slice(TB * b, TB * b + TB)
                wide = [P, TB, D]
                gp.wait_ge(xs_ok, TB * (b + 1))
                gp.tensor_tensor(c.rows[:, sl, :], c.rows[:, sl, :], b2[:, :].unsqueeze(1).to_broadcast(wide), ALU.add).then_inc(rb_ok, 1)
                gp.tensor_tensor(keep.x1[:, sl, :], keep.x1[:, sl, :], b_out[:, :].unsqueeze(1).to_broadcast(wide), ALU.add).then_inc(finp, 1)
            with gp.Fori(0, T) as t:
                gp.wait_ge(fin, t + 1)
                r = row(c.rows, t)
                gp.tensor_tensor(r, r, g_out[:, :], ALU.mult).then_inc(finp, 1)

        @blk.scalar
        def _(act):
            act.wait_ge(var_ok, 1)
            nc.scalar.activation(rstd[:, :], tmp[:, 0, :], ACT.Sqrt).then_inc(std_ok, 1)
            for b in range(B):
                for m in range(MH):
                    n = MH * b + m
                    act.wait_ge(h_ok, n + 1)
                    if m == 0:
                        act.wait_ge(dve_bias, 1)
                        wait(act, o_ok, TB * b, TB * b)
                    nc.scalar.activation(hid[:, m, :], h_ps[n % 3][:, :], ACT.Gelu, bias=b1s[:, m:m + 1]).then_inc(act_ok, 1)
            act.wait_ge(var_ok, 2)
            nc.scalar.activation(rstd[:, :], tmp[:, 0, :], ACT.Sqrt).then_inc(std_ok, 1)

        @blk.tensor
        def _(pe):
            pe.wait_ge(ld, LOADS)
            for m in range(MH):
                for k in range(KD):
                    x = nc.tensor.matmul(o_ps[0][:, m:m + 1], w1[:, k, m * P:(m + 1) * P], bT[:, k:k + 1], start=(k == 0), stop=(k == KD - 1))
            x.then_inc(bias_ok, 1)

            def turn(b):
                for i in range(TB):
                    pe.wait_ge(xs_ok, TB * b + i + 1)
                    if i == 0:
                        wait(pe, xTs_ok, 2 * b, 2 * b)
                    for k in range(KD):
                        x = nc.tensor.transpose(t_ps[:, k, i * P:(i + 1) * P], xs[:, i, k * P:(k + 1) * P], keep.ident[:, :])
                    x.then_inc(xT_ok, 1)

            turn(0)
            pe.wait_ge(w1_ok, 2)
            for b in range(B):
                pe.wait_ge(xTs_ok, 2 * b + 2)
                for m in range(MH):
                    n = MH * b + m
                    wait(pe, act_ok, n - 2, n - 2)
                    for k in range(KD):
                        x = nc.tensor.matmul(h_ps[n % 3][:, :], w1g[:, k, m * P:(m + 1) * P], xT[:, b % 2, k, :], start=(k == 0), stop=(k == KD - 1))
                    x.then_inc(h_ok, 1)
                if b + 1 < B:
                    turn(b + 1)
                pe.wait_ge(act_ok, MH * (b + 1))
                for i in range(TB):
                    n = TB * b + i
                    if n == 0:
                        pe.wait_ge(dve_bias, 1)
                    wait(pe, x5_ok, n - 1, n - 1)
                    for k in range(MH):
                        x = nc.tensor.matmul(o_ps[n % 2][:, 0:D], hid[:, k, i * P:(i + 1) * P], w2[:, k, :], start=(k == 0), stop=(k == MH - 1))
                    x.then_inc(o_ok, 1)

        @blk.vector
        def _(v):
            n = norm_from_stats(v, 0, dve, keep.stats, tmp, mean, rstd)
            v.wait_ge(dve, n)
            v.sem_inc(var_ok, 1)
            v.wait_ge(ld, LOADS)
            for k in range(KD):
                v.tensor_scalar(w1g[:, k, :], w1[:, k, :], gT[:, k:k + 1], None, ALU.mult).then_inc(w1_ok, 1)
            v.wait_ge(std_ok, 1)
            v.reciprocal(rstd[:, :], rstd[:, :]).then_inc(dve, 1)
            n += 1
            v.wait_ge(dve, n)

            def ln(b):
                for i in range(TB):
                    t = TB * b + i
                    wait(v, xT_ok, TB * (b - 1) + i + 1, TB * (b - 1) + i + 1)
                    v.tensor_scalar(xs[:, i, :], c.rows[:, t, :], mean[:, t:t + 1], rstd[:, t:t + 1], ALU.subtract, ALU.mult).then_inc(xs_ok, 1)
                v.wait_ge(xT_ok, TB * (b + 1))
                wait(v, h_ok, MH * (b - 1), MH * (b - 1))
                for k in range(KD):
                    v.tensor_copy(xT[:, b % 2, k, :], t_ps[:, k, :]).then_inc(xTs_ok, 1)

            ln(0)
            v.wait_ge(bias_ok, 1)
            v.tensor_tensor(b1s[:, :], o_ps[0][:, 0:MH], b1T[:, :], ALU.add).then_inc(dve_bias, 1)
            for b in range(B):
                if b + 1 < B:
                    ln(b + 1)
                v.wait_ge(rb_ok, b + 1)
                for i in range(TB):
                    t = TB * b + i
                    v.wait_ge(o_ok, t + 1)
                    v.tensor_tensor(c.rows[:, t, :], c.rows[:, t, :], o_ps[t % 2][:, 0:D], ALU.add).then_inc(x5_ok, 1)
                    v.wait_ge(x5_ok, t + 1)
                    v.bn_stats(keep.stats[:, t, :], c.rows[:, t, :]).then_inc(st_ok, 1)
            v.wait_ge(st_ok, T)
            n = norm_from_stats(v, n, dve, keep.stats, tmp, mean, rstd)
            v.wait_ge(dve, n)
            v.sem_inc(var_ok, 1)
            v.wait_ge(std_ok, 2)
            v.reciprocal(rstd[:, :], rstd[:, :]).then_inc(dve, 1)
            v.wait_ge(dve, n + 1)
            with v.Fori(0, T) as t:
                v.tensor_scalar(row(c.rows, t), row(c.rows, t), mean[:, bass.ds(t, 1)], rstd[:, bass.ds(t, 1)], ALU.subtract, ALU.mult).then_inc(fin, 1)
            with v.Fori(0, T) as t:
                v.wait_ge(finp, t + (2 + B + 1))
                v.tensor_tensor(row(keep.x1, t), row(keep.x1, t), row(c.rows, t), ALU.add).then_inc(x5_ok, 1)
                v.wait_ge(x5_ok, t + (T + 1))
                v.bn_stats(row(keep.stats, t), row(keep.x1, t)).then_inc(st_ok, 1)
            v.wait_ge(st_ok, 2 * T)


class Kept:
    pass


def store_x(nc, x1, out):
    with ExitStack() as ctx:
        written = ctx.enter_context(nc.semaphore("written"))
        blk = ctx.enter_context(nc.Block())

        @blk.sync
        def _(sp):
            sp.dma_start(out.rearrange("(n p) d -> p n d", p=P), x1[:, :, :]).then_inc(written, 16)
            sp.wait_ge(written, 16)


def build(nc, io, out):
    with ExitStack() as ctx:
        def sb(name, shape, dt=F32):
            return ctx.enter_context(nc.sbuf_tensor(name, shape, dt))

        keep = Kept()
        keep.x1 = sb("x1", [P, T, D])
        keep.stats = sb("stats", [P, T, 6])
        keep.gate = sb("gate", [P, 4])
        keep.ident, keep.ustrict = sb("ident", [P, P]), sb("ustrict", [P, P])
        keep.ones = sb("ones_", [P, P])
        keep.z = sb("z_powers", [P, 2, 9, P])
        keep.dc = sb("dc_twice", [P, 2, P])
        keep.xslots, keep.yslots, keep.zeroed, keep.zero_loads = {}, {}, {}, {}
        for tag, k in (("0", 1), ("1", 2)):
            n = k * T + E - 1
            keep.xslots[tag] = nc.dram_tensor(f"xslots{tag}", (n * P, D), F32, kind="Internal").ap()
            keep.yslots[tag] = nc.dram_tensor(f"yslots{tag}", (n * P, D), F32, kind="Internal").ap()
            keep.zeroed[tag] = ctx.enter_context(nc.semaphore(f"zeroed{tag}"))
            keep.zero_loads[tag] = 1
        keep.ld_w2 = ctx.enter_context(nc.semaphore("ld_expert_w2"))
        keep.ld_w1 = ctx.enter_context(nc.semaphore("ld_expert_w1"))
        with ExitStack() as w0:
            keep.sems = w0.enter_context(LayerSemaphores(nc))
            keep.w1 = w0.enter_context(nc.sbuf_tensor("w1_0", [P, E, KD, F0], F32))
            layer0_attention(nc, io, keep)
            keep.w2 = w0.enter_context(nc.sbuf_tensor("w2_0", [P, E, F0 // P, D], F32))
            routed_experts(nc, io, keep, 1, F0, ACT.Silu, 2, "0")
        with ExitStack() as w1:
            c = Kept()
            c.rows = w1.enter_context(nc.sbuf_tensor("xt_rows", [P, T, D], F32))
            with ExitStack() as lc:
                keep.sems = lc.enter_context(LayerSemaphores(nc))
                c.kernel_dram = nc.dram_tensor("conv_kernel", (D, S), F32, kind="Internal").ap()
                with ExitStack() as lx:
                    c.xm = lx.enter_context(nc.sbuf_tensor("xm", [P, T, D], F32))
                    c.film = lx.enter_context(nc.sbuf_tensor("film", [P, T, 2 * D], F32))
                    layer1_attention(nc, io, keep, c)
                    c.fwd = lx.enter_context(nc.sbuf_tensor("dft_table", [P, 2, 6 * P], F32))
                    c.inv = lx.enter_context(nc.sbuf_tensor("idft_table", [P, 4, W], F32))
                    c.sign = lx.enter_context(nc.sbuf_tensor("sign", [P, 1], F32))
                    c.dskip = lx.enter_context(nc.sbuf_tensor("d_skip", [P, D], F32))
                    c.kf = lx.enter_context(nc.sbuf_tensor("kernel_hat", [P, 6, 2, D], F32))
                    kernel_transform(nc, io, keep, c)
                    convolution(nc, io, keep, c)
                keep.w1 = w1.enter_context(nc.sbuf_tensor("w1_1", [P, E, KD, F1], F32))
                keep.w2 = w1.enter_context(nc.sbuf_tensor("w2_1", [P, E, F1 // P, D], F32))
                dense_ffn(nc, io, keep, c)
            keep.sems = w1.enter_context(LayerSemaphores(nc))
            routed_experts(nc, io, keep, 2, F1, ACT.Gelu, 3, "1")
            store_x(nc, keep.x1, out)


def constants():
    import numpy as np

    c = {"ident": np.eye(P, dtype=np.float32), "ustrict": np.triu(np.ones((P, P), np.float32), 1)}
    ch = np.arange(P)
    c["headmask16"] = np.where(ch[:, None] // DH0 == np.arange(8)[None], np.float32(DH0 ** -0.5), np.float32(0)).astype(np.float32)
    c["headmask32"] = (ch[:, None] // DH1 == np.arange(H1)[None]).astype(np.float32)
    f, t = np.arange(W)[None], np.arange(W)[:, None]
    turn = 2 * np.pi * ((f * t) % (2 * W)) / (2 * W)
    cos, sin = np.cos(turn), -np.sin(turn)
    nyquist = np.where(t % 2, -1.0, 1.0)
    ca, cb, sa, sb = cos[:, :P], cos[:, P:], sin[:, :P], sin[:, P:]
    c["dft"] = np.concatenate([ca, cb, np.hstack([nyquist, sa[:, 1:]]), sb, sa, np.hstack([nyquist, ca[:, 1:]])], 1).astype(np.float32)
    back = np.concatenate([ca, cb, np.hstack([nyquist, sa[:, 1:]]), sb], 1).T / W
    back[[0, 2 * P]] /= 2
    c["idft"] = back.astype(np.float32)
    c["sign"] = np.where(ch % 2, -1.0, 1.0).astype(np.float32)[:, None]
    e = np.arange(E, dtype=np.float32)
    c["iota_e"] = np.stack([e - 100, e])
    c["iota_t"] = np.arange(2 * T + E - 1, dtype=np.float32)
    c["part"] = np.concatenate([np.repeat(np.eye(3, dtype=np.float32), E, 0), np.tile(e, 3)[:, None]], 1)
    return c


def kernel(**inputs):
    import numpy as np
    import concourse.bacc as bacc
    from concourse.bass_utils import run_bass_kernel_spmd

    g = {k: np.asarray(v) for k, v in inputs.items()}

    def col(name, k):
        return g[name].reshape(k, -1).T

    arrays = {
        "x": g["x"].reshape(B * S, D),
        "ctxT": g["ctx_768"].reshape(B * SK, DC).T,
        "g_xattn": g["g_xattn"], "g_ffn": g["g_ffn"],
        "wq0": g["L0_xattn_Wq"], "wk0": g["L0_xattn_Wk"], "wv0": g["L0_xattn_Wv"], "wo0": g["L0_xattn_Wo"],
        "bq0T": col("L0_xattn_bq", KD), "bk0T": col("L0_xattn_bk", KD), "bv0T": col("L0_xattn_bv", KD),
        "bv0": g["L0_xattn_bv"], "bo0": g["L0_xattn_bo"],
        "w1_0": g["L0_ffn_W1"], "w2_0": g["L0_ffn_W2"], "b1_0": g["L0_ffn_b1"], "b2_0": g["L0_ffn_b2"],
        "wg0": g["L0_ffn_Wg"], "bg0": g["L0_ffn_bg"],
        "wq1": g["L1_xattn_Wq"], "wk1": g["L1_xattn_Wk"], "wv1": g["L1_xattn_Wv"],
        "w_film_in": g["L1_xattn_W_film_in"], "w_film_out": g["L1_xattn_W_film_out"],
        "b_film_in": g["L1_xattn_b_film_in"], "b_film_out": g["L1_xattn_b_film_out"],
        "mod_gate": g["L1_xattn_mod_gate"].reshape(1),
        "g_norm_in": g["L1_xattn_g_norm_in"], "b_norm_in": g["L1_xattn_b_norm_in"],
        "key_mask": g["mask_BxS2_bf1"].reshape(B * SK).view(np.uint8), "token_mask": g["mask_BxS_bf1"].reshape(T, P).T.copy().view(np.uint8),
        "a_reT": g["L1_xattn_A_re"].T, "a_imT": g["L1_xattn_A_im"].T, "c_reT": g["L1_xattn_C_re"].T, "c_imT": g["L1_xattn_C_im"].T,
        "log_dt": g["L1_xattn_log_dt"], "d_skip": g["L1_xattn_D_skip"],
        "ffn_w1": g["L1_xattn_W1"], "ffn_w2": g["L1_xattn_W2"], "ffn_b1T": col("L1_xattn_b1", 8), "ffn_b2": g["L1_xattn_b2"],
        "g_ffnT": col("L1_xattn_g_ffn", KD), "b_ffnT": col("L1_xattn_b_ffn", KD),
        "g_norm_out": g["L1_xattn_g_norm_out"], "b_norm_out": g["L1_xattn_b_norm_out"],
        "w1_1": g["L1_ffn_w1"].transpose(0, 2, 1), "w2_1": g["L1_ffn_w2"].transpose(0, 2, 1),
        "b1_1": g["L1_ffn_b1"], "b2_1": g["L1_ffn_b2"], "wg1": g["L1_ffn_router_w"].T,
        **constants(),
    }
    nc = bacc.Bacc("TRN2", target_bir_lowering=False, num_devices=1)
    arrays = {f"in_{k}": np.ascontiguousarray(a) for k, a in arrays.items()}
    io = {k[3:]: nc.dram_tensor(k, a.shape, mybir.dt.from_np(a.dtype), kind="ExternalInput").ap() for k, a in arrays.items()}
    out = nc.dram_tensor("x_out", (B * S, D), F32, kind="ExternalOutput").ap()
    build(nc, io, out)
    got = run_bass_kernel_spmd(nc, [arrays], core_ids=[0])
    return got.results[0]["x_out"].reshape(B, S, D)
```

```python
from contextlib import ExitStack

import concourse.bass as bass
from concourse import mybir

ALU = mybir.AluOpType
ACT = mybir.ActivationFunctionType
F32 = mybir.dt.float32
BF16 = mybir.dt.bfloat16
I32 = mybir.dt.int32
U32 = mybir.dt.uint32
U8 = mybir.dt.uint8
AX = mybir.AxisListType.X

P = 128
B, S, D = 4, 512, 256
SK, DC = 64, 192
T = B * S // P
TB = S // P
KD = D // P
KC = 96
H0 = 16
DH0 = D // H0
HP0 = H0 // 2
CLAMP = 10000.0
EPS = 1e-5
E = 8
F0, F1 = 1024, 512
LOWEST = -3.0e38


def static(v):
    return isinstance(v, int)


def wait(eng, sem, value, at):
    if at >= 1:
        eng.wait_ge(sem, value)


def pipeline(eng, slot, first, steady, stop, last):
    for t in range(first, steady):
        slot(t, t)
    with eng.Fori(0, (stop - steady) // 2) as i:
        for u in range(2):
            slot(i * 2 + (steady + u), steady + u)
    for t in range(stop, last + 1):
        slot(t, t)


def row(buf, t):
    return buf[:, bass.ds(t, 1), :].rearrange("p a n -> p (a n)")


def halves(stats):
    return stats[:, :, 1], stats[:, :, 2], stats[:, :, 4], stats[:, :, 5]


def norm_from_stats(v, act_done, sem, stats, tmp, mean, rstd, var_only=None):
    m0, q0, m1, q1 = halves(stats)
    v.tensor_tensor(tmp[:, 1, :], m0, m1, ALU.subtract).then_inc(sem, 1)
    v.tensor_tensor(tmp[:, 2, :], q0, q1, ALU.add).then_inc(sem, 1)
    v.tensor_tensor(mean[:, :], m0, m1, ALU.add).then_inc(sem, 1)
    v.wait_ge(sem, act_done + 3)
    v.tensor_tensor(tmp[:, 3, :], tmp[:, 1, :], tmp[:, 1, :], ALU.mult).then_inc(sem, 1)
    v.tensor_scalar(tmp[:, 2, :], tmp[:, 2, :], 1.0 / D, EPS, ALU.mult, ALU.add).then_inc(sem, 1)
    v.tensor_scalar(mean[:, :], mean[:, :], 0.5, None, ALU.mult).then_inc(sem, 1)
    v.wait_ge(sem, act_done + 6)
    v.scalar_tensor_tensor(tmp[:, 0, :], tmp[:, 3, :], 0.25, tmp[:, 2, :], ALU.mult, ALU.add).then_inc(sem, 1)
    return act_done + 7


class LayerSemaphores:

    def __init__(self, nc):
        self.nc, self.held = nc, []

    def __enter__(self):
        return self

    def new(self, name):
        self.held.append(self.nc.alloc_semaphore(name))
        return self.held[-1]

    def __exit__(self, *failed):
        if failed[0] is None:
            self.nc.clear_and_free_semaphores(self.held)
            self.nc.all_engine_barrier()


def layer0_attention(nc, io, keep):
    with ExitStack() as ctx:
        def sb(name, shape, dt=F32):
            return ctx.enter_context(nc.sbuf_tensor(name, shape, dt))

        def bank(name):
            return ctx.enter_context(nc.psum_tensor(name, [P, 512], F32))

        sem = keep.sems.new

        x = sb("x_in", [P, T, D])
        ctxT = sb("ctxT", [KC, 2, B, 2, SK])
        wq, wo = sb("wq0", [P, KD, D]), sb("wo0", [P, KD, D])
        wk, wv = sb("wk0", [KC, 2, D]), sb("wv0", [KC, 2, D])
        bqT, bkT, bvT = sb("bqT", [P, KD]), sb("bkT", [P, KD]), sb("bvT", [P, KD])
        bv, bo = sb("bv_rows", [P, D]), sb("bo_rows", [P, D])
        headmask = sb("headmask", [P, 8])
        kT = sb("kT", [P, KD, B, SK])
        kbd = sb("k_blockdiag", [P, B, KD, 8, SK])
        vbd = sb("v_blockdiag", [P, B, HP0, 2 * (DH0 + 1)])
        csum = sb("ctx_sum", [KC, 2, B])
        vmT = sb("vmeanT", [P, KD, B])
        vmTw = sb("vmeanT_wide", [P, KD, B, P])
        gv = sb("guard_rows", [P, B, D])
        stats = sb("stats_x", [P, T, 6])
        gstats = sb("stats_guard", [P, T, 6])
        tmp, mean, rstd = sb("tmp_x", [P, 4, T]), sb("mean_x", [P, T]), sb("rstd_x", [P, T])
        xn = sb("xn", [P, 2, D])
        xnT, qT = sb("xnT", [P, KD, P]), sb("qT", [P, 2, KD, P])
        sc = sb("scores", [P, 2, H0, SK])
        top = sb("rowmax", [P, 2, H0])
        pT = sb("probsT", [P, HP0, P])
        junk = sb("junk", [P, 2, 512], BF16)
        nanp, nans, nanm = sb("nan_part", [P, 4]), sb("nan_sum", [P, 1]), sb("nan_mask", [P, 1])
        ones = sb("ones", [P, P])
        nanw = sb("nan_wide", [P, D], I32)
        zeros = sb("zeros", [P, 2 * D])
        rden, oN, oT = sb("rden", [P, H0]), sb("oN", [P, D]), sb("oT", [P, KD, P])

        s0 = [ctx.enter_context(nc.psum_tensor(f"S{i}", [P, 2, 512], F32)) for i in range(2)]
        pt0 = ctx.enter_context(nc.psum_tensor("PT", [P, 2, 512], F32))
        m0, m1 = bank("M0"), bank("M1")

        ld_x = [sem(f"ld_x{b}") for b in range(B)]
        ld_w = sem("ld_w")
        ld_ctx = sem("ld_ctx")
        gates = sem("gates_done")
        dve = sem("dve_chain")
        pool = sem("pool_chain")
        setup_mm = sem("setup_matmuls")
        kbd_ok, vbd_ok = sem("kbd_ready"), sem("vbd_ready")
        std_ok, rstd_ok = sem("std_ready"), sem("rstd_ready")
        xn_ok, xT_ok, xnT_ok, q_ok, qT_ok = (sem(n) for n in ("xn_ready", "xT_in_psum", "xnT_ready", "q_in_psum", "qT_ready"))
        s_ok, max_ok, cmax_ok, clip_ok, abs_ok = (sem(n) for n in ("scores_ready", "max_ready", "cmax_ready", "clip_ready", "abs_done"))
        sub_ok, exp_ok = sem("shifted_ready"), sem("probs_ready")
        pT_ok, pTa_ok, pTd_ok = sem("probsT_in_psum"), sem("probsT_act_half"), sem("probsT_dve_half")
        o_ok, rden_ok, oN_ok, oT_ok, oTs_ok, wo_ok = (sem(n) for n in ("o_in_psum", "rden_ready", "oN_ready", "oT_in_psum", "oT_ready", "proj_ready"))
        res_ok, xb_ok, xg_ok = sem("x1_ready"), sem("xb_ready"), sem("xg_ready")
        gst_ok, st_ok, nan_ok, flag_ok = sem("guard_stats_done"), sem("stats_done"), sem("nan_added"), sem("flag_ready")
        zero_ok = sem("zeros_ready")
        gv_ok, vm_ok = sem("gv_ready"), sem("vm_ready")

        xv = io["x"].rearrange("(n p) d -> p n d", p=P)
        cv = io["ctxT"].rearrange("(k c) (b s) -> c k b s", k=2, b=B)

        N_SMALL = 10
        blk = ctx.enter_context(nc.Block())

        @blk.sync
        def _(sp):
            for k in range(2):
                for dup in range(2):
                    sp.dma_start(ctxT[:, k, :, dup, :], cv[:, k]).then_inc(ld_ctx, 16)
            sp.dma_start(wk[:, :, :], io["wk0"].rearrange("(k c) n -> c k n", k=2)).then_inc(ld_ctx, 16)
            sp.dma_start(wv[:, :, :], io["wv0"].rearrange("(k c) n -> c k n", k=2)).then_inc(ld_ctx, 16)
            for b in range(B):
                sp.dma_start(x[:, TB * b:TB * b + TB, :], xv[:, TB * b:TB * b + TB, :]).then_inc(ld_x[b], 16)
            sp.dma_start(wq[:, :, :], io["wq0"].rearrange("(k c) n -> c k n", k=KD)).then_inc(ld_w, 16)
            sp.dma_start(wo[:, :, :], io["wo0"].rearrange("(k c) n -> c k n", k=KD)).then_inc(ld_w, 16)
            sp.dma_start(keep.gate[:, 0:2], io["g_xattn"].partition_broadcast(P)).then_inc(ld_w, 16)
            sp.dma_start(keep.gate[:, 2:4], io["g_ffn"].partition_broadcast(P)).then_inc(ld_w, 16)
            sp.dma_start(bqT[:, :], io["bq0T"]).then_inc(ld_w, 16)
            sp.dma_start(bkT[:, :], io["bk0T"]).then_inc(ld_w, 16)
            sp.dma_start(bvT[:, :], io["bv0T"]).then_inc(ld_w, 16)
            sp.dma_start(bv[:, :], io["bv0"].partition_broadcast(P)).then_inc(ld_w, 16)
            sp.dma_start(bo[:, :], io["bo0"].partition_broadcast(P)).then_inc(ld_w, 16)
            sp.dma_start(headmask[:, :], io["headmask16"]).then_inc(ld_w, 16)
            sp.dma_start(keep.ident[:, :], io["ident"]).then_inc(ld_w, 16)
            sp.dma_start(keep.ustrict[:, :], io["ustrict"]).then_inc(ld_w, 16)
            sp.wait_ge(zero_ok, 1)
            for tag, slots in keep.xslots.items():
                sp.dma_start(slots.rearrange("(n p) d -> p n d", p=P),
                             zeros[:, 0:D].unsqueeze(1).to_broadcast([P, slots.shape[0] // P, D])).then_inc(keep.zeroed[tag], 16)
            for e in range(E):
                sp.dma_start(keep.w1[:, e, :, :], io["w1_0"][e].rearrange("(k c) n -> c k n", k=KD)).then_inc(keep.ld_w1, 16)


        @blk.gpsimd
        def _(gp):
            gp.memset(zeros[:, :], 0.0).then_inc(zero_ok, 1)
            gp.memset(ones[:, :], 1.0).then_inc(pool, 1)
            gp.memset(vbd[:, :, :, :], 0.0).then_inc(pool, 1)
            gp.wait_ge(gates, 1)
            gp.tensor_scalar(bo[:, :], bo[:, :], keep.gate[:, 0:1], None, ALU.mult).then_inc(pool, 1)
            gp.wait_ge(pool, 3)
            def slot(t, at):
                if 0 <= at < T:
                    gp.wait_ge(clip_ok, t + 1)
                    gp.wait_ge(cmax_ok, t + 1)
                    b = sc[:, at % 2, :, :]
                    gp.tensor_tensor(b, b, top[:, at % 2, :].unsqueeze(2).to_broadcast([P, H0, SK]), ALU.subtract).then_inc(sub_ok, 1)
                    gp.tensor_tensor(row(x, t), row(x, t), bo[:, :], ALU.add).then_inc(xb_ok, 1)
                if 0 <= at - 4 < T:
                    gp.wait_ge(res_ok, t - 3)
                    gp.tensor_tensor(row(x, t - 4), row(x, t - 4), row(gv, (t - 4) // TB), ALU.add).then_inc(xg_ok, 1)
            for b in range(B):
                gp.wait_ge(ld_x[b], 16)
            gp.wait_ge(rstd_ok, 1)
            gp.wait_ge(xn_ok, 1)
            gp.wait_ge(gv_ok, B)
            pipeline(gp, slot, 0, 4, T, T + 3)

        @blk.scalar
        def _(act):
            act.wait_ge(ld_w, 16 * (N_SMALL + 2))
            nc.scalar.activation(keep.gate[:, :], keep.gate[:, :], ACT.Tanh).then_inc(gates, 1)
            act.wait_ge(rstd_ok, 1)
            nc.scalar.activation(rstd[:, :], tmp[:, 0, :], ACT.Sqrt).then_inc(std_ok, 1)

            def slot(t, at):
                if 0 <= at - 3 < T:
                    act.wait_ge(oT_ok, t - 2)
                    wait(act, wo_ok, t - 3, at - 3)
                    nc.scalar.activation(oT[:, :, :], m1[:, 0:KD * P].rearrange("p (k n) -> p k n", k=KD), ACT.Copy).then_inc(oTs_ok, 1)
                if 0 <= at + 1 < T:
                    act.wait_ge(xT_ok, t + 2)
                    wait(act, q_ok, t + 1, at + 1)
                    nc.scalar.activation(xnT[:, :, :], m0[:, 0:KD * P].rearrange("p (k n) -> p k n", k=KD), ACT.Copy).then_inc(xnT_ok, 1)
                if 0 <= at - 2 < T:
                    act.wait_ge(pT_ok, t - 1)
                    wait(act, o_ok, t - 2, at - 2)
                    nc.scalar.activation(pT[:, 0:4, :], pt0[:, 0, :].rearrange("p (a n) -> p a n", n=P), ACT.Copy).then_inc(pTa_ok, 1)
                if 0 <= at - 1 < T:
                    u = (at - 1) % 2
                    act.wait_ge(sub_ok, t)
                    nc.scalar.activation(sc[:, u, :, :], sc[:, u, :, :], ACT.Exp).then_inc(exp_ok, 1)
                    act.wait_ge(clip_ok, t)
                    wait(act, nan_ok, t - 2, at - 2)
                    wait(act, abs_ok, 2 * t - 2, 2 * at - 2)
                    for h in range(2):
                        nc.scalar.activation(junk[:, h, :], s0[u][:, h, :], ACT.Abs,
                                             accum_out=nanp[:, 2 * u + h:2 * u + h + 1]).then_inc(abs_ok, 1)
            pipeline(act, slot, -1, 4, T - 2, T + 2)

        @blk.tensor
        def _(pe):
            pe.wait_ge(ld_ctx, 16 * 6)
            for m in range(KD):
                for k in range(2):
                    mm = nc.tensor.matmul(s0[0][:, m, 0:B * SK], wk[:, k, m * P:(m + 1) * P], ctxT[:, k, :, 0, :],
                                          start=(k == 0), stop=(k == 1))
                mm.then_inc(setup_mm, 1)
            for b in range(B):
                for k in range(2):
                    mm = nc.tensor.matmul((s0[1], pt0)[b // 2][:, b % 2, 0:D], ctxT[:, k, b, :, :].rearrange("c u s -> c (u s)"), wv[:, k, :],
                                          start=(k == 0), stop=(k == 1))
                mm.then_inc(setup_mm, 1)
            pe.wait_ge(vm_ok, 1)
            for m in range(KD):
                for k in range(2):
                    mm = nc.tensor.matmul(m1[:, m * B:(m + 1) * B], wv[:, k, m * P:(m + 1) * P], csum[:, k, :],
                                          start=(k == 0), stop=(k == 1))
            mm.then_inc(setup_mm, 1)
            pe.wait_ge(vm_ok, 3)
            pe.wait_ge(ld_w, 16 * (N_SMALL + 2))
            for b in range(B):
                pe.wait_ge(vbd_ok, 2 * B + 2)
                for k in range(KD):
                    mm = nc.tensor.matmul((s0[1], pt0)[b // 2][:, b % 2, 0:D], vmTw[:, k, b, :], wo[:, k, :],
                                          start=(k == 0), stop=(k == KD - 1))
                mm.then_inc(setup_mm, 1)
            pe.wait_ge(gv_ok, B)
            pe.wait_ge(kbd_ok, B * KD)

            def slot(t, at):
                def scores(m):
                    return nc.tensor.matmul(s0[at % 2][:, m, :], qT[:, at % 2, m, :],
                                            kbd[:, bass.ds(t // TB, 1), m, :, :].rearrange("p a h s -> p (a h s)"),
                                            start=True, stop=True)

                if 0 <= at < T:
                    pe.wait_ge(qT_ok, t + 1)
                    wait(pe, abs_ok, 2 * t - 2, 2 * at - 2)
                    scores(0)
                if 0 <= at - 3 < T:
                    pe.wait_ge(oN_ok, t - 2)
                    for k in range(KD):
                        mm = nc.tensor.transpose(m1[:, k * P:(k + 1) * P], oN[:, k * P:(k + 1) * P], keep.ident[:, :])
                    mm.then_inc(oT_ok, 1)
                if 0 <= at + 1 < T:
                    u = (at + 1) % 2
                    pe.wait_ge(xn_ok, t + 2)
                    wait(pe, qT_ok, t + 1, at + 1)
                    for k in range(KD):
                        mm = nc.tensor.transpose(m0[:, k * P:(k + 1) * P], xn[:, u, k * P:(k + 1) * P], keep.ident[:, :])
                    mm.then_inc(xT_ok, 1)
                if 0 <= at - 2 < T:
                    u = at % 2
                    pe.wait_ge(exp_ok, t - 1)
                    wait(pe, pTa_ok, t - 2, at - 2)
                    wait(pe, pTd_ok, t - 2, at - 2)
                    for a in range(HP0):
                        mm = nc.tensor.transpose(pt0[:, a // 4, (a % 4) * P:(a % 4 + 1) * P],
                                                 sc[:, u, 2 * a:2 * a + 2, :].rearrange("p h s -> p (h s)"), keep.ident[:, :])
                    mm.then_inc(pT_ok, 1)
                if 0 <= at - 3 < T:
                    pe.wait_ge(oTs_ok, t - 2)
                    for k in range(KD):
                        mm = nc.tensor.matmul(m1[:, 0:D], oT[:, k, :], wo[:, k, :], start=(k == 0), stop=(k == KD - 1))
                    mm.then_inc(wo_ok, 1)
                if 0 <= at + 1 < T:
                    pe.wait_ge(xnT_ok, t + 2)
                    for m in range(KD):
                        for k in range(KD):
                            mm = nc.tensor.matmul(m0[:, m * P:(m + 1) * P], wq[:, k, m * P:(m + 1) * P], xnT[:, k, :],
                                                  start=(k == 0), stop=(k == KD - 1))
                    mm.then_inc(q_ok, 1)
                if 0 <= at < T:
                    scores(1).then_inc(s_ok, 1)
                if 0 <= at - 2 < T:
                    pe.wait_ge(pTa_ok, t - 1)
                    pe.wait_ge(pTd_ok, t - 1)
                    wait(pe, res_ok, t - 2, at - 2)
                    for a in range(HP0):
                        mm = nc.tensor.matmul(m1[:, 34 * a:34 * a + 34], pT[:, a, :],
                                              vbd[:, bass.ds((t - 2) // TB, 1), a, :].rearrange("p a n -> p (a n)"), start=True, stop=True)
                    mm.then_inc(o_ok, 1)
            pipeline(pe, slot, -1, 4, T - 2, T + 2)
            pe.wait_ge(flag_ok, 1)
            nc.tensor.matmul(m0[:, 0:1], ones[:, :], nans[:, :], start=True, stop=True).then_inc(setup_mm, 1)

        @blk.vector
        def _(v):
            v.memset(nans[:, :], 0.0).then_inc(dve, 1)
            for b in range(B):
                v.wait_ge(ld_x[b], 16)
                for t in range(TB * b, TB * b + TB):
                    v.bn_stats(stats[:, t, :], x[:, t, :]).then_inc(dve, 1)
            v.wait_ge(dve, 1 + T)
            n = norm_from_stats(v, 1 + T, dve, stats, tmp, mean, rstd)
            v.wait_ge(dve, n)
            v.sem_inc(rstd_ok, 1)
            v.wait_ge(ld_ctx, 16 * 6)
            v.reduce_sum(csum[:, :, :], ctxT[:, :, :, 0, :], AX).then_inc(vm_ok, 1)
            v.wait_ge(ld_w, 16 * (N_SMALL + 2))
            for m in range(KD):
                v.wait_ge(setup_mm, m + 1)
                v.tensor_scalar(kT[:, m, :, :], s0[0][:, m, 0:B * SK].rearrange("p (b s) -> p b s", b=B), bkT[:, m:m + 1], None, ALU.add).then_inc(dve, 1)
            v.wait_ge(dve, n + 2)
            for m in range(KD):
                for b in range(B):
                    v.tensor_tensor(kbd[:, b, m, :, :], kT[:, m, b, :].unsqueeze(1).to_broadcast([P, 8, SK]),
                                    headmask[:, :].unsqueeze(2).to_broadcast([P, 8, SK]), ALU.mult).then_inc(kbd_ok, 1)
            v.wait_ge(pool, 2)
            for u in range(2):
                v.memset(vbd[64 * u:64 * u + 64, :, :, 17 * u + DH0:17 * u + DH0 + 1], 1.0).then_inc(vbd_ok, 1)
            bvv = bv[:, :].rearrange("p (a u j) -> p a u j", u=2, j=DH0)
            for b in range(B):
                v.wait_ge(setup_mm, KD + b + 1)
                vp = (s0[1], pt0)[b // 2][:, b % 2, 0:D].rearrange("p (a u j) -> p a u j", u=2, j=DH0)
                for u in range(2):
                    q = slice(64 * u, 64 * u + 64)
                    v.tensor_tensor(vbd[q, b, :, 17 * u:17 * u + DH0], vp[q, :, u, :], bvv[q, :, u, :], ALU.add).then_inc(vbd_ok, 1)
            v.wait_ge(setup_mm, KD + B + 1)
            for m in range(KD):
                v.tensor_scalar(vmT[:, m, :], m1[:, m * B:(m + 1) * B], 1.0 / SK, bvT[:, m:m + 1], ALU.mult, ALU.add).then_inc(dve, 1)
            v.wait_ge(dve, n + 4)
            for m in range(KD):
                v.tensor_copy(vmTw[:, m, :, :], vmT[:, m, :].unsqueeze(2).to_broadcast([P, B, P])).then_inc(vm_ok, 1)
            v.wait_ge(gates, 1)
            for b in range(B):
                v.wait_ge(setup_mm, KD + B + 2 + b)
                v.tensor_scalar(gv[:, b, :], (s0[1], pt0)[b // 2][:, b % 2, 0:D], keep.gate[:, 0:1], None, ALU.mult).then_inc(gv_ok, 1)
            v.wait_ge(std_ok, 1)
            v.reciprocal(rstd[:, :], rstd[:, :]).then_inc(dve, 1)
            v.wait_ge(dve, n + 5)

            def slot(t, at):
                if 0 <= at - 2 < T:
                    v.wait_ge(pT_ok, t - 1)
                    wait(v, o_ok, t - 2, at - 2)
                    v.tensor_copy(pT[:, 4:8, :], pt0[:, 1, :].rearrange("p (a n) -> p a n", n=P)).then_inc(pTd_ok, 1)
                if 0 <= at + 2 < T:
                    wait(v, xT_ok, t + 1, at + 1)
                    v.tensor_scalar(xn[:, at % 2, :], row(x, t + 2), mean[:, bass.ds(t + 2, 1)], rstd[:, bass.ds(t + 2, 1)],
                                    ALU.subtract, ALU.mult).then_inc(xn_ok, 1)
                if 0 <= at - 3 < T:
                    v.wait_ge(wo_ok, t - 2)
                    v.wait_ge(xb_ok, t - 2)
                    v.scalar_tensor_tensor(row(keep.x1, t - 3), m1[:, 0:D], keep.gate[:, 0:1], row(x, t - 3), ALU.mult, ALU.add).then_inc(res_ok, 1)
                if 0 <= at + 1 < T:
                    u = (at + 1) % 2
                    v.wait_ge(q_ok, t + 2)
                    wait(v, s_ok, t, at)
                    v.tensor_tensor(qT[:, u, :, :], m0[:, 0:KD * P].rearrange("p (k n) -> p k n", k=KD),
                                    bqT[:, :].unsqueeze(2).to_broadcast([P, KD, P]), ALU.add).then_inc(qT_ok, 1)
                if 0 <= at < T:
                    u = at % 2
                    sv = s0[u][:, :, :].rearrange("p m (h s) -> p (m h) s", s=SK)
                    v.wait_ge(s_ok, t + 1)
                    wait(v, sub_ok, t - 1, at - 1)
                    v.reduce_max(top[:, u, :], sv, AX).then_inc(max_ok, 1)
                if 0 <= at - 2 < T:
                    ov = m1[:, 0:34 * HP0].rearrange("p (h j) -> p h j", j=DH0 + 1)
                    v.wait_ge(o_ok, t - 1)
                    v.reciprocal(rden[:, :], ov[:, :, DH0]).then_inc(rden_ok, 1)
                    v.wait_ge(rden_ok, t - 1)
                    wait(v, oT_ok, t - 2, at - 2)
                    v.tensor_tensor(oN[:, :].rearrange("p (h j) -> p h j", j=DH0), ov[:, :, 0:DH0],
                                    rden[:, :].unsqueeze(2).to_broadcast([P, H0, DH0]), ALU.mult).then_inc(oN_ok, 1)
                if 0 <= at < T:
                    u = at % 2
                    wait(v, pT_ok, t - 1, at - 1)
                    v.tensor_scalar(sc[:, u, :, :], sv, CLAMP, -CLAMP, ALU.min, ALU.max).then_inc(clip_ok, 1)
                    v.wait_ge(max_ok, t + 1)
                    v.tensor_scalar(top[:, u, :], top[:, u, :], CLAMP, -CLAMP, ALU.min, ALU.max).then_inc(cmax_ok, 1)
                if 0 <= at - 1 < T:
                    u = (at - 1) % 2
                    v.wait_ge(abs_ok, 2 * t)
                    wait(v, nan_ok, t - 1, at - 1)
                    v.scalar_tensor_tensor(nans[:, :], nanp[:, 2 * u:2 * u + 1], nanp[:, 2 * u + 1:2 * u + 2],
                                           nans[:, :], ALU.add, ALU.add).then_inc(nan_ok, 1)
                if 0 <= at - 4 < T:
                    v.wait_ge(res_ok, t - 3)
                    v.bn_stats(row(keep.stats, t - 4), row(keep.x1, t - 4)).then_inc(st_ok, 1)
                if 0 <= at - 5 < T:
                    v.wait_ge(xg_ok, t - 4)
                    v.bn_stats(row(gstats, t - 5), row(x, t - 5)).then_inc(gst_ok, 1)
            pipeline(v, slot, -2, 6, T - 2, T + 4)
            v.wait_ge(nan_ok, T)
            v.tensor_tensor(nans[:, :], nans[:, :], nans[:, :], ALU.not_equal).then_inc(flag_ok, 1)
            v.wait_ge(setup_mm, KD + B + 1 + B + 1)
            v.tensor_scalar(nanm[:, :], m0[:, 0:1], 0.0, None, ALU.is_gt).then_inc(flag_ok, 1)
            v.wait_ge(flag_ok, 2)
            v.tensor_copy(nanw[:, :], nanm[:, :].to_broadcast([P, D])).then_inc(flag_ok, 1)
            v.wait_ge(flag_ok, 3)
            v.wait_ge(xg_ok, T)
            v.wait_ge(st_ok, T)
            v.wait_ge(gst_ok, T)
            v.copy_predicated(keep.x1[:, :, :], nanw[:, :].unsqueeze(1).to_broadcast([P, T, D]), x[:, :, :]).then_inc(flag_ok, 1)
            v.copy_predicated(keep.stats[:, :, :], nanw[:, 0:6].unsqueeze(1).to_broadcast([P, T, 6]), gstats[:, :, :]).then_inc(flag_ok, 1)
            v.wait_ge(flag_ok, 5)


def routed_experts(nc, io, keep, K, F, act_fn, gate_col, tag, out=None):
    V = K * T
    NT = V + E - 1
    KF = F // P
    BP = 96
    xslots, yslots = keep.xslots[tag], keep.yslots[tag]

    with ExitStack() as ctx:
        def sb(name, shape, dt=F32):
            return ctx.enter_context(nc.sbuf_tensor(f"{name}{tag}", shape, dt))

        rows = sb("ln_rows", [P, T, D])
        picks = sb("picks", [P, V], U32)
        prob = sb("prob", [P, V])
        tile_expert = sb("tile_expert", [P, NT], I32)
        hot = sb("tile_hot", [BP, NT, P], BF16)
        bx = sb("b2_parts", [P, D], BF16)
        b1T = sb("b1T", [P, E, KF])

        with ExitStack() as rctx:
            def rb(name, shape, dt=F32):
                return rctx.enter_context(nc.sbuf_tensor(f"{name}{tag}", shape, dt))

            def rsem(name):
                return keep.sems.new(f"{name}{tag}")

            xs, xsT = rb("xs", [P, 2, D]), rb("xsT", [P, 2, KD, P])
            tmp, mean, rstd = rb("tmp", [P, 4, T]), rb("mean", [P, T]), rb("rstd", [P, T])
            wg = rb("wg", [P, KD, E])
            bg = rb("bg", [P, E])
            lg, ex = rb("logits", [P, T, E]), rb("ex", [P, T, E])
            oh = rb("onehot", [P, V, E])
            pre = [rb(f"prefix{i}", [P, V, E]) for i in range(2)]
            lmax = rb("lmax", [P, 2, T])
            first = rb("first", [P, T])
            iota = rb("iota", [P, 2, E])
            iota_t = rb("iota_t", [P, NT])
            cnt, cnti = rb("cnt", [P, E]), rb("cnti", [P, E], I32)
            ends = [rb(f"ends{i}", [P, E]) for i in range(2)]
            base = rb("base", [P, E])
            slotf = rb("slot_f", [P, V])
            past = rb("past", [P, NT, E])
            tef = rb("tile_expert_f", [P, NT])
            owner = rb("bias_owner", [BP, 1])
            bf = rb("b2_rows", [P, D])
            xT_bank = [rctx.enter_context(nc.psum_tensor(f"xT_ps{tag}{i}", [P, 512], F32)) for i in range(2)]
            lg_bank = rctx.enter_context(nc.psum_tensor(f"lg{tag}", [P, 512], F32))
            rank_bank = rctx.enter_context(nc.psum_tensor(f"rank{tag}", [P, 512], F32))
            cnt_bank = rctx.enter_context(nc.psum_tensor(f"count_ps{tag}", [P, 512], F32))

            ld, dve, pool = rsem("ld_route"), rsem("dve_chain"), rsem("pool_chain")
            var_ok, std_ok, ones_ok = rsem("var_ready"), rsem("std_ready"), rsem("ones_ready")
            xs_ok, xT_ok, xsT_ok, lg_ok = rsem("xs_ready"), rsem("xT_in_psum"), rsem("xsT_ready"), rsem("logits_ready")
            rows_ok, shift_ok, ex_ok = rsem("rows_ready"), rsem("shifted_ready"), rsem("exp_ready")
            oh_ok, pre_ok, rank_ok = rsem("onehot_ready"), rsem("prefix_ready"), rsem("rank_ready")
            pick_ok, scattered = rsem("picks_ready"), rsem("scattered")
            rstd_ok = rsem("rstd_ready")
            part_ok, split_ok = rsem("bias_part_ready"), rsem("bias_rest_ready")

            blk = rctx.enter_context(nc.Block())

            @blk.sync
            def _(sp):
                sp.dma_start(wg[:, :, :], io["wg" + tag].rearrange("(k c) e -> c k e", k=KD)).then_inc(ld, 16)
                if K == 1:
                    sp.dma_start(bg[:, :], io["bg" + tag].partition_broadcast(P)).then_inc(ld, 16)
                sp.dma_start(iota[:, :, :], io["iota_e"].partition_broadcast(P)).then_inc(ld, 16)
                sp.dma_start(iota_t[:, :], io["iota_t"][0:NT].partition_broadcast(P)).then_inc(ld, 16)
                sp.dma_start(owner[:, :], io["bias_owner"]).then_inc(ld, 16)
                sp.dma_start(bf[:, :], io["b2_rows" + tag]).then_inc(ld, 16)
                sp.dma_start(b1T[:, :, :], io["b1T_" + tag]).then_inc(ld, 16)
                if K == 1:
                    for e in range(E):
                        sp.dma_start(keep.w2[:, e, :, :], io["w2_" + tag][e].rearrange("(k c) n -> c k n", k=KF)).then_inc(keep.ld_w2, 16)

            LOADS = 16 * (7 if K == 1 else 6)

            @blk.gpsimd
            def _(gp):
                gp.wait_ge(rstd_ok, 1)
                gp.tensor_tensor(rows[:, :, :], keep.x1[:, :, :], mean[:, :].unsqueeze(2).to_broadcast([P, T, D]), ALU.subtract).then_inc(rows_ok, 1)
                gp.wait_ge(rows_ok, 1)
                gp.tensor_tensor(rows[:, :, :], rows[:, :, :], rstd[:, :].unsqueeze(2).to_broadcast([P, T, D]), ALU.mult).then_inc(rows_ok, 1)
                for q in range(1, 3):
                    gp.wait_ge(part_ok, q)
                    gp.tensor_tensor(bf[:, :], bf[:, :], bx[:, :], ALU.subtract).then_inc(split_ok, 1)
                gp.wait_ge(pick_ok, 1)
                gp.wait_ge(rows_ok, 2)
                gp.wait_ge(keep.zeroed[tag], 16 * keep.zero_loads[tag])
                for c in range(V):
                    gp.indirect_dma_start(xslots, bass.IndirectOffsetOnAxis(ap=picks[:, c:c + 1], axis=0), rows[:, c % T, :], None,
                                          bounds_check=NT * P - 1, oob_is_err=False).then_inc(scattered, 16)
                gp.wait_ge(scattered, 16 * V)

            @blk.scalar
            def _(act):
                act.wait_ge(var_ok, 1)
                nc.scalar.activation(rstd[:, :], tmp[:, 0, :], ACT.Sqrt).then_inc(std_ok, 1)
                with act.Fori(0, T // 2) as i:
                    for u in range(2):
                        act.wait_ge(xT_ok, i * 2 + (u + 1))
                        nc.scalar.activation(xsT[:, u, :, :], xT_bank[u][:, 0:D].rearrange("p (k n) -> p k n", k=KD), ACT.Copy).then_inc(xsT_ok, 1)
                act.wait_ge(ld, LOADS)
                for q in range(3):
                    wait(act, split_ok, q, q)
                    r = slice(0, (P, 64, 32)[q])
                    nc.scalar.activation(bx[r, :], bf[r, :], ACT.Copy).then_inc(part_ok, 1)
                act.wait_ge(shift_ok, 1)
                shifted = ex[:, :, :] if K == 1 else ex[:, :, 0]
                nc.scalar.activation(shifted, shifted, ACT.Exp).then_inc(ex_ok, 1)

            @blk.tensor
            def _(pe):
                def slot(t, at):
                    u = at % 2
                    if at < T:
                        pe.wait_ge(xs_ok, t + 1)
                        wait(pe, xsT_ok, t - 1, at - 1)
                        for k in range(KD):
                            mm = nc.tensor.transpose(xT_bank[u][:, k * P:(k + 1) * P], xs[:, u, k * P:(k + 1) * P], keep.ident[:, :])
                        mm.then_inc(xT_ok, 1)
                    if at >= 1:
                        if at == 1:
                            pe.wait_ge(ld, LOADS)
                        pe.wait_ge(xsT_ok, t)
                        for k in range(KD):
                            mm = nc.tensor.matmul(lg_bank[:, bass.ds((t - 1) * E, E)], xsT[:, 1 - u, k, :], wg[:, k, :],
                                                  start=(k == 0), stop=(k == KD - 1))
                        mm.then_inc(lg_ok, 1)
                pipeline(pe, slot, 0, 2, T, T)
                pe.wait_ge(oh_ok, 1)
                nc.tensor.matmul(rank_bank[:, 0:V * E], keep.ustrict[:, :], oh[:, :, :].rearrange("p v e -> p (v e)"), start=True, stop=False)
                pe.wait_ge(pre_ok, 1)
                pe.wait_ge(ones_ok, 1)
                nc.tensor.matmul(rank_bank[:, 0:V * E], keep.ones[:, :], pre[1][:, :, :].rearrange("p v e -> p (v e)"), start=False, stop=True).then_inc(rank_ok, 1)
                nc.tensor.matmul(cnt_bank[:, 0:E], keep.ones[:, :], pre[1][:, V - 1, :], start=True, stop=False)
                nc.tensor.matmul(cnt_bank[:, 0:E], keep.ones[:, :], oh[:, V - 1, :], start=False, stop=True).then_inc(rank_ok, 1)

            @blk.vector
            def _(v):
                done = [0]

                def link(ins):
                    done[0] += 1
                    ins.then_inc(dve, 1)
                    v.wait_ge(dve, done[0])

                def e_cols(a):
                    return a.unsqueeze(2).to_broadcast([P, T, E])

                def over_t(a, n=T):
                    return a.unsqueeze(1).to_broadcast([P, n, E])

                v.memset(keep.ones[:, :], 1.0).then_inc(ones_ok, 1)
                done[0] = norm_from_stats(v, 0, dve, keep.stats, tmp, mean, rstd)
                v.wait_ge(dve, done[0])
                v.sem_inc(var_ok, 1)
                v.wait_ge(std_ok, 1)
                link(v.reciprocal(rstd[:, :], rstd[:, :]))
                v.sem_inc(rstd_ok, 1)

                def slot(t, at):
                    wait(v, xT_ok, t - 1, at - 1)
                    v.tensor_scalar(xs[:, at % 2, :], row(keep.x1, t), mean[:, bass.ds(t, 1)], rstd[:, bass.ds(t, 1)], ALU.subtract, ALU.mult).then_inc(xs_ok, 1)
                pipeline(v, slot, 0, 2, T, T - 1)

                v.wait_ge(lg_ok, T)
                v.wait_ge(ld, LOADS)
                logits = lg_bank[:, 0:T * E].rearrange("p (t e) -> p t e", e=E)
                link(v.tensor_tensor(lg[:, :, :], logits, over_t(bg[:, :]), ALU.add) if K == 1 else v.tensor_copy(lg[:, :, :], logits))
                for c in range(K):
                    o = oh[:, c * T:(c + 1) * T, :]
                    link(v.reduce_max(lmax[:, c, :], lg[:, :, :], AX))
                    link(v.tensor_tensor(o, lg[:, :, :], e_cols(lmax[:, c, :]), ALU.is_equal))
                    link(v.tensor_tensor(o, o, over_t(iota[:, 0, :]), ALU.mult))
                    link(v.tensor_reduce(first[:, :], o, AX, ALU.min))
                    link(v.tensor_tensor(o, e_cols(first[:, :]), over_t(iota[:, 0, :]), ALU.is_equal))
                    if c == 0:
                        if K == 1:
                            v.tensor_tensor(ex[:, :, :], lg[:, :, :], e_cols(lmax[:, 0, :]), ALU.subtract).then_inc(shift_ok, 1)
                        else:
                            link(v.scalar_tensor_tensor(lg[:, :, :], o, LOWEST, lg[:, :, :], ALU.mult, ALU.add))
                if K == 2:
                    v.tensor_tensor(ex[:, :, 0], lmax[:, 1, :], lmax[:, 0, :], ALU.subtract).then_inc(shift_ok, 1)
                v.sem_inc(oh_ok, 1)
                cur, w, n = oh, 1, 0
                while w < V:
                    dst = pre[n % 2]
                    v.tensor_copy(dst[:, 0:w, :], cur[:, 0:w, :]).then_inc(dve, 1)
                    v.tensor_tensor(dst[:, w:V, :], cur[:, w:V, :], cur[:, 0:V - w, :], ALU.add).then_inc(dve, 1)
                    done[0] += 2
                    v.wait_ge(dve, done[0])
                    cur = dst
                    w *= 2
                    n += 1
                other = pre[n % 2]
                link(v.tensor_tensor(other[:, :, :], cur[:, :, :], oh[:, :, :], ALU.subtract))
                if other is not pre[1]:
                    link(v.tensor_copy(pre[1][:, :, :], other[:, :, :]))
                v.sem_inc(pre_ok, 1)
                v.wait_ge(rank_ok, 2)
                link(v.tensor_scalar(cnt[:, :], cnt_bank[:, 0:E], float(P - 1), None, ALU.add))
                link(v.tensor_copy(cnti[:, :], cnt[:, :]))
                link(v.tensor_scalar(cnti[:, :], cnti[:, :], 7, None, ALU.arith_shift_right))
                link(v.tensor_copy(cnt[:, :], cnti[:, :]))
                cur, w, n = cnt, 1, 0
                while w < E:
                    dst = ends[n % 2]
                    v.tensor_copy(dst[:, 0:w], cur[:, 0:w]).then_inc(dve, 1)
                    v.tensor_tensor(dst[:, w:E], cur[:, w:E], cur[:, 0:E - w], ALU.add).then_inc(dve, 1)
                    done[0] += 2
                    v.wait_ge(dve, done[0])
                    cur, w, n = dst, 2 * w, n + 1
                tends = cur
                link(v.tensor_tensor(base[:, :], tends[:, :], cnt[:, :], ALU.subtract))
                link(v.tensor_scalar(base[:, :], base[:, :], float(P), None, ALU.mult))
                link(v.tensor_tensor(pre[0][:, :, :], rank_bank[:, 0:V * E].rearrange("p (v e) -> p v e", e=E), over_t(base[:, :], V), ALU.add))
                link(v.tensor_tensor(pre[0][:, :, :], pre[0][:, :, :], oh[:, :, :], ALU.mult))
                link(v.reduce_sum(slotf[:, :], pre[0][:, :, :], AX))
                v.tensor_copy(picks[:, :], slotf[:, :]).then_inc(pick_ok, 1)
                v.wait_ge(ex_ok, 1)
                gate = keep.gate[:, gate_col:gate_col + 1]
                if K == 1:
                    link(v.reduce_sum(first[:, :], ex[:, :, :], AX))
                    link(v.reciprocal(first[:, :], first[:, :]))
                    v.tensor_scalar(prob[:, 0:T], first[:, :], gate, None, ALU.mult).then_inc(dve, 1)
                    done[0] += 1
                else:
                    link(v.tensor_scalar(first[:, :], ex[:, :, 0], 1.0, None, ALU.add))
                    link(v.reciprocal(first[:, :], first[:, :]))
                    link(v.tensor_scalar(prob[:, 0:T], first[:, :], gate, None, ALU.mult))
                    v.tensor_tensor(prob[:, T:2 * T], prob[:, 0:T], ex[:, :, 0], ALU.mult).then_inc(dve, 1)
                    done[0] += 1
                link(v.tensor_tensor(past[:, :, :], iota_t[:, :].unsqueeze(2).to_broadcast([P, NT, E]), over_t(tends[:, :], NT), ALU.is_ge))
                link(v.reduce_sum(tef[:, :], past[:, :, :], AX))
                link(v.tensor_scalar(tef[:, :], tef[:, :], float(E - 1), None, ALU.min))
                v.tensor_copy(tile_expert[:, :], tef[:, :]).then_inc(dve, 1)
                v.tensor_scalar(hot[:, :, :], tef[0:BP, :].unsqueeze(2).to_broadcast([BP, NT, P]), owner[:, 0:1], None, ALU.is_equal).then_inc(dve, 1)
                v.wait_ge(dve, done[0] + 2)

        with ExitStack() as ectx:
            def eb(name, shape, dt=F32):
                return ectx.enter_context(nc.sbuf_tensor(f"{name}{tag}", shape, dt))

            def esem(name):
                return keep.sems.new(f"{name}{tag}")

            xb, ys = rows[:, T - 2:T, :], rows[:, T - 4:T - 2, :]
            xT = eb("slotT", [P, 2, KD, P])
            w1, b1 = eb("w1_tile", [P, 2, KD, F]), eb("b1_tile", [P, 2, KF])
            hT = eb("hiddenT", [P, 2, KF, P])
            h_ps = [ectx.enter_context(nc.psum_tensor(f"h_ps{tag}{i}", [P, 2, 512], F32)) for i in range(2)]
            x_ps = ectx.enter_context(nc.psum_tensor(f"x_ps{tag}", [P, 512], F32))
            y_ps = [ectx.enter_context(nc.psum_tensor(f"y_ps{tag}{i}", [P, 512], F32)) for i in range(2)]
            ld = [esem(f"slot_rows_{i}") for i in range(2)]
            stored = [esem(f"y_stored_{i}") for i in range(2)]
            xT_ok, xTs_ok, h_ok, act_ok = esem("x_in_psum"), esem("slotT_ready"), esem("h_in_psum"), esem("hidden_ready")
            w1_ok, b1_ok, y_ok, ys_ok = (esem(n) for n in ("w1_tile_ready", "b1_tile_ready", "y_in_psum", "y_ready"))
            ALL = NT
            EVEN = NT - NT % 2
            LASTF = EVEN - 2 if EVEN == NT else EVEN - 1
            BPB = KF // 2

            side = StatePowers(nc, keep, rows) if K == 1 else None
            blk = ectx.enter_context(nc.Block())

            @blk.sync
            def _(sp):
                def slot(t, at):
                    u = at % 2
                    if at >= 4:
                        sp.wait_ge(ys_ok, t - 3)
                        sp.dma_start(yslots[bass.ds(t * P - 4 * P, P), :], ys[:, u, :]).then_inc(stored[u], 16)
                    if at < ALL:
                        wait(sp, xT_ok, t - 1, at - 1)
                        sp.dma_start(xb[:, u, :], xslots[bass.ds(t * P, P), :]).then_inc(ld[u], 16)
                pipeline(sp, slot, 0, 4, EVEN, ALL + 3)
                sp.wait_ge(stored[0], 16 * ((ALL + 1) // 2))
                sp.wait_ge(stored[1], 16 * (ALL // 2))

            @blk.gpsimd
            def _(gp):
                if side:
                    side.load(gp, io)
                    side.powers(gp)

            @blk.scalar
            def _(act):
                def slot(t, at):
                    if at + 1 < ALL:
                        act.wait_ge(xT_ok, t + 2)
                        wait(act, h_ok, t * 2, at * 2)
                        nc.scalar.activation(xT[:, (at + 1) % 2, :, :], x_ps[:, 0:D].rearrange("p (k n) -> p k n", k=KD), ACT.Copy).then_inc(xTs_ok, 1)
                    if 0 <= at < ALL:
                        u = at % 2
                        act.wait_ge(b1_ok, t + 1)
                        wait(act, y_ok, t - 1, at - 1)
                        for m in range(KF):
                            if m % BPB == 0:
                                act.wait_ge(h_ok, t * 2 + (m // BPB + 1))
                            x = nc.scalar.activation(hT[:, u, m, :], h_ps[u][:, m // BPB, (m % BPB) * P:(m % BPB + 1) * P], act_fn, bias=b1[:, u, m:m + 1])
                        x.then_inc(act_ok, 1)
                pipeline(act, slot, -1, 3, LASTF, ALL - 1)

            @blk.tensor
            def _(pe):
                if K == 1:
                    pe.wait_ge(keep.ld_w1, 16 * E)
                else:
                    pe.wait_ge(keep.ld_w1, 16 * 2 * E)
                    pe.wait_ge(keep.ld_w2, 16 * 2 * E)

                def slot(t, at):
                    if at + 1 < ALL:
                        u = (at + 1) % 2
                        pe.wait_ge(ld[u], ((t + 1) // 2 + 1) * 16)
                        wait(pe, xTs_ok, t + 1, at + 1)
                        for k in range(KD):
                            mm = nc.tensor.transpose(x_ps[:, k * P:(k + 1) * P], xb[:, u, k * P:(k + 1) * P], keep.ident[:, :])
                        mm.then_inc(xT_ok, 1)
                    if 0 <= at < ALL:
                        u = at % 2
                        pe.wait_ge(xTs_ok, t + 1)
                        pe.wait_ge(w1_ok, t + 1)
                        wait(pe, act_ok, t - 1, at - 1)
                        for m in range(KF):
                            for k in range(KD):
                                mm = nc.tensor.matmul(h_ps[u][:, m // BPB, (m % BPB) * P:(m % BPB + 1) * P], w1[:, u, k, m * P:(m + 1) * P], xT[:, u, k, :],
                                                      start=(k == 0), stop=(k == KD - 1))
                            if m % BPB == BPB - 1:
                                mm.then_inc(h_ok, 1)
                    if 1 <= at <= ALL:
                        u = (at - 1) % 2
                        e = pe.value_load(tile_expert[0:1, bass.ds(t - 1, 1)], min_val=0, max_val=E - 1)
                        if at == 1 and K == 1:
                            pe.wait_ge(keep.ld_w2, 16 * E)
                        pe.wait_ge(act_ok, t)
                        wait(pe, ys_ok, t - 2, at - 2)
                        for k in range(KF):
                            nc.tensor.matmul(y_ps[u][:, 0:D], hT[:, u, k, :], keep.w2[:, bass.ds(e, 1), k, :].rearrange("p a n -> p (a n)"),
                                             start=(k == 0), stop=False)
                        mm = nc.tensor.matmul(y_ps[u][:, 0:D], hot[:, bass.ds(t - 1, 1), :].rearrange("p a n -> p (a n)"), bx[0:BP, :], start=False, stop=True)
                        mm.then_inc(y_ok, 1)
                pipeline(pe, slot, -1, 3, LASTF, ALL)

            @blk.vector
            def _(v):
                v.wait_ge(keep.ld_w1, 16 * E if K == 1 else 16 * 2 * E)

                def slot(t, at):
                    if side and at == 2:
                        side.inverse_square(v)
                    if at + 1 < ALL:
                        u = (at + 1) % 2
                        e = v.value_load(tile_expert[0:1, bass.ds(t + 1, 1)], min_val=0, max_val=E - 1)
                        wait(v, h_ok, t * 2, at * 2)
                        v.tensor_copy(w1[:, u, :, :], keep.w1[:, bass.ds(e, 1), :, :].rearrange("p a k n -> p (a k) n")).then_inc(w1_ok, 1)
                        wait(v, act_ok, t, at)
                        v.tensor_copy(b1[:, u, :], b1T[:, bass.ds(e, 1), :].rearrange("p a k -> p (a k)")).then_inc(b1_ok, 1)
                    if 1 <= at <= ALL:
                        u = (at - 1) % 2
                        v.wait_ge(y_ok, t)
                        if at >= 3:
                            v.wait_ge(stored[u], ((t - 1) // 2) * 16)
                        v.tensor_copy(ys[:, u, :], y_ps[u][:, 0:D]).then_inc(ys_ok, 1)
                pipeline(v, slot, -1, 3, LASTF, ALL)

        with ExitStack() as gctx:
            more = [gctx.enter_context(nc.sbuf_tensor(f"second{tag}", [P, T, D], F32))] if K == 2 else []
            got = [rows, *more]
            new = keep.sems.new
            gathered = [new(f"gathered{tag}_{c}") for c in range(V)]
            added, stat, written = new(f"added{tag}"), new(f"row_stats{tag}"), new(f"written{tag}")
            blk = gctx.enter_context(nc.Block())

            @blk.gpsimd
            def _(gp):
                for t in range(T):
                    for c in range(K):
                        gp.indirect_dma_start(got[c][:, t, :], None, yslots,
                                              bass.IndirectOffsetOnAxis(ap=picks[:, c * T + t:c * T + t + 1], axis=0),
                                              bounds_check=NT * P - 1, oob_is_err=False).then_inc(gathered[c * T + t], 16)

            @blk.vector
            def _(v):
                for t in range(T):
                    for c in range(K):
                        v.wait_ge(gathered[c * T + t], 16)
                        wait(v, added, K * t + c, K * t + c if c else 0)
                        v.scalar_tensor_tensor(keep.x1[:, t, :], got[c][:, t, :], prob[:, c * T + t:c * T + t + 1], keep.x1[:, t, :],
                                               ALU.mult, ALU.add).then_inc(added, 1)
                    if K == 1:
                        v.wait_ge(added, t + 1)
                        v.bn_stats(keep.stats[:, t, :], keep.x1[:, t, :]).then_inc(stat, 1)

            if out is not None:
                @blk.sync
                def _(sp):
                    rows_out = out.rearrange("(n p) d -> p n d", p=P)
                    for t in range(T):
                        sp.wait_ge(added, K * (t + 1))
                        sp.dma_start(rows_out[:, t, :], keep.x1[:, t, :]).then_inc(written, 16)
                    sp.wait_ge(written, 16 * T)


H1 = 4
DQ = 128
DH1 = DQ // H1
TOP = 32
MOVED = -3.0e38


class ConvKernel:

    CH, PART = 16, 8
    NB, NA = 32, S // 32
    SLOTS = P // 8

    def __init__(self, nc, io, keep, c, sb):
        CH, PART, NB, NA = self.CH, self.PART, self.NB, self.NA
        self.nc, self.keep, self.dram = nc, keep, c.kernel_dram
        self.low, self.high = sb("z_low", [P, 2, 2 * CH, NB]), sb("z_high", [P, 2, 2 * CH, NA])
        self.prod = [sb(f"z_products{i}", [P, 2, CH, NB // 2]) for i in range(2)]
        self.mov = [sb(f"z_low_part{i}", [P, 2, PART, NB]) for i in range(2)]
        self.sta = [sb(f"z_high_part{i}", [P, 3, PART, 2, NA]) for i in range(2)]
        self.kout = [sb(f"k_out{i}", [2 * NA, PART, NB]) for i in range(2)]
        self.chain, self.tab_ok, self.staged, self.mm_ok = (keep.sems.new(n) for n in ("table_chain", "table_ready", "part_laid_out", "k_in_psum"))
        self.turn_ok = keep.sems.new("product_turns")
        self.out_ok, self.zero_ok = keep.sems.new("k_ready"), keep.sems.new("blocks_zeroed")
        self.stored = [keep.sems.new(f"k_stored{i}") for i in range(2)]

    def tables(self, gp):
        CH, NB, NA = self.CH, self.NB, self.NA
        n = 0
        for u in range(2):
            gp.memset(self.sta[u][:, :, :, :, :], 0.0).then_inc(self.zero_ok, 1)
        for turn in range(P // CH):
            sl = slice(turn * CH, turn * CH + CH)
            at = (turn % 2) * CH
            low, high = self.low[:, :, at:at + CH, :], self.high[:, :, at:at + CH, :]

            def step(*ins):
                nonlocal n
                for y in ins:
                    y.then_inc(self.chain, 1)
                n += len(ins)
                gp.wait_ge(self.chain, n)

            def grow(tab, width, j0):
                x, j = 1, j0
                while x < width:
                    re, im = (self.keep.z[:, i, j, sl].unsqueeze(1).unsqueeze(3).to_broadcast([P, 2, CH, x]) for i in range(2))
                    by_re, by_im = (q[:, :, :, 0:x] for q in self.prod)
                    have = tab[:, :, :, 0:x]
                    step(gp.tensor_tensor(by_re, have, re, ALU.mult), gp.tensor_tensor(by_im, have, im, ALU.mult))
                    step(gp.tensor_tensor(tab[:, 0, :, x:2 * x], by_re[:, 0], by_im[:, 1], ALU.subtract),
                         gp.tensor_tensor(tab[:, 1, :, x:2 * x], by_re[:, 1], by_im[:, 0], ALU.add))
                    x, j = 2 * x, j + 1

            if turn >= 2:
                gp.wait_ge(self.staged, (turn - 1) * (CH // self.PART))
            step(gp.memset(low[:, 0, :, 0:1], 1.0), gp.memset(low[:, 1, :, 0:1], 0.0), gp.tensor_copy(high[:, :, :, 0], self.keep.dc[:, :, sl]))
            grow(low, NB, 0)
            grow(high, NA, 5)
            gp.sem_inc(self.tab_ok, 1)

    def stage(self, act, k, at):
        u = at % 2
        a = self.nc.scalar.activation
        ring = bass.ds((k % (2 * self.CH // self.PART)) * self.PART, self.PART)
        act.wait_ge(self.tab_ok, k // (self.CH // self.PART) + 1)
        if at == 0:
            act.wait_ge(self.zero_ok, 2)
        wait(act, self.mm_ok, k - 1, at - 1)
        a(self.mov[u][:, :, :, :], self.low[:, :, ring, :], ACT.Copy)
        for h in range(2):
            q = slice(64 * h, 64 * h + 64)
            a(self.sta[u][q, 0:2, :, h, :], self.high[q, :, ring, :], ACT.Copy)
            x = a(self.sta[u][q, 2, :, h, :], self.high[q, 1, ring, :], ACT.Copy, scale=-1.0)
        x.then_inc(self.staged, 1)

    def product(self, pe, k, at):
        u = at % 2
        pe.wait_ge(self.staged, k + 1)
        wait(pe, self.out_ok, k, at)
        pe.sem_inc(self.turn_ok, 1)
        for d in range(self.PART):
            o = self.bank[0:2 * self.NA, D + d * self.NB:D + (d + 1) * self.NB]
            self.nc.tensor.matmul(o, self.sta[u][:, 0, d, :, :].rearrange("p h a -> p (h a)"), self.mov[u][:, 0, d, :], start=True, stop=False)
            mm = self.nc.tensor.matmul(o, self.sta[u][:, 2, d, :, :].rearrange("p h a -> p (h a)"), self.mov[u][:, 1, d, :], start=False, stop=True)
        mm.then_inc(self.mm_ok, 1)

    def evacuate(self, act, k, at):
        u = at % 2
        act.wait_ge(self.mm_ok, k + 1)
        if at >= 2:
            act.wait_ge(self.stored[u], (k // 2) * 32)
        self.nc.scalar.activation(self.kout[u][:, :, :], self.bank[0:2 * self.NA, D:2 * D].rearrange("p (d b) -> p d b", d=self.PART),
                                  ACT.Copy).then_inc(self.out_ok, 1)

    def store(self, sp):
        def slot(k, at):
            sp.wait_ge(self.out_ok, k + 1)
            for h in range(2):
                sp.dma_start(self.dram[bass.ds(k * self.PART + h * P, self.PART), :].rearrange("d (a b) -> a d b", a=self.NA),
                             self.kout[at % 2][h * self.NA:(h + 1) * self.NA, :, :]).then_inc(self.stored[at % 2], 16)
        pipeline(sp, slot, 0, 2, self.SLOTS, self.SLOTS - 1)
        for u in range(2):
            sp.wait_ge(self.stored[u], 16 * self.SLOTS)


def layer1_attention(nc, io, keep, c):
    with ExitStack() as ctx:
        def sb(name, shape, dt=F32):
            return ctx.enter_context(nc.sbuf_tensor(name, shape, dt))

        def bank(name):
            return ctx.enter_context(nc.psum_tensor(name, [P, 512], F32))

        sem = keep.sems.new

        NF = 4 * D
        ctxT = sb("ctxT1", [KC, 2, B * SK])
        wq, wk, wv = sb("wq1", [P, KD, DQ]), sb("wk1", [KC, 2, DQ]), sb("wv1", [KC, 2, D])
        wf = sb("w_film", [P, KD, NF])
        mask4 = sb("headmask32", [P, H1])
        kbd = sb("k1_blockdiag", [P, B, H1, SK])
        vT = sb("v1T", [P, KD, B * SK])
        vw = sb("v_film", [SK + 1, B, NF])
        modg = sb("mod_gate", [P, 1])
        g_in, b_in = sb("g_norm_in", [P, D]), sb("b_norm_in", [P, D])
        key_u8, key_bias = sb("key_mask_u8", [P, B * SK], U8), sb("key_bias", [P, B, SK])
        tok_u8, tok = sb("token_mask_u8", [P, T], U8), sb("token_mask", [P, T])
        tmp, mean, rstd, rstd2 = sb("tmp_c", [P, 4, T]), sb("mean_c", [P, T]), sb("rstd_c", [P, T]), sb("rstd2_c", [P, T])
        xs, xsT, qT = sb("xs_c", [P, 2, D]), sb("xsT_c", [P, KD, P]), sb("qT_c", [P, P])
        s, work = sb("s_c", [P, 2, H1, SK]), sb("work_c", [P, 2, H1, SK])
        best, neg = sb("best8", [P, 2, H1, 8]), sb("minus_max", [P, 2, H1])
        later = sb("later8", [P, H1, 8])
        e = sb("e_c", [P, 2, H1, SK])
        den, rden = sb("den_c", [P, H1]), sb("rden_c", [P, 2, H1])
        am, aT = sb("attn_mean", [P, P]), sb("attn_meanT", [SK + 1, P])
        xl = sb("xl_c", [P, D])
        vw_b = sb("film_offset", [SK + 1, B, D])
        ssm = ConvKernel(nc, io, keep, c, sb)
        s_ps = [bank(f"s1_{i}") for i in range(2)]
        m0, m1 = bank("c_m0"), bank("c_m1")
        f_ps = [ctx.enter_context(nc.psum_tensor(f"film_ps{i}", [P, 2, 512], F32)) for i in range(2)]

        ld, ld_f, ld_dft = sem("ld_c"), sem("ld_film"), sem("ld_dft")
        dve, pool, mm_ok = sem("dve_c"), sem("pool_c"), sem("setup_c")
        var_ok, std_ok, var2_ok, std2_ok = sem("var_c"), sem("std_c"), sem("var2_c"), sem("std2_c")
        kbd_ok, vT_ok, vw_ok = sem("kbd_c"), sem("vT_c"), sem("vw_c")
        xs_ok, rows_ok, xT_ok, xTs_ok, q_ok, qT_ok, s_ok, ssb_ok = (sem(n + "_c1") for n in ("xs", "rows", "xT", "xTs", "q", "qT", "s", "ssb"))
        best_ok, neg_ok, e_ok, em_ok, den_ok, inv_ok, rden_ok, er_ok, am_ok = (sem(n + "_c1") for n in ("best", "neg", "e", "em", "den", "inv", "rden", "er", "am"))
        aT_ok, aTs_ok, f_ok, fo_ok, xg_ok, xm_ok = (sem(n + "_c1") for n in ("aT", "aTs", "film", "film_out", "xg", "xm"))

        gate_ok = sem("top_steps")
        fold_ok, film_ok = sem("film_folded"), sem("film_steps")
        ssm.bank = m0
        KS = ssm.SLOTS
        blk = ctx.enter_context(nc.Block())

        @blk.sync
        def _(sp):
            for sm, dst, src in ((ld, ctxT[:, :, :], io["ctxT"].rearrange("(k c) n -> c k n", k=2)),
                                 (ld, wk[:, :, :], io["wk1"].rearrange("(k c) n -> c k n", k=2)),
                                 (ld, wq[:, :, :], io["wq1"].rearrange("(k c) n -> c k n", k=KD)),
                                 (ld, mask4[:, :], io["headmask32"]),
                                 (ld, key_u8[:, :], io["key_mask"].partition_broadcast(P)),
                                 (ld, tok_u8[:, :], io["token_mask"]),
                                 (ld_f, wv[:, :, :], io["wv1"].rearrange("(k c) n -> c k n", k=2)),
                                 (ld_f, wf[:, :, 0:2 * D], io["w_film_in"].rearrange("(k c) n -> c k n", k=KD)),
                                 (ld_f, wf[:, :, 2 * D:NF], io["w_film_out"].rearrange("(k c) n -> c k n", k=KD)),
                                 (ld_f, modg[:, :], io["mod_gate"].partition_broadcast(P)),
                                 (ld_f, vw[SK:SK + 1, 0, 0:2 * D], io["b_film_in"].unsqueeze(0)),
                                 (ld_f, vw[SK:SK + 1, 0, 2 * D:NF], io["b_film_out"].unsqueeze(0)),
                                 (ld_f, g_in[:, :], io["g_norm_in"].partition_broadcast(P)),
                                 (ld_f, b_in[:, :], io["b_norm_in"].partition_broadcast(P))):
                sp.dma_start(dst, src).then_inc(sm, 16)
            sp.dma_start(c.fwd[:, :, :], io["dft"].rearrange("(k p) f -> p k f", k=2)).then_inc(ld_dft, 16)
            sp.dma_start(c.inv[:, :, :], io["idft"].rearrange("(k p) t -> p k t", p=P)).then_inc(ld_dft, 16)
            sp.dma_start(c.sign[:, :], io["sign"]).then_inc(ld_dft, 16)
            sp.dma_start(c.dskip[:, :], io["d_skip"].partition_broadcast(P)).then_inc(ld_dft, 16)
            ssm.store(sp)
            sp.wait_ge(ld_dft, 64)

        LOADS, FILM_LOADS = 16 * 6, 16 * 8

        @blk.gpsimd
        def _(gp):
            ssm.tables(gp)

        @blk.scalar
        def _(act):
            act.wait_ge(var_ok, 1)
            nc.scalar.activation(rstd[:, :], tmp[:, 0, :], ACT.Sqrt).then_inc(std_ok, 1)
            act.wait_ge(var2_ok, 1)
            nc.scalar.activation(rstd2[:, :], tmp[:, 1, :], ACT.Sqrt).then_inc(std2_ok, 1)

            def film_products():
                act.wait_ge(ld_f, FILM_LOADS)
                for b in range(B):
                    for n in range(2):
                        act.wait_ge(mm_ok, 3 + 2 * b + n + 1)
                        nc.scalar.activation(vw[0:SK, b, n * 512:(n + 1) * 512], f_ps[b % 2][0:SK, n, :], ACT.Copy, scale=modg[0:SK, 0:1]).then_inc(vw_ok, 1)

            def slot(t, at):
                if at == 0:
                    film_products()
                if 0 <= at - 1 < KS:
                    ssm.stage(act, t - 1, at - 1)
                if 0 <= at + 1 < T:
                    act.wait_ge(xT_ok, t + 2)
                    wait(act, q_ok, t + 1, at + 1)
                    nc.scalar.activation(xsT[:, :, :], m0[:, 0:D].rearrange("p (k n) -> p k n", k=KD), ACT.Copy).then_inc(xTs_ok, 1)
                if 0 <= at - 2 < KS:
                    ssm.evacuate(act, t - 2, at - 2)
                if 0 <= at - 2 < T:
                    act.wait_ge(aT_ok, t - 1)
                    wait(act, f_ok, t - 2, at - 2)
                    nc.scalar.activation(aT[0:SK, :], m1[0:SK, 0:P], ACT.Copy).then_inc(aTs_ok, 1)
                if 0 <= at + 1 < T:
                    act.wait_ge(q_ok, t + 2)
                    wait(act, s_ok, t + 1, at + 1)
                    nc.scalar.activation(qT[:, :], m0[:, 0:P], ACT.Copy).then_inc(qT_ok, 1)
                if 0 <= at < T:
                    u = at % 2
                    act.wait_ge(neg_ok, t + 1)
                    wait(act, er_ok, t - 1, at - 1)
                    wait(act, am_ok, t - 1, at - 1)
                    for h in range(H1):
                        x = nc.scalar.activation(e[:, u, h, :], s[:, u, h, :], ACT.Exp, bias=neg[:, u, h:h + 1])
                    x.then_inc(e_ok, 1)
                if 0 <= at - 2 < T:
                    act.wait_ge(f_ok, t - 1)
                    nc.scalar.activation(row(c.film, t - 2), f_ps[at % 2][:, 1, :], ACT.Copy).then_inc(fo_ok, 1)
            pipeline(act, slot, -1, 5, T - 1, T + 2)

        @blk.tensor
        def _(pe):
            pe.wait_ge(ld, LOADS)
            for k in range(2):
                mm = nc.tensor.matmul(s_ps[0][:, 0:B * SK], wk[:, k, :], ctxT[:, k, :], start=(k == 0), stop=(k == 1))
            mm.then_inc(mm_ok, 1)
            pe.wait_ge(kbd_ok, B)

            def film_products():
                pe.wait_ge(ld_f, FILM_LOADS)
                for m in range(KD):
                    for k in range(2):
                        mm = nc.tensor.matmul((s_ps[1], m1)[m][:, 0:B * SK], wv[:, k, m * P:(m + 1) * P], ctxT[:, k, :], start=(k == 0), stop=(k == 1))
                    mm.then_inc(mm_ok, 1)
                pe.wait_ge(vT_ok, 2)
                for b in range(B):
                    wait(pe, vw_ok, 2 * (b - 1), 2 * (b - 1))
                    for n in range(2):
                        for k in range(KD):
                            mm = nc.tensor.matmul(f_ps[b % 2][0:SK, n, :], vT[:, k, b * SK:(b + 1) * SK], wf[:, k, n * 512:(n + 1) * 512],
                                                  start=(k == 0), stop=(k == KD - 1))
                        mm.then_inc(mm_ok, 1)

            def slot(t, at):
                if at == 0:
                    film_products()
                if at == 2:
                    pe.wait_ge(fold_ok, 1)
                if 0 <= at - 2 < KS:
                    wait(pe, qT_ok, t + 1 if at < T else T, at + 1)
                    ssm.product(pe, t - 2, at - 2)
                if 0 <= at + 1 < T:
                    u = (at + 1) % 2
                    pe.wait_ge(xs_ok, t + 2)
                    wait(pe, qT_ok, t + 1, at + 1)
                    for k in range(KD):
                        mm = nc.tensor.transpose(m0[:, k * P:(k + 1) * P], xs[:, u, k * P:(k + 1) * P], keep.ident[:, :])
                    mm.then_inc(xT_ok, 1)
                if 0 <= at - 2 < T:
                    pe.wait_ge(am_ok, t - 1)
                    wait(pe, aTs_ok, t - 2, at - 2)
                    nc.tensor.transpose(m1[:, 0:P], am[:, :], keep.ident[:, :]).then_inc(aT_ok, 1)
                if 0 <= at + 1 < T:
                    pe.wait_ge(xTs_ok, t + 2)
                    if 0 <= at - 2 < KS:
                        pe.wait_ge(ssm.out_ok, t - 1)
                    for k in range(KD):
                        mm = nc.tensor.matmul(m0[:, 0:P], wq[:, k, :], xsT[:, k, :], start=(k == 0), stop=(k == KD - 1))
                    mm.then_inc(q_ok, 1)
                if 0 <= at - 2 < T:
                    pe.wait_ge(aTs_ok, t - 1)
                    wait(pe, fo_ok, t - 3, at - 3)
                    wait(pe, xm_ok, t - 3, at - 3)
                    for n in range(2):
                        mm = nc.tensor.matmul(f_ps[at % 2][:, n, :], aT[:, :], vw[:, bass.ds((t - 2) // TB, 1), n * 512:(n + 1) * 512].rearrange("p a n -> p (a n)"),
                                              start=True, stop=True)
                    mm.then_inc(f_ok, 1)
                if 0 <= at + 1 < T:
                    pe.wait_ge(qT_ok, t + 2)
                    wait(pe, ssb_ok, t, at)
                    nc.tensor.matmul(s_ps[(at + 1) % 2][:, 0:H1 * SK], qT[:, :], kbd[:, bass.ds((t + 1) // TB, 1), :, :].rearrange("p a h s -> p (a h s)"),
                                     start=True, stop=True).then_inc(s_ok, 1)
            pipeline(pe, slot, -1, 5, T - 1, T + 2)

        @blk.vector
        def _(v):
            done = [0]

            def link(ins):
                done[0] += 1
                ins.then_inc(dve, 1)
                v.wait_ge(dve, done[0])

            done[0] = norm_from_stats(v, 0, dve, keep.stats, tmp, mean, rstd)
            v.wait_ge(dve, done[0])
            v.sem_inc(var_ok, 1)
            v.wait_ge(std_ok, 1)
            link(v.reciprocal(rstd[:, :], rstd[:, :]))
            link(v.tensor_tensor(tmp[:, 1, :], rstd[:, :], rstd[:, :], ALU.mult))
            link(v.tensor_scalar(tmp[:, 1, :], tmp[:, 1, :], -EPS, 1.0 + EPS, ALU.mult, ALU.add))
            v.sem_inc(var2_ok, 1)
            v.wait_ge(ld, LOADS)
            v.wait_ge(std2_ok, 1)
            link(v.reciprocal(rstd2[:, :], rstd2[:, :]))
            link(v.tensor_copy(key_bias[:, :, :].rearrange("p b s -> p (b s)"), key_u8[:, :]))
            link(v.tensor_scalar(key_bias[:, :, :], key_bias[:, :, :], 1.0, 3.0e38, ALU.subtract, ALU.mult))
            link(v.tensor_scalar(key_bias[:, :, :], key_bias[:, :, :], 10.0, None, ALU.mult))
            link(v.tensor_copy(tok[:, :], tok_u8[:, :]))
            link(v.tensor_scalar(tok[:, :], tok[:, :], 1.0 / H1, None, ALU.mult))
            v.wait_ge(mm_ok, 1)
            link(v.tensor_copy(vT[:, 0, :], s_ps[0][:, 0:B * SK]))
            for b in range(B):
                v.tensor_tensor(kbd[:, b, :, :], vT[:, 0, b * SK:(b + 1) * SK].unsqueeze(1).to_broadcast([P, H1, SK]),
                                mask4[:, :].unsqueeze(2).to_broadcast([P, H1, SK]), ALU.mult).then_inc(kbd_ok, 1)
            v.memset(aT[SK:SK + 1, :], 1.0).then_inc(dve, 1)
            v.memset(am[:, SK:P], 0.0).then_inc(dve, 1)
            done[0] += 2
            v.wait_ge(dve, done[0])
            D0 = done[0]

            def film_values():
                v.wait_ge(kbd_ok, B)
                for m in range(KD):
                    v.wait_ge(mm_ok, 2 + m)
                    v.tensor_copy(vT[:, m, :], (s_ps[1], m1)[m][:, 0:B * SK]).then_inc(vT_ok, 1)

            def film_bias():
                def fold(ins, n):
                    ins.then_inc(film_ok, 1)
                    v.wait_ge(film_ok, n)

                bias = vw[SK:SK + 1, :, :].rearrange("p b (n d) -> p b n d", d=D)
                v.wait_ge(ld_f, FILM_LOADS)
                fold(v.tensor_scalar(bias[:, 0, :, :], bias[:, 0, :, :], modg[SK:SK + 1, 0:1], None, ALU.mult), 1)
                for n in (0, 2):
                    fold(v.tensor_scalar(bias[:, 0, n, :], bias[:, 0, n, :], 1.0, None, ALU.add), 2 + n // 2)
                for b in range(1, B):
                    fold(v.tensor_copy(vw[SK:SK + 1, b, :], vw[SK:SK + 1, 0, :]), 3 + b)
                v.wait_ge(vw_ok, 2 * B)

                def g_rows(a):
                    return a[0:SK + 1, :].unsqueeze(1).to_broadcast([SK + 1, B, D])
                fold(v.tensor_tensor(vw_b[:, :, :], vw[:, :, 0:D], g_rows(b_in), ALU.mult), B + 3)
                fold(v.tensor_tensor(vw[:, :, D:2 * D], vw[:, :, D:2 * D], vw_b[:, :, :], ALU.add), B + 4)
                fold(v.tensor_tensor(vw[:, :, 0:D], vw[:, :, 0:D], g_rows(g_in), ALU.mult), B + 5)
                v.sem_inc(fold_ok, 1)
            PER = 7

            def slot(t, at):
                if at == 0:
                    film_values()
                if at == 1:
                    film_bias()
                if 0 <= at + 1 < T:
                    wait(v, xT_ok, t, at)
                    v.tensor_scalar(xs[:, (at + 1) % 2, :], row(keep.x1, t + 1), mean[:, bass.ds(t + 1, 1)], rstd[:, bass.ds(t + 1, 1)], ALU.subtract, ALU.mult).then_inc(xs_ok, 1)
                    v.tensor_scalar(row(c.rows, t + 1), row(keep.x1, t + 1), mean[:, bass.ds(t + 1, 1)], rstd[:, bass.ds(t + 1, 1)], ALU.subtract, ALU.mult).then_inc(rows_ok, 1)

                p = (at - 1) % 2
                prev, mod = 0 <= at - 1 < T, 0 <= at - 3 < T
                film = f_ps[(at - 3) % 2]

                def taken():
                    v.wait_ge(e_ok, t)
                    v.scalar_tensor_tensor(e[:, p, :, :], work[:, p, :, :], MOVED, e[:, p, :, :], ALU.is_equal, ALU.mult).then_inc(em_ok, 1)

                def sums():
                    v.wait_ge(em_ok, t)
                    v.reduce_sum(den[:, :], e[:, p, :, :], AX).then_inc(den_ok, 1)

                def inverses():
                    v.wait_ge(den_ok, t)
                    v.reciprocal(rden[:, 0, :], den[:, :]).then_inc(inv_ok, 1)

                def mean_weights():
                    v.wait_ge(inv_ok, t)
                    v.tensor_scalar(rden[:, 1, :], rden[:, 0, :], tok[:, bass.ds(t - 1, 1)], None, ALU.mult).then_inc(rden_ok, 1)

                def weigh():
                    v.wait_ge(rden_ok, t)
                    v.tensor_tensor(e[:, p, :, :], e[:, p, :, :], rden[:, 1, :].unsqueeze(2).to_broadcast([P, H1, SK]), ALU.mult).then_inc(er_ok, 1)

                def head_mean():
                    v.wait_ge(er_ok, t)
                    wait(v, aT_ok, t - 1, at - 1)
                    v.reduce_sum(am[:, 0:SK], e[:, p, :, :].rearrange("p h s -> p s h"), AX).then_inc(am_ok, 1)

                def modulate():
                    v.wait_ge(f_ok, t - 2)
                    v.wait_ge(fo_ok, t - 2)
                    wait(v, xm_ok, t - 3, at - 3)
                    v.scalar_tensor_tensor(xl[:, :], row(c.rows, t - 3), rstd2[:, bass.ds(t - 3, 1)], film[:, 0, 0:D], ALU.mult, ALU.mult).then_inc(xg_ok, 1)

                def shift():
                    v.wait_ge(xg_ok, t - 2)
                    v.tensor_tensor(row(c.xm, t - 3), xl[:, :], film[:, 0, D:2 * D], ALU.add).then_inc(xm_ok, 1)

                fill = [(prev, taken), (mod, modulate), (prev, sums), (mod, shift), (prev, inverses), (prev, mean_weights), (prev, weigh), (prev, head_mean)]
                fill = [f if there else None for there, f in fill]

                def next_fill():
                    f = fill.pop(0)
                    if f:
                        f()

                if 0 <= at < T:
                    u = at % 2
                    v.wait_ge(s_ok, t + 1)
                    v.scalar_tensor_tensor(s[:, u, :, :], s_ps[u][:, 0:H1 * SK].rearrange("p (h s) -> p h s", h=H1), 1.0 / DH1 ** 0.5,
                                           key_bias[:, bass.ds(t // TB, 1), :].to_broadcast([P, H1, SK]), ALU.mult, ALU.add).then_inc(ssb_ok, 1)
                    v.wait_ge(ssb_ok, t + 1)
                    v.sem_inc(gate_ok, 1)
                    for r in range(TOP // 8):
                        src = s if r == 0 else work
                        for h in range(H1):
                            mx = best[:, u, h, :] if r == 0 else later[:, h, :]
                            ins = v.max(mx, src[:, u, h, :])
                        if r == 0:
                            ins.then_inc(best_ok, 1)
                            next_fill()
                            v.wait_ge(best_ok, t + 1)
                            v.tensor_scalar(neg[:, u, :], best[:, u, :, 0], -1.0, None, ALU.mult).then_inc(neg_ok, 1)
                        else:
                            ins.then_inc(dve, 1)
                            next_fill()
                            v.wait_ge(dve, t * PER + (D0 + 2 * r))
                            v.sem_inc(gate_ok, 1)
                        for h in range(H1):
                            mx = best[:, u, h, :] if r == 0 else later[:, h, :]
                            ins = v.match_replace(work[:, u, h, :], mx, src[:, u, h, :], MOVED)
                        ins.then_inc(dve, 1)
                        next_fill()
                        v.wait_ge(dve, t * PER + (D0 + 2 * r + 1))
                        v.sem_inc(gate_ok, 1)
                while fill:
                    next_fill()
            pipeline(v, slot, -1, 5, T - 1, T + 2)
            v.wait_ge(xm_ok, T)


class StatePowers:

    N = 64
    DL = P

    def __init__(self, nc, keep, rows):
        room = [rows[:, i // 2, (i % 2) * P:(i % 2) * P + P] for i in range(17)]
        self.ar, self.ai, self.cr, self.ci, self.dt = room[0:5]
        self.t = room[5:11]
        self.ki, self.inv = room[11].bitcast(I32), room[12]
        self.ur, self.ui, self.pr, self.pi = room[13:17]
        self.keep = keep
        self.ld, self.chain, self.inv_ok, self.inv_steps = (keep.sems.new(n) for n in ("ld_state", "state_chain", "inverse_ready", "inverse_steps"))

    def load(self, sp, io):
        for h in range(2):
            q = slice(self.N * h, self.N * h + self.N)
            for buf, name in ((self.ar, "a_reT"), (self.ai, "a_imT"), (self.cr, "c_reT"), (self.ci, "c_imT")):
                sp.dma_start(buf[q], io[name][:, h * self.DL:(h + 1) * self.DL]).then_inc(self.ld, 16)
            sp.dma_start(self.dt[q], io["log_dt"][h * self.DL:(h + 1) * self.DL].partition_broadcast(self.N)).then_inc(self.ld, 16)

    def inverse_square(self, v):
        sq = self.t[5]
        v.wait_ge(self.ld, 160)
        v.tensor_tensor(self.inv, self.ar, self.ar, ALU.mult).then_inc(self.inv_steps, 1)
        v.tensor_tensor(sq, self.ai, self.ai, ALU.mult).then_inc(self.inv_steps, 1)
        v.wait_ge(self.inv_steps, 2)
        v.tensor_tensor(sq, self.inv, sq, ALU.add).then_inc(self.inv_steps, 1)
        v.wait_ge(self.inv_steps, 3)
        v.reciprocal(self.inv, sq).then_inc(self.inv_ok, 1)

    def powers(self, gp):
        n = 0

        def link(*ins):
            nonlocal n
            for x in ins:
                x.then_inc(self.chain, 1)
            n += len(ins)
            gp.wait_ge(self.chain, n)

        def tt(o, a, b, op):
            return gp.tensor_tensor(o, a, b, op)

        def ts(o, a, s0, s1, op0, op1=None):
            return gp.tensor_scalar(o, a, s0, s1, op0, *([op1] if op1 else []))

        gp.wait_ge(self.ld, 160)
        gp.wait_ge(self.inv_ok, 1)
        keep, x = self.keep, self.dt
        k, r, q, f = self.t[0:4]
        MAGIC = 12582912.0
        link(ts(k, x, 1.4426950408889634, MAGIC, ALU.mult, ALU.add))
        link(ts(k, k, MAGIC, None, ALU.subtract))
        for part in (-0.693359375, 2.12194440e-4):
            link(ts(f, k, part, None, ALU.mult))
            link(tt(x if part < 0 else r, x, f, ALU.add))
        link(ts(q, r, 1.0 / 5040, None, ALU.mult))
        for co in (1 / 720, 1 / 120, 1 / 24, 1 / 6, 0.5, 1.0):
            link(ts(q, q, co, None, ALU.add))
            link(tt(q, q, r, ALU.mult))
        link(ts(f, k, 127.0, 8388608.0, ALU.add, ALU.mult), ts(q, q, 1.0, None, ALU.add))
        link(gp.tensor_copy(self.ki, f))
        link(tt(x, q, self.ki.bitcast(F32), ALU.mult))
        wr, wi = self.t[4], self.t[5]
        link(tt(wr, x, self.ar, ALU.mult), tt(wi, x, self.ai, ALU.mult))
        link(ts(k, wi, 0.15915494309189535, MAGIC, ALU.mult, ALU.add))
        link(ts(k, k, MAGIC, None, ALU.subtract))
        for part in (6.28125, 1.93500518798828125e-3, 3.01991598196e-7):
            link(ts(f, k, part, None, ALU.mult))
            link(tt(wi, wi, f, ALU.subtract))
        ur, ui, pr, pi = self.ur, self.ui, self.pr, self.pi
        a, b, c, d = self.t[0:4]
        link(ts(ur, wr, 1 / 256, None, ALU.mult), ts(ui, wi, 1 / 256, None, ALU.mult))
        link(ts(pr, ur, 0.2, None, ALU.mult), ts(pi, ui, 0.2, None, ALU.mult))
        for co in (1 / 4, 1 / 3, 1 / 2, 1.0):
            link(ts(pr, pr, 1.0, None, ALU.add), tt(b, pi, ui, ALU.mult), tt(d, pi, ur, ALU.mult))
            link(tt(a, pr, ur, ALU.mult), tt(c, pr, ui, ALU.mult))
            link(tt(pr, a, b, ALU.subtract), tt(pi, c, d, ALU.add))
            if co != 1.0:
                link(ts(pr, pr, co, None, ALU.mult), ts(pi, pi, co, None, ALU.mult))

        def double():
            link(ts(a, pr, 2.0, None, ALU.add), ts(c, pr, 1.0, 2.0, ALU.add, ALU.mult), tt(b, pi, pi, ALU.mult))
            link(tt(a, a, pr, ALU.mult), tt(pi, c, pi, ALU.mult))
            link(tt(pr, a, b, ALU.subtract))

        for _ in range(8):
            double()
        link(tt(a, self.cr, pr, ALU.mult), tt(b, self.ci, pi, ALU.mult), tt(c, self.cr, pi, ALU.mult), tt(d, self.ci, pr, ALU.mult))
        link(tt(ur, a, b, ALU.subtract), tt(ui, c, d, ALU.add))
        link(tt(a, ur, self.ar, ALU.mult), tt(b, ui, self.ai, ALU.mult), tt(c, ui, self.ar, ALU.mult), tt(d, ur, self.ai, ALU.mult))
        link(tt(ur, a, b, ALU.add), tt(ui, c, d, ALU.subtract), ts(self.inv, self.inv, 2.0, None, ALU.mult))
        link(tt(keep.dc[:, 0, :], ur, self.inv, ALU.mult), tt(keep.dc[:, 1, :], ui, self.inv, ALU.mult))
        for j in range(9):
            link(ts(keep.z[:, 0, j, :], pr, 1.0, None, ALU.add), gp.tensor_copy(keep.z[:, 1, j, :], pi))
            if j < 8:
                double()


W = S // 2
X_TILES = (0, 1, 2, 3)
K_TILES = (0, 1, 4, 3, 5, 1)


FH = 4 * D
MH = FH // P


def kernel_transform(nc, io, keep, c):
    with ExitStack() as ctx:
        k_rows = ctx.enter_context(nc.sbuf_tensor("k_rows", [P, 2, S], F32))
        kT = ctx.enter_context(nc.sbuf_tensor("k_T", [P, 4, D], F32))
        t_ps = ctx.enter_context(nc.psum_tensor("kt_ps", [P, 2, 512], F32))
        f_ps = ctx.enter_context(nc.psum_tensor("kf_ps", [P, 6, 512], F32))
        sem = keep.sems.new
        ld_ffn = sem("ld_ffn")
        ld, tr, ev, mm = (sem(n) for n in ("ld_kt", "kT_in_psum", "kT_ready", "kf_in_psum"))
        blk = ctx.enter_context(nc.Block())

        @blk.sync
        def _(sp):
            sp.dma_start(k_rows[:, :, :], c.kernel_dram.rearrange("(h p) l -> p h l", p=P)).then_inc(ld, 16)
            w1, w2, gT, bT, b1T, b2, g_out, b_out = c.ffn
            for dst, src in ((w1[:, :, :], io["ffn_w1"].rearrange("(k c) n -> c k n", k=KD)), (gT[:, :], io["g_ffnT"]), (bT[:, :], io["b_ffnT"]),
                             (b1T[:, :], io["ffn_b1T"]), (b2[:, :], io["ffn_b2"].partition_broadcast(P)),
                             (w2[:, :, :], io["ffn_w2"].rearrange("(k c) n -> c k n", k=MH)),
                             (g_out[:, :], io["g_norm_out"].partition_broadcast(P)), (b_out[:, :], io["b_norm_out"].partition_broadcast(P))):
                sp.dma_start(dst, src).then_inc(ld_ffn, 16)
            sp.wait_ge(ld_ffn, 16 * 8)

        @blk.tensor
        def _(pe):
            pe.wait_ge(ld, 16)
            for lc in range(4):
                for h in range(2):
                    x = nc.tensor.transpose(t_ps[:, lc // 2, (lc % 2) * D + h * P:(lc % 2) * D + h * P + P], k_rows[:, h, lc * P:(lc + 1) * P], keep.ident[:, :])
                if lc % 2:
                    x.then_inc(tr, 1)
            pe.wait_ge(ev, 2)
            kv = kT[:, :, :].rearrange("p (w k) d -> p w k d", k=2)
            for j, f in enumerate(K_TILES):
                for k in range(2):
                    x = nc.tensor.matmul(f_ps[:, j, :], c.fwd[:, k, f * P:(f + 1) * P], kv[:, :, k, :], start=(k == 0), stop=(k == 1))
                x.then_inc(mm, 1)

        @blk.vector
        def _(v):
            for i in range(2):
                v.wait_ge(tr, i + 1)
                v.tensor_copy(kT[:, 2 * i:2 * i + 2, :], t_ps[:, i, :].rearrange("p (a d) -> p a d", a=2)).then_inc(ev, 1)
            for j in range(6):
                v.wait_ge(mm, j + 1)
                v.tensor_copy(c.kf[:, j, :, :], f_ps[:, j, :].rearrange("p (w d) -> p w d", w=2)).then_inc(ev, 1)
            v.wait_ge(ev, 8)


def convolution(nc, io, keep, c):
    with ExitStack() as ctx:
        def sb(name, shape, dt=F32):
            return ctx.enter_context(nc.sbuf_tensor(name, shape, dt))

        sem = keep.sems.new

        xz = sb("x_hat", [P, 4, 2, D])
        yhs = [sb(f"y_hat{i}", [P, 4, 2, D]) for i in range(2)]
        t = [sb(f"prod{i}", [P, 2, 2, D]) for i in range(4)]
        xf_ps = ctx.enter_context(nc.psum_tensor("xf_ps", [P, 4, 512], F32))
        y_ps = [ctx.enter_context(nc.psum_tensor(f"yt_ps{i}", [P, 512], F32)) for i in range(2)]
        fwd_ok, x0_ok, xz_ok, prod, ppool, yh_ok = (sem(n) for n in ("fwd_done", "x0_ready", "xz_ready", "dve_products", "pool_products", "yhat_ready"))
        inv_ok, y_ok, skip_ok, base_ok, st_ok = (sem(n) for n in ("inv_done", "y_added", "skip_ready", "base_ready", "stats_conv"))
        blk = ctx.enter_context(nc.Block())

        def win(buf, b, k):
            return buf[:, :, :].rearrange("p (b q k) d -> p b q k d", b=B, q=2)[:, b, :, k, :]

        UA = c.kf[:, 0:2, 0, :].unsqueeze(2).to_broadcast([P, 2, 2, D])
        UB = c.kf[:, 2:4, 0, :].unsqueeze(2).to_broadcast([P, 2, 2, D])
        UD = c.kf[:, 4:6, 0, :].unsqueeze(2).to_broadcast([P, 2, 2, D])
        VA, VB, VD = (c.kf[:, j:j + 2, 1, :] for j in (0, 2, 4))

        @blk.tensor
        def _(pe):
            for b in range(B + 1):
                if b < B:
                    for j, f in enumerate(X_TILES):
                        wait(pe, xz_ok, b, b)
                        for k in range(2):
                            x = nc.tensor.matmul(xf_ps[:, j, :], c.fwd[:, k, f * P:(f + 1) * P], win(c.xm, b, k), start=(k == 0), stop=(k == 1))
                    x.then_inc(fwd_ok, 1)
                if b >= 1:
                    pe.wait_ge(yh_ok, b)
                    for k in range(2):
                        wait(pe, y_ok, 2 * (b - 2) + k + 1, 2 * (b - 2) + k + 1)
                        for j in range(4):
                            x = nc.tensor.matmul(y_ps[k][:, :], c.inv[:, j, k * P:(k + 1) * P], yhs[(b - 1) % 2][:, j, :, :].rearrange("p q d -> p (q d)"),
                                                 start=(j == 0), stop=(j == 3))
                        x.then_inc(inv_ok, 1)

        @blk.scalar
        def _(act):
            for b in range(B):
                act.wait_ge(fwd_ok, b + 1)
                wait(act, yh_ok, b, b)
                nc.scalar.activation(xz[:, :, 0, :], xf_ps[:, :, 0:D], ACT.Copy).then_inc(x0_ok, 1)

        @blk.gpsimd
        def _(gp):
            n = 0
            for b in range(B):
                xr, xi = xz[:, 0:2, :, :], xz[:, 2:4, :, :]
                gp.wait_ge(xz_ok, b + 1)
                wait(gp, yh_ok, b, b)
                gp.tensor_tensor(t[2][:, :, :, :], xr, UB, ALU.mult).then_inc(ppool, 1)
                gp.tensor_tensor(t[3][:, :, :, :], xi, UD, ALU.mult).then_inc(ppool, 1)
                gp.wait_ge(fwd_ok, b + 1)
                for k in range(2):
                    xm, rows = win(c.xm, b, k), win(c.rows, b, k)
                    gp.tensor_tensor(xm, xm, c.dskip[:, :].unsqueeze(1).to_broadcast([P, 2, D]), ALU.mult).then_inc(skip_ok, 1)
                    gp.tensor_tensor(rows, rows, win(c.film, b, k)[:, :, D:2 * D], ALU.add).then_inc(base_ok, 1)

        @blk.vector
        def _(v):
            n = 0

            def link(*ins):
                nonlocal n
                for x in ins:
                    x.then_inc(prod, 1)
                n += len(ins)
                v.wait_ge(prod, n)

            def tt(o, a, b, op):
                return v.tensor_tensor(o, a, b, op)

            def products(b):
                v.wait_ge(x0_ok, b + 1)
                v.scalar_tensor_tensor(xz[:, :, 1, :], xz[:, :, 0, :], c.sign[:, 0:1], xf_ps[:, :, D:2 * D], ALU.mult, ALU.add).then_inc(xz_ok, 1)
                v.wait_ge(xz_ok, b + 1)
                xr, xi = xz[:, 0:2, :, :], xz[:, 2:4, :, :]
                r0, i0 = xr[:, :, 0, :], xi[:, :, 0, :]
                yr, yi = yhs[b % 2][:, 0:2, :, :], yhs[b % 2][:, 2:4, :, :]
                link(tt(t[0][:, :, :, :], xr, UA, ALU.mult), tt(t[1][:, :, :, :], xi, UB, ALU.mult))
                wait(v, inv_ok, 2 * (b - 1), 2 * (b - 1))
                link(tt(yr, t[0][:, :, :, :], t[1][:, :, :, :], ALU.subtract))
                v.wait_ge(ppool, 2 * b + 2)
                link(tt(yi, t[2][:, :, :, :], t[3][:, :, :, :], ALU.add), tt(t[0][:, :, 0, :], r0, VA, ALU.mult), tt(t[0][:, :, 1, :], i0, VB, ALU.mult),
                     tt(t[1][:, :, 0, :], r0, VB, ALU.mult), tt(t[1][:, :, 1, :], i0, VD, ALU.mult))
                link(tt(yr[:, :, 1, :], yr[:, :, 1, :], t[0][:, :, 0, :], ALU.add), tt(yi[:, :, 1, :], yi[:, :, 1, :], t[1][:, :, 0, :], ALU.add))
                link(tt(yr[:, :, 1, :], yr[:, :, 1, :], t[0][:, :, 1, :], ALU.subtract), tt(yi[:, :, 1, :], yi[:, :, 1, :], t[1][:, :, 1, :], ALU.add))
                v.sem_inc(yh_ok, 1)

            def outer(b):
                for k in range(2):
                    xm, rows = win(c.xm, b, k), win(c.rows, b, k)
                    v.wait_ge(inv_ok, 2 * b + k + 1)
                    v.wait_ge(skip_ok, 2 * b + k + 1)
                    v.tensor_tensor(xm, xm, y_ps[k][:, :].rearrange("p (q d) -> p q d", q=2), ALU.add).then_inc(y_ok, 1)
                    v.wait_ge(y_ok, 2 * b + k + 1)
                    link(tt(xm, xm, win(c.film, b, k)[:, :, 0:D], ALU.mult))
                    v.wait_ge(base_ok, 2 * b + k + 1)
                    link(tt(rows, rows, xm, ALU.add))
                for i in range(TB * b, TB * b + TB):
                    v.bn_stats(keep.stats[:, i, :], c.rows[:, i, :]).then_inc(st_ok, 1)

            for b in range(B):
                products(b)
                if b >= 1:
                    outer(b - 1)
            outer(B - 1)
            v.wait_ge(st_ok, T)


def dense_ffn(nc, io, keep, c):
    with ExitStack() as ctx:
        def sb(name, shape, dt=F32):
            return ctx.enter_context(nc.sbuf_tensor(name, shape, dt))

        sem = keep.sems.new

        w1, w2, gT, bT, b1T, b2, g_out, b_out = c.ffn
        tmp, mean, rstd = sb("tmp_f", [P, 4, T]), sb("mean_f", [P, T]), sb("rstd_f", [P, T])
        stats2 = sb("stats_f2", [P, T, 6])
        tmp2, mean2, rstd2 = sb("tmp_f2", [P, 4, T]), sb("mean_f2", [P, T]), sb("rstd_f2", [P, T])
        xs, xT = sb("xs_f", [P, TB, D]), sb("xT_f", [P, 2, KD, S])
        hid = sb("hid_f", [P, MH, S])
        t_ps = ctx.enter_context(nc.psum_tensor("ft_ps", [P, KD, 512], F32))
        h_ps = [ctx.enter_context(nc.psum_tensor(f"fh_ps{i}", [P, 512], F32)) for i in range(3)]
        o_ps = [ctx.enter_context(nc.psum_tensor(f"fo_ps{i}", [P, 512], F32)) for i in range(2)]
        dve, var_ok, std_ok = (sem(n) for n in ("dve_f", "var_f", "std_f"))
        xs_ok, xT_ok, xTs_ok, h_ok, act_ok, o_ok, x5_ok, rb_ok, st_ok = (sem(n + "_f") for n in ("xs", "xT", "xTs", "h", "act", "o", "x5", "rb", "stats"))
        fin, finp = sem("final_dve"), sem("final_pool")
        blk = ctx.enter_context(nc.Block())

        @blk.sync
        def _(sp):
            for x in range(E):
                sp.dma_start(keep.w1[:, x, :, :], io["w1_1"][x].rearrange("(k c) n -> c k n", k=KD)).then_inc(keep.ld_w1, 16)
                sp.dma_start(keep.w2[:, x, :, :], io["w2_1"][x].rearrange("(k c) n -> c k n", k=F1 // P)).then_inc(keep.ld_w2, 16)

        @blk.gpsimd
        def _(gp):
            gate = keep.gate[:, 1:2]
            gp.tensor_scalar(g_out[:, :], g_out[:, :], gate, None, ALU.mult).then_inc(finp, 1)
            gp.tensor_scalar(b_out[:, :], b_out[:, :], gate, None, ALU.mult).then_inc(finp, 1)
            gp.wait_ge(finp, 2)
            for b in range(B):
                sl = slice(TB * b, TB * b + TB)
                wide = [P, TB, D]
                gp.wait_ge(xs_ok, TB * (b + 1))
                gp.tensor_tensor(c.rows[:, sl, :], c.rows[:, sl, :], b2[:, :].unsqueeze(1).to_broadcast(wide), ALU.add).then_inc(rb_ok, 1)
                gp.tensor_tensor(keep.x1[:, sl, :], keep.x1[:, sl, :], b_out[:, :].unsqueeze(1).to_broadcast(wide), ALU.add).then_inc(finp, 1)

        @blk.scalar
        def _(act):
            act.wait_ge(var_ok, 1)
            nc.scalar.activation(rstd[:, :], tmp[:, 0, :], ACT.Sqrt).then_inc(std_ok, 1)

            def deviation(b):
                sl = slice(TB * b, TB * b + TB)
                act.wait_ge(var_ok, b + 2)
                nc.scalar.activation(rstd2[:, sl], tmp2[:, 0, sl], ACT.Sqrt).then_inc(std_ok, 1)

            for b in range(B):
                for m in range(MH):
                    n = MH * b + m
                    act.wait_ge(h_ok, n + 1)
                    if m == 0:
                        wait(act, o_ok, TB * b, TB * b)
                    if b and m == 2:
                        deviation(b - 1)
                    nc.scalar.activation(hid[:, m, :], h_ps[n % 3][:, :], ACT.Gelu, bias=b1T[:, m:m + 1]).then_inc(act_ok, 1)
            deviation(B - 1)

        @blk.tensor
        def _(pe):
            def turn(b):
                for i in range(TB):
                    pe.wait_ge(xs_ok, TB * b + i + 1)
                    if i == 0:
                        wait(pe, xTs_ok, 2 * b, 2 * b)
                    for k in range(KD):
                        x = nc.tensor.transpose(t_ps[:, k, i * P:(i + 1) * P], xs[:, i, k * P:(k + 1) * P], keep.ident[:, :])
                    x.then_inc(xT_ok, 1)

            turn(0)
            for b in range(B):
                pe.wait_ge(xTs_ok, 2 * b + 2)
                for m in range(MH):
                    n = MH * b + m
                    wait(pe, act_ok, n - 2, n - 2)
                    for k in range(KD):
                        x = nc.tensor.matmul(h_ps[n % 3][:, :], w1[:, k, m * P:(m + 1) * P], xT[:, b % 2, k, :], start=(k == 0), stop=(k == KD - 1))
                    x.then_inc(h_ok, 1)
                if b + 1 < B:
                    turn(b + 1)
                pe.wait_ge(act_ok, MH * (b + 1))
                for i in range(TB):
                    n = TB * b + i
                    wait(pe, x5_ok, n - 1, n - 1)
                    for k in range(MH):
                        x = nc.tensor.matmul(o_ps[n % 2][:, 0:D], hid[:, k, i * P:(i + 1) * P], w2[:, k, :], start=(k == 0), stop=(k == MH - 1))
                    x.then_inc(o_ok, 1)

        @blk.vector
        def _(v):
            n = norm_from_stats(v, 0, dve, keep.stats, tmp, mean, rstd)
            v.wait_ge(dve, n)
            v.sem_inc(var_ok, 1)
            v.wait_ge(std_ok, 1)
            v.reciprocal(rstd[:, :], rstd[:, :]).then_inc(dve, 1)
            n += 1
            v.wait_ge(dve, n)

            def ln(b):
                for i in range(TB):
                    t = TB * b + i
                    wait(v, xT_ok, TB * (b - 1) + i + 1, TB * (b - 1) + i + 1)
                    v.tensor_scalar(xs[:, i, :], c.rows[:, t, :], mean[:, t:t + 1], rstd[:, t:t + 1], ALU.subtract, ALU.mult).then_inc(xs_ok, 1)
                v.wait_ge(xT_ok, TB * (b + 1))
                wait(v, h_ok, MH * (b - 1), MH * (b - 1))
                for k in range(KD):
                    v.tensor_scalar(xT[:, b % 2, k, :], t_ps[:, k, :], gT[:, k:k + 1], bT[:, k:k + 1], ALU.mult, ALU.add).then_inc(xTs_ok, 1)

            ln(0)
            for b in range(B):
                if b + 1 < B:
                    ln(b + 1)
                v.wait_ge(rb_ok, b + 1)
                for i in range(TB):
                    t = TB * b + i
                    v.wait_ge(o_ok, t + 1)
                    v.tensor_tensor(c.rows[:, t, :], c.rows[:, t, :], o_ps[t % 2][:, 0:D], ALU.add).then_inc(x5_ok, 1)
                    v.wait_ge(x5_ok, t + 1)
                    v.bn_stats(stats2[:, t, :], c.rows[:, t, :]).then_inc(st_ok, 1)
                sl = slice(TB * b, TB * b + TB)
                v.wait_ge(st_ok, (2 * b + 1) * TB)
                n = norm_from_stats(v, n, dve, stats2[:, sl, :], tmp2[:, :, sl], mean2[:, sl], rstd2)
                v.wait_ge(dve, n)
                v.sem_inc(var_ok, 1)
                v.wait_ge(std_ok, b + 2)
                v.reciprocal(rstd2[:, sl], rstd2[:, sl]).then_inc(dve, 1)
                n += 1
                v.wait_ge(dve, n)
                v.wait_ge(finp, 3 + b)
                for t in range(TB * b, TB * b + TB):
                    v.scalar_tensor_tensor(c.rows[:, t, :], c.rows[:, t, :], mean2[:, t:t + 1], g_out[:, :], ALU.subtract, ALU.mult).then_inc(fin, 1)
                for t in range(TB * b, TB * b + TB):
                    v.wait_ge(fin, TB * b + t + 1)
                    v.scalar_tensor_tensor(keep.x1[:, t, :], c.rows[:, t, :], rstd2[:, t:t + 1], keep.x1[:, t, :], ALU.mult, ALU.add).then_inc(fin, 1)
                for t in range(TB * b, TB * b + TB):
                    v.wait_ge(fin, TB * (b + 1) + t + 1)
                    v.bn_stats(keep.stats[:, t, :], keep.x1[:, t, :]).then_inc(st_ok, 1)
            v.wait_ge(st_ok, 2 * T)


class Kept:
    pass


def build(nc, io, out):
    with ExitStack() as ctx:
        def sb(name, shape, dt=F32):
            return ctx.enter_context(nc.sbuf_tensor(name, shape, dt))

        keep = Kept()
        keep.x1 = sb("x1", [P, T, D])
        keep.stats = sb("stats", [P, T, 6])
        keep.gate = sb("gate", [P, 4])
        keep.ident, keep.ustrict = sb("ident", [P, P]), sb("ustrict", [P, P])
        keep.ones = sb("ones_", [P, P])
        keep.z = sb("z_powers", [P, 2, 9, P])
        keep.dc = sb("dc_twice", [P, 2, P])
        keep.xslots, keep.yslots, keep.zeroed, keep.zero_loads = {}, {}, {}, {}
        for tag, k in (("0", 1), ("1", 2)):
            n = k * T + E - 1
            keep.xslots[tag] = nc.dram_tensor(f"xslots{tag}", (n * P, D), F32, kind="Internal").ap()
            keep.yslots[tag] = nc.dram_tensor(f"yslots{tag}", (n * P, D), F32, kind="Internal").ap()
            keep.zeroed[tag] = ctx.enter_context(nc.semaphore(f"zeroed{tag}"))
            keep.zero_loads[tag] = 1
        keep.ld_w2 = ctx.enter_context(nc.semaphore("ld_expert_w2"))
        keep.ld_w1 = ctx.enter_context(nc.semaphore("ld_expert_w1"))
        with ExitStack() as w0:
            keep.sems = w0.enter_context(LayerSemaphores(nc))
            keep.w1 = w0.enter_context(nc.sbuf_tensor("w1_0", [P, E, KD, F0], F32))
            layer0_attention(nc, io, keep)
            keep.w2 = w0.enter_context(nc.sbuf_tensor("w2_0", [P, E, F0 // P, D], F32))
            routed_experts(nc, io, keep, 1, F0, ACT.Silu, 2, "0")
        with ExitStack() as w1:
            c = Kept()
            c.rows = w1.enter_context(nc.sbuf_tensor("xt_rows", [P, T, D], F32))
            with ExitStack() as lc:
                keep.sems = lc.enter_context(LayerSemaphores(nc))
                c.ffn = tuple(w1.enter_context(nc.sbuf_tensor(name, shape, F32)) for name, shape in (
                    ("ffn_w1", [P, KD, FH]), ("ffn_w2", [P, MH, D]), ("g_ffnT", [P, KD]), ("b_ffnT", [P, KD]), ("ffn_b1T", [P, MH]),
                    ("ffn_b2", [P, D]), ("g_norm_out", [P, D]), ("b_norm_out", [P, D])))
                c.kernel_dram = nc.dram_tensor("conv_kernel", (D, S), F32, kind="Internal").ap()
                with ExitStack() as lx:
                    c.xm = lx.enter_context(nc.sbuf_tensor("xm", [P, T, D], F32))
                    c.film = lx.enter_context(nc.sbuf_tensor("film", [P, T, 2 * D], F32))
                    c.fwd = lx.enter_context(nc.sbuf_tensor("dft_table", [P, 2, 6 * P], F32))
                    c.inv = lx.enter_context(nc.sbuf_tensor("idft_table", [P, 4, W], F32))
                    c.sign = lx.enter_context(nc.sbuf_tensor("sign", [P, 1], F32))
                    c.dskip = lx.enter_context(nc.sbuf_tensor("d_skip", [P, D], F32))
                    layer1_attention(nc, io, keep, c)
                    c.kf = lx.enter_context(nc.sbuf_tensor("kernel_hat", [P, 6, 2, D], F32))
                    kernel_transform(nc, io, keep, c)
                    convolution(nc, io, keep, c)
                keep.w1 = w1.enter_context(nc.sbuf_tensor("w1_1", [P, E, KD, F1], F32))
                keep.w2 = w1.enter_context(nc.sbuf_tensor("w2_1", [P, E, F1 // P, D], F32))
                dense_ffn(nc, io, keep, c)
            keep.sems = w1.enter_context(LayerSemaphores(nc))
            routed_experts(nc, io, keep, 2, F1, ACT.Gelu, 3, "1", out)


def constants():
    import numpy as np

    c = {"ident": np.eye(P, dtype=np.float32), "ustrict": np.triu(np.ones((P, P), np.float32), 1)}
    ch = np.arange(P)
    c["headmask16"] = np.where(ch[:, None] // DH0 == np.arange(8)[None], np.float32(DH0 ** -0.5), np.float32(0)).astype(np.float32)
    c["headmask32"] = (ch[:, None] // DH1 == np.arange(H1)[None]).astype(np.float32)
    f, t = np.arange(W)[None], np.arange(W)[:, None]
    turn = 2 * np.pi * ((f * t) % (2 * W)) / (2 * W)
    cos, sin = np.cos(turn), -np.sin(turn)
    nyquist = np.where(t % 2, -1.0, 1.0)
    ca, cb, sa, sb = cos[:, :P], cos[:, P:], sin[:, :P], sin[:, P:]
    c["dft"] = np.concatenate([ca, cb, np.hstack([nyquist, sa[:, 1:]]), sb, sa, np.hstack([nyquist, ca[:, 1:]])], 1).astype(np.float32)
    back = np.concatenate([ca, cb, np.hstack([nyquist, sa[:, 1:]]), sb], 1).T / W
    back[[0, 2 * P]] /= 2
    c["idft"] = back.astype(np.float32)
    c["sign"] = np.where(ch % 2, -1.0, 1.0).astype(np.float32)[:, None]
    e = np.arange(E, dtype=np.float32)
    c["iota_e"] = np.stack([e - 100, e])
    c["iota_t"] = np.arange(2 * T + E - 1, dtype=np.float32)
    owner = np.full((96, 1), -1, np.float32)
    for q in range(3):
        owner[32 * q:32 * q + E, 0] = e
    c["bias_owner"] = owner
    return c


def kernel(**inputs):
    import numpy as np
    import concourse.bacc as bacc
    from concourse.bass_utils import run_bass_kernel_spmd

    g = {k: np.asarray(v) for k, v in inputs.items()}

    def b2_rows(b2):
        rows = np.zeros((4, 32, D), b2.dtype)
        rows[:3, :E] = b2
        return rows.reshape(P, D)

    def b1T(b1):
        return b1.reshape(E, -1, P).transpose(2, 0, 1)

    def col(name, k):
        return g[name].reshape(k, -1).T

    arrays = {
        "x": g["x"].reshape(B * S, D),
        "ctxT": g["ctx_768"].reshape(B * SK, DC).T,
        "g_xattn": g["g_xattn"], "g_ffn": g["g_ffn"],
        "wq0": g["L0_xattn_Wq"], "wk0": g["L0_xattn_Wk"], "wv0": g["L0_xattn_Wv"], "wo0": g["L0_xattn_Wo"],
        "bq0T": col("L0_xattn_bq", KD), "bk0T": col("L0_xattn_bk", KD), "bv0T": col("L0_xattn_bv", KD),
        "bv0": g["L0_xattn_bv"], "bo0": g["L0_xattn_bo"],
        "w1_0": g["L0_ffn_W1"], "w2_0": g["L0_ffn_W2"], "b1T_0": b1T(g["L0_ffn_b1"]), "b2_rows0": b2_rows(g["L0_ffn_b2"]),
        "wg0": g["L0_ffn_Wg"], "bg0": g["L0_ffn_bg"],
        "wq1": g["L1_xattn_Wq"], "wk1": g["L1_xattn_Wk"], "wv1": g["L1_xattn_Wv"],
        "w_film_in": g["L1_xattn_W_film_in"], "w_film_out": g["L1_xattn_W_film_out"],
        "b_film_in": g["L1_xattn_b_film_in"], "b_film_out": g["L1_xattn_b_film_out"],
        "mod_gate": g["L1_xattn_mod_gate"].reshape(1),
        "g_norm_in": g["L1_xattn_g_norm_in"], "b_norm_in": g["L1_xattn_b_norm_in"],
        "key_mask": g["mask_BxS2_bf1"].reshape(B * SK).view(np.uint8), "token_mask": g["mask_BxS_bf1"].reshape(T, P).T.copy().view(np.uint8),
        "a_reT": g["L1_xattn_A_re"].T, "a_imT": g["L1_xattn_A_im"].T, "c_reT": g["L1_xattn_C_re"].T, "c_imT": g["L1_xattn_C_im"].T,
        "log_dt": g["L1_xattn_log_dt"], "d_skip": g["L1_xattn_D_skip"],
        "ffn_w1": g["L1_xattn_W1"], "ffn_w2": g["L1_xattn_W2"], "ffn_b1T": col("L1_xattn_b1", 8), "ffn_b2": g["L1_xattn_b2"],
        "g_ffnT": col("L1_xattn_g_ffn", KD), "b_ffnT": col("L1_xattn_b_ffn", KD),
        "g_norm_out": g["L1_xattn_g_norm_out"], "b_norm_out": g["L1_xattn_b_norm_out"],
        "w1_1": g["L1_ffn_w1"].transpose(0, 2, 1), "w2_1": g["L1_ffn_w2"].transpose(0, 2, 1),
        "b1T_1": b1T(g["L1_ffn_b1"]), "b2_rows1": b2_rows(g["L1_ffn_b2"]), "wg1": g["L1_ffn_router_w"].T,
        **constants(),
    }
    nc = bacc.Bacc("TRN2", target_bir_lowering=False, num_devices=1)
    arrays = {f"in_{k}": np.ascontiguousarray(a) for k, a in arrays.items()}
    io = {k[3:]: nc.dram_tensor(k, a.shape, mybir.dt.from_np(a.dtype), kind="ExternalInput").ap() for k, a in arrays.items()}
    out = nc.dram_tensor("x_out", (B * S, D), F32, kind="ExternalOutput").ap()
    build(nc, io, out)
    got = run_bass_kernel_spmd(nc, [arrays], core_ids=[0])
    return got.results[0]["x_out"].reshape(B, S, D)
```
